# Optimizing a Trainium2 kernel written in Bass

```python
import numpy as np
import jax
import jax.numpy as jnp

def _softmax(x, axis=-1):
    return jax.nn.softmax(x, axis=axis)

def _gelu(x):
    return jax.nn.gelu(x, approximate=True)

def _silu(x):
    return jax.nn.silu(x)

def _sigmoid(x):
    return jax.nn.sigmoid(x)

def _layernorm(x, axis=-1, eps=1e-05):
    m = jnp.mean(x, axis=axis, keepdims=True)
    v = jnp.var(x, axis=axis, keepdims=True)
    return (x - m) / jnp.sqrt(v + eps)

def _scatter_add(tgt, idx, src, axis=0):
    return tgt.at[idx].add(src)

def _segment_sum(src, seg, n):
    return jax.ops.segment_sum(src, seg, n)
kernel_name = 'mk_gnn_ffn_d2_gnn_r8_f85f87'

def setup_inputs(seed: int=0):
    np.random.seed(seed)
    _w = jnp.asarray

    def _rec_inputs():
        import jax
        import jax.numpy as jnp
        _gk = jax.random.key(seed)
        x = -0.0003713 + 1 * jax.random.normal(jax.random.fold_in(_gk, 1), (6250, 256), jnp.float32)
        src = jax.random.randint(jax.random.fold_in(_gk, 2), (200000,), 0, 6250, jnp.int32)
        dst = jax.random.randint(jax.random.fold_in(_gk, 3), (200000,), 0, 6250, jnp.int32)
        _o = jnp.argsort(dst, stable=True)
        src = src[_o]
        dst = dst[_o]
        return (x, src, dst)
    x, src, dst = _rec_inputs()

    def _L0_gnn_setup():
        import jax, jax.numpy as jnp
        import numpy as np
        N_NODES = 6250
        N_EDGES = 200000
        H_SIZE = 256
        HEADS = 8
        HEAD_DIM = H_SIZE // HEADS
        NEG_SLOPE = 0.2
        key = jax.random.key(seed)
        k_x, k_e, k_w, k_as, k_ad, k_b = jax.random.split(key, 6)
        x = jax.random.normal(k_x, (N_NODES, H_SIZE), dtype=jnp.float32)
        edge_index = jax.random.randint(k_e, (2, N_EDGES), 0, N_NODES, dtype=jnp.int64)
        scale = 1.0 / np.sqrt(H_SIZE)
        W = jax.random.normal(k_w, (H_SIZE, HEADS, HEAD_DIM), dtype=jnp.float32) * scale
        att_src = jax.random.normal(k_as, (HEADS, HEAD_DIM), dtype=jnp.float32) * scale
        att_dst = jax.random.normal(k_ad, (HEADS, HEAD_DIM), dtype=jnp.float32) * scale
        bias = jnp.zeros((H_SIZE,), dtype=jnp.float32)
        return {'x': x, 'edge_index': edge_index, 'W': W, 'att_src': att_src, 'att_dst': att_dst, 'bias': bias}
    _L0_gnn_all = _L0_gnn_setup()
    _L0_gnn_in = {k: v for k, v in _L0_gnn_all.items() if k in ('W', 'att_src', 'att_dst', 'bias')}
    del _L0_gnn_all

    def _L0_ffn_setup():
        import jax, jax.numpy as jnp
        import numpy as np
        E = 8
        K = 2
        D = 256
        H = 512
        DOUT = 256
        EPS = 1e-05
        key = jax.random.key(seed)
        ks = jax.random.split(key, 9)
        s = 0.02
        return {'x': jax.random.normal(ks[0], (4, 1024, D), jnp.float32), 'gamma': 1.0 + 0.05 * jax.random.normal(ks[1], (D,), jnp.float32), 'beta': 0.05 * jax.random.normal(ks[2], (D,), jnp.float32), 'Wr': 0.01 * jax.random.normal(ks[3], (D, E), jnp.float32), 'br': jnp.zeros((E,), jnp.float32), 'W1': s * jax.random.normal(ks[4], (E, D, H), jnp.float32), 'b1': s * jax.random.normal(ks[5], (E, H), jnp.float32), 'W2': s * jax.random.normal(ks[6], (E, H, DOUT), jnp.float32), 'b2': s * jax.random.normal(ks[7], (E, DOUT), jnp.float32)}
    _L0_ffn_all = _L0_ffn_setup()
    _L0_ffn_in = {k: v for k, v in _L0_ffn_all.items() if k in ('gamma', 'beta', 'Wr', 'br', 'W1', 'b1', 'W2', 'b2')}
    del _L0_ffn_all

    def _L1_gnn_setup():
        import jax, jax.numpy as jnp
        import numpy as np

        def _inv_sqrt(deg):
            return jnp.where(deg > 0, jax.lax.rsqrt(deg), 0.0)
        key = jax.random.key(seed)
        k1, k2, k3, k4 = jax.random.split(key, 4)
        n_nodes, n_edges, d_in, d_half = (12500, 200000, 256, 128)
        x = jax.random.normal(k1, (n_nodes, d_in), dtype=jnp.float32)
        edge_index = jax.random.randint(k2, (2, n_edges), 0, n_nodes, dtype=jnp.int64)
        W_f = jax.random.normal(k3, (d_half, d_in), dtype=jnp.float32) * (1.0 / np.sqrt(d_in))
        W_b = jax.random.normal(k4, (d_half, d_in), dtype=jnp.float32) * (1.0 / np.sqrt(d_in))
        bias_param = jnp.zeros((2 * d_half,), dtype=jnp.float32)
        return {'x': x, 'edge_index': edge_index, 'W_f': W_f, 'W_b': W_b, 'bias_param': bias_param}
    _L1_gnn_all = _L1_gnn_setup()
    _L1_gnn_in = {k: v for k, v in _L1_gnn_all.items() if k in ('W_f', 'W_b', 'bias_param')}
    del _L1_gnn_all

    def _L1_ffn_setup():
        import math
        import jax, jax.numpy as jnp
        import numpy as np
        CAPACITY_FACTOR = 1.25
        key = jax.random.key(seed)
        ks = jax.random.split(key, 5)
        B, L, D, F, E = (8, 1024, 256, 1024, 8)
        h = jax.random.normal(ks[0], (B, L, D), dtype=jnp.float32)
        gate_w = jax.random.normal(ks[1], (D, E), dtype=jnp.float32) * 0.02
        gate_b = jnp.zeros((E,), dtype=jnp.float32)
        w1 = jax.random.normal(ks[2], (E, D, F), dtype=jnp.float32) * (1.0 / math.sqrt(D))
        b1 = jnp.zeros((E, F), dtype=jnp.float32)
        w2 = jax.random.normal(ks[3], (E, F, D), dtype=jnp.float32) * (1.0 / math.sqrt(F))
        b2 = jnp.zeros((E, D), dtype=jnp.float32)
        return {'h': h, 'gate_w': gate_w, 'gate_b': gate_b, 'w1': w1, 'b1': b1, 'w2': w2, 'b2': b2}
    _L1_ffn_all = _L1_ffn_setup()
    _L1_ffn_in = {k: v for k, v in _L1_ffn_all.items() if k in ('gate_w', 'gate_b', 'w1', 'b1', 'w2', 'b2')}
    del _L1_ffn_all
    return {'x': x, 'src': src, 'dst': dst, 'L0_gnn_W': _L0_gnn_in['W'], 'L0_gnn_att_src': _L0_gnn_in['att_src'], 'L0_gnn_att_dst': _L0_gnn_in['att_dst'], 'L0_gnn_bias': _L0_gnn_in['bias'], 'L0_ffn_gamma': _L0_ffn_in['gamma'], 'L0_ffn_beta': _L0_ffn_in['beta'], 'L0_ffn_Wr': _L0_ffn_in['Wr'], 'L0_ffn_br': _L0_ffn_in['br'], 'L0_ffn_W1': _L0_ffn_in['W1'], 'L0_ffn_b1': _L0_ffn_in['b1'], 'L0_ffn_W2': _L0_ffn_in['W2'], 'L0_ffn_b2': _L0_ffn_in['b2'], 'L1_gnn_W_f': _L1_gnn_in['W_f'], 'L1_gnn_W_b': _L1_gnn_in['W_b'], 'L1_gnn_bias_param': _L1_gnn_in['bias_param'], 'L1_ffn_gate_w': _L1_ffn_in['gate_w'], 'L1_ffn_gate_b': _L1_ffn_in['gate_b'], 'L1_ffn_w1': _L1_ffn_in['w1'], 'L1_ffn_b1': _L1_ffn_in['b1'], 'L1_ffn_w2': _L1_ffn_in['w2'], 'L1_ffn_b2': _L1_ffn_in['b2']}

def reference(x, src, dst, L0_gnn_W, L0_gnn_att_src, L0_gnn_att_dst, L0_gnn_bias, L0_ffn_gamma, L0_ffn_beta, L0_ffn_Wr, L0_ffn_br, L0_ffn_W1, L0_ffn_b1, L0_ffn_W2, L0_ffn_b2, L1_gnn_W_f, L1_gnn_W_b, L1_gnn_bias_param, L1_ffn_gate_w, L1_ffn_gate_b, L1_ffn_w1, L1_ffn_b1, L1_ffn_w2, L1_ffn_b2):
    import jax
    import jax.numpy as jnp

    def _L0_gnn_ref(x, edge_index, W, att_src, att_dst, bias):
        import jax, jax.numpy as jnp
        import numpy as np
        N_NODES = 6250
        N_EDGES = 200000
        H_SIZE = 256
        HEADS = 8
        HEAD_DIM = H_SIZE // HEADS
        NEG_SLOPE = 0.2
        'GATConv (concat heads) -> relu -> dropout(eval=identity).\n\n            x: [N, F]; edge_index: [2, E] with (src=row0, dst=row1) meaning message j->i.\n            '
        N = x.shape[0]
        h = jnp.einsum('nf,fhd->nhd', x, W)
        a_src = jnp.sum(h * att_src, axis=-1)
        a_dst = jnp.sum(h * att_dst, axis=-1)
        src = edge_index[0]
        dst = edge_index[1]
        e = jax.nn.leaky_relu(a_src[src] + a_dst[dst], NEG_SLOPE)
        e_max = jax.ops.segment_max(e, dst, num_segments=N)
        e_exp = jnp.exp(e - e_max[dst])
        denom = jax.ops.segment_sum(e_exp, dst, num_segments=N)
        alpha = e_exp / (denom[dst] + 1e-16)
        msg = h[src] * alpha[:, :, None]
        out = jax.ops.segment_sum(msg, dst, num_segments=N)
        out = out.reshape(N, -1) + bias
        return jax.nn.relu(out)

    def _L0_ffn_ref(x, gamma, beta, Wr, br, W1, b1, W2, b2):
        import jax, jax.numpy as jnp
        import numpy as np
        E = 8
        K = 2
        D = 256
        H = 512
        DOUT = 256
        EPS = 1e-05
        mu = jnp.mean(x, axis=-1, keepdims=True)
        var = jnp.mean(jnp.square(x - mu), axis=-1, keepdims=True)
        xn = (x - mu) * jax.lax.rsqrt(var + EPS) * gamma + beta
        logits = jnp.einsum('bsd,de->bse', xn, Wr) + br
        top_vals, top_idx = jax.lax.top_k(logits, K)
        w = jax.nn.softmax(top_vals, axis=-1)
        w_full = jnp.einsum('bsk,bske->bse', w, jax.nn.one_hot(top_idx, E, dtype=w.dtype))
        y = jnp.zeros(x.shape[:-1] + (DOUT,), x.dtype)
        for e in range(E):
            h = jax.nn.gelu(jnp.einsum('bsd,dh->bsh', xn, W1[e]) + b1[e], approximate=False)
            y_e = jnp.einsum('bsh,hd->bsd', h, W2[e]) + b2[e]
            y = y + y_e * w_full[..., e, None]
        return y

    def _L1_gnn_ref(x, edge_index, W_f, W_b, bias_param):
        import jax, jax.numpy as jnp
        import numpy as np

        def _inv_sqrt(deg):
            return jnp.where(deg > 0, jax.lax.rsqrt(deg), 0.0)
        n_nodes = x.shape[0]
        loops = jnp.arange(n_nodes, dtype=edge_index.dtype)
        ei = jnp.concatenate([edge_index, jnp.stack([loops, loops])], axis=1)
        n_e = ei.shape[1]
        w = jnp.ones((n_e,), dtype=x.dtype)
        col, row = (ei[0], ei[1])
        in_deg = jax.ops.segment_sum(w, col, num_segments=n_nodes)
        out_deg = jax.ops.segment_sum(w, row, num_segments=n_nodes)
        ew = _inv_sqrt(out_deg)[row] * w * _inv_sqrt(in_deg)[col]
        mf = (x @ W_f.T)[row] * ew[:, None]
        y_forward = jax.ops.segment_sum(mf, col, num_segments=n_nodes)
        mb = (x @ W_b.T)[col] * ew[:, None]
        y_backward = jax.ops.segment_sum(mb, row, num_segments=n_nodes)
        y = jnp.concatenate([y_forward, y_backward], axis=-1) + bias_param
        return y

    def _L1_ffn_ref(h, gate_w, gate_b, w1, b1, w2, b2):
        import math
        import jax, jax.numpy as jnp
        import numpy as np
        CAPACITY_FACTOR = 1.25
        B, L, D = h.shape
        E = gate_w.shape[1]
        T = B * L
        C = max(1, math.ceil(CAPACITY_FACTOR * T / E))
        x = h.reshape(T, D)
        logits = x @ gate_w + gate_b
        probs = jax.nn.softmax(logits, axis=-1)
        idx = jnp.argmax(probs, axis=-1)
        prb = jnp.take_along_axis(probs, idx[:, None], axis=1)[:, 0]
        one_hot = jax.nn.one_hot(idx, E, dtype=jnp.float32)
        pos = (jnp.cumsum(one_hot, axis=0) * one_hot).sum(-1).astype(jnp.int32) - 1
        kept = pos < C
        pos_safe = jnp.where(kept, pos, C)
        buf = jnp.zeros((E, C, D), dtype=h.dtype).at[idx, pos_safe].set(x, mode='drop')
        hmid = jax.nn.relu(jnp.einsum('ecd,edf->ecf', buf, w1) + b1[:, None, :])
        ybuf = jnp.einsum('ecf,efd->ecd', hmid, w2) + b2[:, None, :]
        pos_g = jnp.minimum(pos, C - 1)
        y_tok = ybuf[idx, pos_g] * (prb * kept)[:, None]
        y = y_tok.reshape(B, L, D)
        y = jnp.nan_to_num(y, nan=0.0, posinf=10000.0, neginf=-10000.0)
        return y
    edge_index = jnp.stack([src, dst])
    x = x + _L0_gnn_ref(_layernorm(x, axis=-1), edge_index, L0_gnn_W, L0_gnn_att_src, L0_gnn_att_dst, L0_gnn_bias)
    x = x + _L0_ffn_ref(_layernorm(x, axis=-1)[None], L0_ffn_gamma, L0_ffn_beta, L0_ffn_Wr, L0_ffn_br, L0_ffn_W1, L0_ffn_b1, L0_ffn_W2, L0_ffn_b2)[0]
    x = x + _L1_gnn_ref(_layernorm(x, axis=-1), edge_index, L1_gnn_W_f, L1_gnn_W_b, L1_gnn_bias_param)
    x = x + _L1_ffn_ref(_layernorm(x, axis=-1)[None], L1_ffn_gate_w, L1_ffn_gate_b, L1_ffn_w1, L1_ffn_b1, L1_ffn_w2, L1_ffn_b2)[0]
    return x

_drawn_inputs = setup_inputs


def setup_inputs(seed=0):
    import zlib

    import numpy as np

    out = dict(_drawn_inputs(seed))
    spreads = {'L0_gnn_bias': (0.0, 0.1),
     'L0_ffn_br': (0.0, 0.1),
     'L1_gnn_bias_param': (0.0, 0.1),
     'L1_ffn_gate_b': (0.0, 0.1),
     'L1_ffn_b1': (0.0, 0.615),
     'L1_ffn_b2': (0.0, 0.431)}
    factors = {'L0_gnn_att_dst': 2.794, 'L0_ffn_gamma': 4.453, 'L0_ffn_beta': 3.731, 'L0_ffn_b1': 5.938}
    for name, (base, spread) in spreads.items():
        noise = np.random.default_rng([zlib.crc32(name.encode()), seed]).standard_normal(out[name].shape)
        drawn = base * np.exp(spread * noise) if base else spread * noise
        out[name] = jnp.asarray(drawn.astype(out[name].dtype))
    for name, factor in factors.items():
        out[name] = (out[name] * factor).astype(out[name].dtype)
    return out
```

```python
from contextlib import ExitStack

import concourse.bass as bass
from concourse import mybir

F32 = mybir.dt.float32
BF16 = mybir.dt.bfloat16
I32 = mybir.dt.int32
ALU = mybir.AluOpType
ACT = mybir.ActivationFunctionType
AX = mybir.AxisListType

P = 128
EPS = 1e-5
NEG_BIG = -1.0e38
ZCOLS = 2048
SUB = 2
STEP = SUB * P
GAT_DEPTH = 8
GNN_DEPTH = 4
BIG_DEPTH = max(GAT_DEPTH, GNN_DEPTH)
TOK = 512
GROUP = 7


class Shapes:

    def __init__(self, x, src, gat_W, w1, w2):
        self.N, self.D = x.shape
        self.E = src.shape[0]
        self.H = gat_W.shape[1]
        self.HD = gat_W.shape[2]
        self.NT = -(-self.N // P)
        self.TAIL = self.N - (self.NT - 1) * P
        self.EP = next(p for p in range(P, 0, -1) if self.E % p == 0)
        self.ET = self.E // self.EP
        self.STEPS = -(-(-(-self.E // STEP) + self.NT) // BIG_DEPTH) * BIG_DEPTH
        self.NX1, self.F1 = w1.shape[0], w1.shape[2]
        self.NX2, self.F2 = w2.shape[0], w2.shape[2]
        self.CAP = -(-5 * self.N // (4 * self.NX2))
        self.CT = -(-self.CAP // P)
        self.KC = -(-self.STEPS // P)
        self.EW = 2 * self.H + 1
        self.G1 = (2 * self.N + self.NX1 * (TOK - 1)) // TOK
        self.G2 = self.NX2 * -(-self.CAP // TOK)
        self.ROWS = self.NT * P
        self.G1 += self.G1 % 2
        self.G2 += self.G2 % 2
        assert self.D == 2 * P and self.NT % GROUP == 0


class Core:

    def __init__(self, nc, ctx):
        self.nc, self.ctx = nc, ctx
        self.used = []

    def sem(self, name):
        self.used.append(self.nc.alloc_semaphore(name))
        return self.used[-1]

    def recycle(self):
        self.nc.clear_and_free_semaphores(self.used)
        self.nc.all_engine_barrier()
        self.used = []

    def sems(self, name, n):
        return [self.sem(f"{name}_{j}") for j in range(n)]

    def sb(self, ctx, name, shape, dt=F32):
        return ctx.enter_context(self.nc.sbuf_tensor(name, shape, dt))

    def ps(self, ctx, name, shape, dt=F32):
        return ctx.enter_context(self.nc.psum_tensor(name, shape, dt))

    def dram(self, name, shape, dt=F32):
        return self.nc.dram_tensor(name, shape, dt, kind="Internal").ap()


class Chain:

    def __init__(self, eng, sem, start=0):
        self.eng, self.sem, self.n = eng, sem, start

    def mark(self, ins):
        ins.then_inc(self.sem, 1)
        self.n = self.n + 1

    def link(self, ins):
        self.mark(ins)
        self.eng.wait_ge(self.sem, self.n)

    def join(self):
        self.eng.wait_ge(self.sem, self.n)


def staged(eng, steps, stages, depth):
    def tick(i, j):
        for s, stage in enumerate(stages):
            if stage is None:
                continue
            back, slot = (0, j - s) if j >= s else (1, j - s + depth)
            if not isinstance(i, int):
                stage(i - back, slot, i * depth + (j - s), False)
            elif 0 <= i * depth + j - s < steps:
                stage(i - back, slot, i * depth + j - s, i == back)

    rounds = steps // depth
    for i in range(2):
        for j in range(depth):
            tick(i, j)
    with eng.Fori(2, rounds) as i:
        for j in range(depth):
            tick(i, j)
    for j in range(len(stages) - 1):
        tick(rounds, j)


def rows_of(dram, S):
    full = dram[0:(S.NT - 1) * P, :].rearrange("(i p) d -> p i d", p=P)
    tail = dram[(S.NT - 1) * P:S.N, :]
    return full, tail



def setup(k, S, ins, C):
    nc = k.nc
    ld = k.sem("weights_loaded")
    io = k.sem("iota_written")
    ch = k.sem("setup_chain")
    tr = k.sem("wfb_transposed")
    with ExitStack() as ctx:
        att = k.sb(ctx, "att_rows", [P, 2, S.D])
        tmp = k.sb(ctx, "w_times_att", [P, S.D])
        wraw = k.sb(ctx, "wfb_raw", [P, 2, S.D])
        ii = k.sb(ctx, "iota_int", [P, P], I32)
        tri_i = k.sb(ctx, "diff_int", [P, P], I32)
        wi = k.sb(ctx, "window_int", [P, S.NT], I32)
        pt = k.ps(ctx, "wfb_ps", [P, 4, P])
        block = ctx.enter_context(nc.Block())

        def row(v):
            return v.rearrange("(a d) -> a d", a=1).partition_broadcast(P) if len(v.shape) == 1 else v

        loads = [
            (C.waug[:, :, 0:S.D], ins["L0_gnn_W"].rearrange("(c p) h d -> p c (h d)", p=P)),
            (att[:, 0, :], ins["L0_gnn_att_src"].rearrange("h d -> (h d)").partition_broadcast(P)),
            (att[:, 1, :], ins["L0_gnn_att_dst"].rearrange("h d -> (h d)").partition_broadcast(P)),
            (C.gat_bias[:, :], ins["L0_gnn_bias"].partition_broadcast(P)),
            (C.gamma[:, :], ins["L0_ffn_gamma"].partition_broadcast(P)),
            (C.beta[:, :], ins["L0_ffn_beta"].partition_broadcast(P)),
            (C.wr[:, :, :], ins["L0_ffn_Wr"].rearrange("(c p) n -> p c n", p=P)),
            (C.br[:, :], ins["L0_ffn_br"].partition_broadcast(P)),
            (wraw[:, 0, :], ins["L1_gnn_W_f"]),
            (wraw[:, 1, :], ins["L1_gnn_W_b"]),
            (C.gnn_bias[:, :], ins["L1_gnn_bias_param"].partition_broadcast(P)),
            (C.wg[:, :, :], ins["L1_ffn_gate_w"].rearrange("(c p) n -> p c n", p=P)),
            (C.bg[:, :], ins["L1_ffn_gate_b"].partition_broadcast(P)),
        ]

        @block.sync
        def _(sp):
            for out, src in loads:
                sp.dma_start(out, src).then_inc(ld, 16)

        @block.gpsimd
        def _(pool):
            pool.iota(ii[:, :], pattern=[[1, P]], base=0, channel_multiplier=0).then_inc(io, 1)
            pool.iota(tri_i[:, :], pattern=[[1, P]], base=0, channel_multiplier=-1).then_inc(io, 1)
            pool.iota(wi[:, :], pattern=[[P, S.NT]], base=0, channel_multiplier=1).then_inc(io, 1)

        @block.vector
        def _(dve):
            c = Chain(dve, ch)
            dve.wait_ge(io, 3)
            c.mark(dve.tensor_copy(C.iota[:, :], ii[:, :]))
            c.mark(dve.tensor_scalar(C.ident[:, :], tri_i[:, :], 0.0, None, ALU.is_equal))
            c.mark(dve.tensor_scalar(C.upper[:, :], tri_i[:, :], 0.0, None, ALU.is_gt))
            c.mark(dve.tensor_scalar(C.lower[:, :], tri_i[:, :], 0.0, None, ALU.is_lt))
            c.mark(dve.tensor_copy(C.wiota[:, :], wi[:, :]))
            c.mark(dve.memset(C.ones[:, :], 1.0))
            c.mark(dve.memset(C.eps[:, :], EPS))
            dve.wait_ge(ld, 16 * len(loads))
            for a in range(2):
                for t in range(2):
                    c.link(dve.tensor_tensor(tmp[:, :], C.waug[:, t, 0:S.D], att[:, a, :], ALU.mult))
                    c.link(dve.tensor_reduce(C.waug[:, t, S.D + a * S.H:S.D + (a + 1) * S.H],
                                             tmp[:, :].rearrange("p (h d) -> p h d", h=S.H), AX.X, ALU.add))
            dve.wait_ge(tr, 1)
            c.link(dve.tensor_copy(C.wfb[:, :, :], pt[:, :, :].rearrange("p (c a) n -> p c (a n)", c=2)))

        @block.tensor
        def _(pe):
            pe.wait_ge(ch, 7)
            pe.wait_ge(ld, 16 * len(loads))
            for t in range(2):
                for a in range(2):
                    last = pe.transpose(pt[:, 2 * t + a, :], wraw[:, a, t * P:(t + 1) * P], C.ident[:, :])
            last.then_inc(tr, 1)



def project_nodes(k, S, C, tag, x_res, rhs, n_out, out_sb, xn_all=None, xnT_all=None, load_x=None, affine=None):
    nc = k.nc
    passes = 2 if affine else 1
    per_row = 3 if affine else 1
    head = 2 * GROUP + 1
    before_last = (passes - 1) * (head + GROUP)
    ops = before_last + head + GROUP * per_row
    ln = k.sem(f"{tag}_ln_steps")
    rt = k.sem(f"{tag}_root_ready")
    xl = k.sem(f"{tag}_x_loaded")
    tp = k.sem(f"{tag}_rows_transposed")
    tc = k.sem(f"{tag}_transpose_copied")
    pj = k.sem(f"{tag}_product_ready")
    ev = k.sem(f"{tag}_product_copied")
    gf = k.sem(f"{tag}_row_slots_free")
    with ExitStack() as ctx:
        st = k.sb(ctx, f"{tag}_stats", [P, GROUP, 6])
        mv = k.sb(ctx, f"{tag}_meanvar", [P, 2, GROUP, 2])
        sd = k.sb(ctx, f"{tag}_std", [P, 2, GROUP])
        rs = k.sb(ctx, f"{tag}_rstd", [P, 2, GROUP])
        xn = k.sb(ctx, f"{tag}_xn", [P, GROUP, S.D])
        xm = k.sb(ctx, f"{tag}_xm", [P, GROUP, S.D]) if affine else None
        xT = k.sb(ctx, f"{tag}_xT", [P, GROUP, 2, P])
        pt = k.ps(ctx, f"{tag}_pt", [P, 2, 512])
        po = k.ps(ctx, f"{tag}_po", [P, 2, 512])
        block = ctx.enter_context(nc.Block())

        def tile_of(t, g, j):
            return t[:, bass.ds(g * GROUP + j, 1), :].rearrange("p a d -> p (a d)")

        @block.sync
        def _(sp):
            if load_x is None:
                return
            sp.wait_ge(xl, 1)
            full, tail = rows_of(load_x, S)
            for g in range(S.NT // GROUP):
                hi = min((g + 1) * GROUP, S.NT - 1)
                sp.dma_start(x_res[:, g * GROUP:hi, :], full[:, g * GROUP:hi, :]).then_inc(xl, 16)
            sp.dma_start(x_res[0:S.TAIL, S.NT - 1, :], tail).then_inc(xl, 16)

        @block.gpsimd
        def _(pool):
            if load_x is not None:
                pool.memset(x_res[:, S.NT - 1, :], 0.0).then_inc(xl, 1)

        @block.vector
        def _(dve):
            if load_x is not None:
                dve.wait_ge(xl, 1 + 16 * (S.NT // GROUP + 1))
            with dve.Fori(0, S.NT // GROUP) as g:
                for r in range(passes):
                    last = r == passes - 1
                    at = g * ops + r * (head + GROUP)
                    src = [xm[:, j, :] if r else tile_of(x_res, g, j) for j in range(GROUP)]
                    for j in range(GROUP):
                        if r:
                            dve.wait_ge(ln, at - GROUP + j + 1)
                        dve.bn_stats(st[:, j, :], src[j]).then_inc(ln, 1)
                    for j in range(GROUP):
                        dve.wait_ge(ln, at + (j + 1))
                        dve.nop(nofuse=True)
                        dve.bn_aggr(mv[:, r, j, :], st[:, j, :]).then_inc(ln, 1)
                    dve.wait_ge(rt, g * passes + (r + 1))
                    dve.reciprocal(rs[:, r, :], sd[:, r, :]).then_inc(ln, 1)
                    dve.wait_ge(ln, at + head)
                    if last:
                        dve.wait_ge(gf, g + 1)
                    for j in range(GROUP):
                        dst = xn[:, j, :] if last else xm[:, j, :]
                        dve.tensor_scalar(dst, src[j], mv[:, r, j, 0:1], rs[:, r, j:j + 1],
                                          ALU.subtract, ALU.mult).then_inc(ln, 1)
                        if last and affine:
                            dve.wait_ge(ln, at + (head + 3 * j + 1))
                            dve.tensor_tensor(dst, dst, affine[0][:, :], ALU.mult).then_inc(ln, 1)
                            dve.wait_ge(ln, at + (head + 3 * j + 2))
                            dve.tensor_tensor(dst, dst, affine[1][:, :], ALU.add).then_inc(ln, 1)

        @block.scalar
        def _(act):
            with act.Fori(0, S.NT // GROUP) as g:
                for r in range(passes):
                    act.wait_ge(ln, g * ops + (r * (head + GROUP) + 2 * GROUP))
                    nc.scalar.activation(sd[:, r, :], mv[:, r, :, 1], ACT.Sqrt, bias=C.eps[:, 0:1]).then_inc(rt, 1)

                def copy_transposed(j):
                    act.wait_ge(tp, g * GROUP + (j + 1))
                    last = nc.scalar.copy(xT[:, j, :, :], pt[:, j % 2, 0:2 * P].rearrange("p (c n) -> p c n", c=2))
                    if xnT_all is not None:
                        for c in range(2):
                            last = nc.scalar.copy(xnT_all[:, c, bass.ds((g * GROUP + j) * P, P)],
                                                  pt[:, j % 2, c * P:(c + 1) * P])
                    last.then_inc(tc, 1)

                copy_transposed(0)
                for j in range(GROUP):
                    if j + 1 < GROUP:
                        copy_transposed(j + 1)
                    if xn_all is not None:
                        nc.scalar.copy(tile_of(xn_all, g, j), xn[:, j, :])
                    act.wait_ge(pj, g * GROUP + (j + 1))
                    nc.scalar.copy(tile_of(out_sb, g, j), po[:, j % 2, 0:n_out]).then_inc(ev, 1)

        @block.tensor
        def _(pe):
            pe.nop(nofuse=True).then_inc(gf, 1)
            with pe.Fori(0, S.NT // GROUP) as g:
                def transpose(j):
                    pe.wait_ge(ln, g * ops + (before_last + head + (j + 1) * per_row))
                    if j >= 2:
                        pe.wait_ge(tc, g * GROUP + (j - 1))
                    for c in range(2):
                        last = pe.transpose(pt[:, j % 2, c * P:(c + 1) * P], xn[:, j, c * P:(c + 1) * P],
                                            C.ident[:, :])
                    last.then_inc(tp, 1)

                transpose(0)
                for j in range(GROUP):
                    if j + 1 < GROUP:
                        transpose(j + 1)
                    pe.wait_ge(tc, g * GROUP + (j + 1))
                    if j >= 2:
                        pe.wait_ge(ev, g * GROUP + (j - 1))
                    for c in range(2):
                        last = pe.matmul(po[:, j % 2, 0:n_out], xT[:, j, c, :], rhs[:, c, :],
                                         start=c == 0, stop=c == 1)
                    last.then_inc(pj, 1)
                pe.wait_ge(ev, g * GROUP + GROUP)
                pe.nop(nofuse=True).then_inc(gf, 1)



def store_gat_tables(k, S, C, pr, T):
    nc = k.nc
    st = k.sem("gat_tables_stored")
    ca = k.sem("dst_terms_kept")
    with ExitStack() as ctx:
        block = ctx.enter_context(nc.Block())

        @block.sync
        def _(sp):
            for i in range(S.NT // GROUP):
                a, b = i * GROUP, (i + 1) * GROUP
                sp.dma_start(T.h[a * P:b * P, :].rearrange("(i p) d -> p i d", p=P), pr[:, a:b, 0:S.D]).then_inc(st, 16)
            sp.dma_start(T.asrc.rearrange("(i p) h -> p i h", p=P), pr[:, :, S.D:S.D + S.H]).then_inc(st, 16)
            sp.wait_ge(st, 16 * (S.NT // GROUP + 1))

        @block.vector
        def _(dve):
            dve.tensor_copy(C.adst[:, :, :], pr[:, :, S.D + S.H:S.D + 2 * S.H]).then_inc(ca, 1)


def gather_source_terms(k, S, C, ins, T, ea):
    nc = k.nc
    CH = 16
    chunks = S.ET // CH
    assert S.ET % (2 * CH) == 0
    src_pt = ins["src"].rearrange("(p t) -> p t", t=S.ET)
    il = k.sems("src_chunk_loaded", 2)
    ga = k.sems("terms_gathered", 2)
    cp = k.sem("terms_copied")
    al = k.sem("edges_loaded")
    oh = k.sem("source_onehots_ready")
    hs = k.sem("source_onehots_used")
    ch = k.sem("gather_chain")
    zm = k.sem("zeros_ready")
    zs = k.sem("buffers_zeroed")
    with ExitStack() as ctx:
        idx = k.sb(ctx, "src_chunk", [S.EP, 2, CH], I32)
        rows = k.sb(ctx, "term_rows", [S.EP, 2, CH * S.H])
        si = k.sb(ctx, "src_int", [S.EP, S.ET], I32)
        hi_i = k.sb(ctx, "src_hi_int", [S.EP, S.ET], I32)
        hi = k.sb(ctx, "src_hi", [S.EP, S.ET])
        lo = k.sb(ctx, "src_lo", [S.EP, S.ET])
        ohl = k.sb(ctx, "onehot_lo", [S.EP, 2, CH, P], BF16)
        ohh = k.sb(ctx, "onehot_hi", [S.EP, 2, CH, S.NT], BF16)
        zz = k.sb(ctx, "zeros_bf", [S.EP, P], BF16)
        zf = k.sb(ctx, "zeros_f", [P, ZCOLS])
        pd = k.ps(ctx, "source_counts", [P, S.NT])
        block = ctx.enter_context(nc.Block())

        @block.sync
        def _(sp):
            sp.dma_start(si[:, :], src_pt).then_inc(al, 16)
            for b in range(2):
                sp.dma_start(idx[:, b, :], src_pt[:, b * CH:(b + 1) * CH]).then_inc(il[b], 16)
            with sp.Fori(1, chunks // 2) as i:
                for b in range(2):
                    sp.wait_ge(ga[b], i * (16 * CH))
                    sp.dma_start(idx[:, b, :], src_pt[:, bass.ds((i * 2 + b) * CH, CH)]).then_inc(il[b], 16)

            n = 0
            sp.wait_ge(zm, 1)
            for buf in [*T.yf, T.xb1[0:S.G1 * TOK, :], T.xb2[0:S.G2 * TOK, :]]:
                flat = buf.rearrange("(p r) d -> p (r d)", p=P)
                for at in range(0, flat.shape[1], ZCOLS):
                    w = min(ZCOLS, flat.shape[1] - at)
                    sp.dma_start(flat[:, at:at + w], zf[:, 0:w]).then_inc(zs, 16)
                    n += 16
            sp.wait_ge(zs, n)

        @block.gpsimd
        def _(pool):
            pool.memset(zf[:, :], 0.0).then_inc(zm, 1)

            def chunk(i, b, first):
                pool.wait_ge(il[b], i * 16 + 16)
                if not first:
                    pool.wait_ge(cp, i * 2 + (b - 1))
                pool.nop(nofuse=True)
                for t in range(CH):
                    pool.indirect_dma_start(
                        out=rows[:, b, t * S.H:(t + 1) * S.H], out_offset=None, in_=T.asrc[:, :],
                        in_offset=bass.IndirectOffsetOnAxis(ap=idx[:, b, t:t + 1], axis=0)).then_inc(ga[b], 16)
            for b in range(2):
                chunk(0, b, True)
            with pool.Fori(1, chunks // 2) as i:
                for b in range(2):
                    chunk(i, b, False)

        @block.scalar
        def _(act):
            with act.Fori(0, chunks // 2) as i:
                for b in range(2):
                    act.wait_ge(ga[b], i * (16 * CH) + 16 * CH)
                    nc.scalar.copy(ea[:, bass.ds((i * 2 + b) * CH, CH), 0:S.H],
                                   rows[:, b, :].rearrange("p (t h) -> p t h", h=S.H)).then_inc(cp, 1)

        @block.vector
        def _(dve):
            c = Chain(dve, ch)
            c.mark(dve.memset(zz[:, :], 0.0))
            dve.wait_ge(al, 16)
            c.link(dve.tensor_scalar(hi_i[:, :], si[:, :], P.bit_length() - 1, None, ALU.arith_shift_right))
            c.link(dve.tensor_copy(hi[:, :], hi_i[:, :]))
            c.link(dve.scalar_tensor_tensor(out=lo[:, :], in0=hi[:, :], scalar=-float(P), in1=si[:, :],
                                            op0=ALU.mult, op1=ALU.add))

            def chunk(i, b, first):
                if not first:
                    dve.wait_ge(hs, i * 2 + (b - 1))
                at = bass.ds((i * 2 + b) * CH, CH) if not first else slice(b * CH, (b + 1) * CH)
                dve.tensor_tensor(ohl[:, b, :, :], lo[:, at].unsqueeze(2).to_broadcast([S.EP, CH, P]),
                                  C.iota[0:S.EP, :].unsqueeze(1).to_broadcast([S.EP, CH, P]), ALU.is_equal)
                dve.tensor_tensor(ohh[:, b, :, :], hi[:, at].unsqueeze(2).to_broadcast([S.EP, CH, S.NT]),
                                  C.iota[0:S.EP, 0:S.NT].unsqueeze(1).to_broadcast([S.EP, CH, S.NT]),
                                  ALU.is_equal).then_inc(oh, 1)
            for b in range(2):
                chunk(0, b, True)
            with dve.Fori(1, chunks // 2) as i:
                for b in range(2):
                    chunk(i, b, False)
            dve.wait_ge(hs, chunks + 1)
            dve.tensor_scalar(C.in_deg[:, :], pd[:, :], 1.0, None, ALU.add).then_inc(ch, 1)

        @block.tensor
        def _(pe):
            pe.wait_ge(ch, 1)
            pe.matmul(pd[:, :], zz[:, :], zz[:, 0:S.NT], start=True, stop=False, skip_group_check=True)
            with pe.Fori(0, chunks // 2) as i:
                for b in range(2):
                    pe.wait_ge(oh, i * 2 + (b + 1))
                    for t in range(CH):
                        last = pe.matmul(pd[:, :], ohl[:, b, t, :], ohh[:, b, t, :], start=False, stop=False,
                                         skip_group_check=True)
                    last.then_inc(hs, 1)
            pe.matmul(pd[:, :], zz[:, :], zz[:, 0:S.NT], start=False, stop=True, skip_group_check=True).then_inc(hs, 1)


def edge_maxima(k, S, C, ins, T, ea):
    nc = k.nc
    EP, ET, H, NT = S.EP, S.ET, S.H, S.NT
    KC = S.KC
    ld = k.sem("dst_loaded")
    ch = k.sem("maxima_chain")
    tr = k.sem("totals_ready")
    tq = k.sem("totals_transposed")
    cr = k.sem("carry_ready")
    cb = k.sem("carry_back")
    cn = k.sem("window_counts_ready")
    cs = k.sem("window_counts_summed")
    sm = k.sem("edge_tails_ready")
    fl = k.sem("dst_edge_column_blank")
    df = k.sem("dst_as_float")
    tb = k.sem("step_table_ready")
    mx = k.sem("maxima_ready")
    st = k.sem("edge_arrays_saved")
    io = k.sem("step_numbers")
    with ExitStack() as ctx:
        di = k.sb(ctx, "dst_int", [EP, 1 + ET + 1], I32)
        sf = k.sb(ctx, "dst_float", [EP, ET])
        fs = k.sb(ctx, "starts_flag", [EP, ET])
        fe = k.sb(ctx, "ends_flag", [EP, ET])
        run = k.sb(ctx, "running", [EP, ET])
        fmin = k.sb(ctx, "flag_min", [EP, 2])
        tot = k.sb(ctx, "totals", [EP, 2, 2 * H])
        totT = k.sb(ctx, "totals_T", [H, 2, 2, EP])
        carT = k.sb(ctx, "carry_T", [H, 2, EP + 1])
        car = k.sb(ctx, "carry", [EP, 2, H])
        cnt = k.sb(ctx, "below_count", [P, NT])
        ends = k.sb(ctx, "window_end", [P, NT])
        wst = k.sb(ctx, "window_start", [P, NT])
        wn = k.sb(ctx, "window_steps", [P, NT])
        wn_i = k.sb(ctx, "window_steps_int", [P, NT], I32)
        kend = k.sb(ctx, "window_last_step", [P, NT])
        wbase = k.sb(ctx, "window_base", [P, NT])
        zero = k.sb(ctx, "window_zero", [P, NT])
        kg_i = k.sb(ctx, "step_number_int", [P, KC], I32)
        kg = k.sb(ctx, "step_number", [P, KC])
        cmp = k.sb(ctx, "step_compare", [P, KC, NT])
        ww = k.sb(ctx, "step_window", [P, KC])
        bb = k.sb(ctx, "step_base", [P, KC])
        tab = k.sb(ctx, "step_table", [P, 2, KC], I32)
        tail = k.sb(ctx, "tail_edges", [P, SUB * S.EW])
        tsd = k.sb(ctx, "tail_src_dst", [P, SUB, 2])
        tzi = k.sb(ctx, "tail_zero_int", [P, SUB], I32)
        sd = k.sb(ctx, "src_dst_float", [EP, ET, 2])
        si = k.sb(ctx, "src_int_list", [EP, ET], I32)
        sff = k.sb(ctx, "src_float", [EP, ET])
        ptot = k.ps(ctx, "totals_ps", [H, 2, P])
        pcar = k.ps(ctx, "carry_ps", [EP, H])
        pc = k.ps(ctx, "window_ps", [P, NT])
        block = ctx.enter_context(nc.Block())
        dst = ins["dst"]
        dst_pt = dst.rearrange("(p t) -> p t", t=ET)

        @block.sync
        def _(sp):
            sp.dma_start(di[:, 1:1 + ET], dst_pt).then_inc(ld, 16)
            sp.dma_start(si[:, :], ins["src"].rearrange("(p t) -> p t", t=ET)).then_inc(ld, 16)
            sp.wait_ge(fl, 2)
            sp.dma_start(di[1:EP, 0:1], dst_pt[0:EP - 1, ET - 1:ET], allow_slow_non_contiguous=True).then_inc(ld, 16)
            sp.dma_start(di[0:EP - 1, 1 + ET:2 + ET], dst_pt[1:EP, 0:1], allow_slow_non_contiguous=True).then_inc(ld, 16)
            sp.dma_start(T.src_i[0:S.E].rearrange("(a e) -> a e", a=16),
                         ins["src"].rearrange("(a e) -> a e", a=16)).then_inc(st, 16)
            sp.wait_ge(sm, 1)
            sp.dma_start(T.src_i[S.E:S.E + STEP].rearrange("(p j) -> p j", j=SUB), tzi[:, :]).then_inc(st, 16)
            sp.dma_start(T.dst_f[S.E:S.E + STEP].rearrange("(p j) -> p j", j=SUB), tail[:, 0:SUB]).then_inc(st, 16)
            sp.dma_start(T.src_f[S.E:S.E + STEP].rearrange("(p j) -> p j", j=SUB), tzi[:, :].bitcast(F32)).then_inc(st, 16)
            sp.dma_start(T.sd[S.E:S.E + STEP, :].rearrange("(p j) c -> p j c", j=SUB), tsd[:, :, :]).then_inc(st, 16)
            sp.dma_start(T.ea[S.E:S.E + STEP, :].rearrange("(p j) h -> p (j h)", j=SUB), tail[:, :]).then_inc(st, 16)
            sp.wait_ge(df, 1)
            sp.dma_start(T.dst_f[0:S.E].rearrange("(p t) -> p t", t=ET), sf[:, :]).then_inc(st, 16)
            sp.dma_start(T.src_f[0:S.E].rearrange("(p t) -> p t", t=ET), sff[:, :]).then_inc(st, 16)
            sp.dma_start(T.sd[0:S.E, :].rearrange("(p t) c -> p (t c)", t=ET),
                         sd[:, :, :].rearrange("p t c -> p (t c)")).then_inc(st, 16)
            sp.wait_ge(tb, 1)
            for a in range(2):
                sp.dma_start(T.steps[a, :].rearrange("(p c) -> p c", c=KC), tab[:, a, :]).then_inc(st, 16)
            sp.wait_ge(mx, 1)
            sp.dma_start(T.ea[0:S.E, :].rearrange("(p t) h -> p (t h)", t=ET),
                         ea[:, :, :].rearrange("p t h -> p (t h)")).then_inc(st, 16)
            sp.wait_ge(st, 16 * 12)

        @block.gpsimd
        def _(pool):
            pool.memset(tail[:, :], -1.0)
            pool.memset(tsd[:, :, 0], 0.0)
            pool.memset(tsd[:, :, 1], -1.0)
            pool.memset(tzi[:, :], 0).then_inc(sm, 1)
            pool.iota(kg_i[:, :], pattern=[[1, KC]], base=0, channel_multiplier=KC).then_inc(io, 1)

        @block.vector
        def _(dve):
            c = Chain(dve, ch)
            dve.memset(di[:, 0:1], -1).then_inc(fl, 1)
            dve.memset(di[:, 1 + ET:2 + ET], -1).then_inc(fl, 1)
            c.mark(dve.memset(carT[:, :, :], NEG_BIG))
            c.mark(dve.memset(zero[:, :], 0.0))
            c.link(dve.memset(cnt[:, :], 0.0))
            dve.wait_ge(ld, 64)
            c.mark(dve.tensor_tensor(fs[:, :], di[:, 1:1 + ET], di[:, 0:ET], ALU.not_equal))
            c.mark(dve.tensor_tensor(fe[:, :], di[:, 1:1 + ET], di[:, 2:2 + ET], ALU.not_equal))
            c.mark(dve.tensor_copy(sff[:, :], si[:, :]))
            c.mark(dve.tensor_copy(sd[:, :, 0], si[:, :]))
            c.mark(dve.tensor_copy(sd[:, :, 1], di[:, 1:1 + ET]))
            c.link(dve.tensor_copy(sf[:, :], di[:, 1:1 + ET]))
            dve.tensor_copy(ea[:, :, 2 * H], sf[:, :]).then_inc(df, 1)
            c.mark(dve.tensor_scalar(fs[:, :], fs[:, :], NEG_BIG, None, ALU.mult))
            c.link(dve.tensor_scalar(fe[:, :], fe[:, :], NEG_BIG, None, ALU.mult))
            for w in range(NT):
                c.link(dve.tensor_scalar(run[:, :], sf[:, :], float((w + 1) * P), 0.0, ALU.is_lt, ALU.add,
                                         accum_out=cnt[0:EP, w:w + 1]))
            dve.nop(nofuse=True).then_inc(cn, 1)
            c.mark(dve.tensor_reduce(fmin[:, 0:1], fs[:, :], AX.X, ALU.min))
            c.link(dve.tensor_reduce(fmin[:, 1:2], fe[:, :], AX.X, ALU.min))
            for a in range(2):
                c.link(dve.tensor_copy(tot[:, a, H:2 * H], fmin[:, a:a + 1].to_broadcast([EP, H])))
            for a in range(2):
                forward = a == 0

                def scan(h, out, initial):
                    data = ea[:, :, h] if forward else ea[:, ::-1, H + h]
                    flag = fs[:, :] if forward else fe[:, ::-1]
                    c.link(dve.tensor_tensor_scan(out, flag, data, initial, ALU.add, ALU.max))
                for h in range(H):
                    scan(h, run[:, :], NEG_BIG)
                    c.link(dve.tensor_copy(tot[:, a, h:h + 1], run[:, ET - 1:ET]))
                dve.nop(nofuse=True).then_inc(tr, 1)
                dve.wait_ge(tq, a + 1)
                c.link(dve.tensor_copy(totT[:, a, :, :], ptot[:, :, 0:EP]))
                if forward:
                    c.link(dve.tensor_tensor_scan(carT[:, a, 1:EP + 1], totT[:, a, 1, :], totT[:, a, 0, :], NEG_BIG,
                                                  ALU.add, ALU.max))
                else:
                    c.link(dve.tensor_tensor_scan(carT[:, a, 0:EP][:, ::-1], totT[:, a, 1, ::-1],
                                                  totT[:, a, 0, ::-1], NEG_BIG, ALU.add, ALU.max))
                dve.nop(nofuse=True).then_inc(cr, 1)
                dve.wait_ge(cb, a + 1)
                c.link(dve.tensor_copy(car[:, a, :], pcar[:, :]))
                for h in range(H):
                    scan(h, ea[:, :, H + h] if forward else ea[:, ::-1, H + h], car[:, a, h:h + 1])
            dve.nop(nofuse=True).then_inc(mx, 1)
            dve.wait_ge(cs, 1)
            dve.wait_ge(io, 1)
            c.link(dve.tensor_copy(kg[:, :], kg_i[:, :]))
            c.link(dve.memset(wst[:, 0:1], 0.0))
            c.link(dve.tensor_copy(ends[:, :], pc[:, :]))
            c.link(dve.tensor_copy(wst[:, 1:NT], ends[:, 0:NT - 1]))
            c.link(dve.tensor_tensor(wn[:, :], ends[:, :], wst[:, :], ALU.subtract))
            c.link(dve.tensor_scalar(wn_i[:, :], wn[:, :], float(STEP - 1), None, ALU.add))
            c.link(dve.tensor_scalar(wn_i[:, :], wn_i[:, :], STEP.bit_length() - 1, None, ALU.arith_shift_right))
            c.link(dve.tensor_copy(wn[:, :], wn_i[:, :]))
            c.link(dve.tensor_tensor_scan(kend[:, :], zero[:, :], wn[:, :], 0.0, ALU.add, ALU.add))
            c.link(dve.tensor_tensor(wbase[:, :], kend[:, :], wn[:, :], ALU.subtract))
            c.link(dve.scalar_tensor_tensor(out=wbase[:, :], in0=wbase[:, :], scalar=-float(STEP), in1=wst[:, :],
                                            op0=ALU.mult, op1=ALU.add))
            grid = [P, KC, NT]
            c.link(dve.tensor_tensor(cmp[:, :, :], kend[:, :].unsqueeze(1).to_broadcast(grid),
                                     kg[:, :].unsqueeze(2).to_broadcast(grid), ALU.is_le))
            c.link(dve.tensor_reduce(ww[:, :], cmp[:, :, :], AX.X, ALU.add))
            c.link(dve.tensor_tensor(cmp[:, :, :], C.iota[:, 0:NT].unsqueeze(1).to_broadcast(grid),
                                     ww[:, :].unsqueeze(2).to_broadcast(grid), ALU.is_equal))
            c.link(dve.tensor_tensor(cmp[:, :, :], cmp[:, :, :], wbase[:, :].unsqueeze(1).to_broadcast(grid),
                                     ALU.mult))
            c.link(dve.tensor_reduce(bb[:, :], cmp[:, :, :], AX.X, ALU.add))
            c.link(dve.scalar_tensor_tensor(out=bb[:, :], in0=kg[:, :], scalar=float(STEP), in1=bb[:, :],
                                            op0=ALU.mult, op1=ALU.add))
            c.link(dve.tensor_scalar(tab[:, 0, :], ww[:, :], float(NT - 1), None, ALU.min))
            c.link(dve.tensor_scalar(tab[:, 1, :], bb[:, :], float(S.E), None, ALU.min))
            dve.nop(nofuse=True).then_inc(tb, 1)

        @block.tensor
        def _(pe):
            pe.wait_ge(cn, 1)
            pe.matmul(pc[:, :], C.ones[:, :], cnt[:, :], start=True, stop=True).then_inc(cs, 1)
            for a in range(2):
                pe.wait_ge(tr, a + 1)
                pe.transpose(ptot[:, 0, 0:EP], tot[:, a, 0:H], C.ident[0:EP, 0:EP])
                pe.transpose(ptot[:, 1, 0:EP], tot[:, a, H:2 * H], C.ident[0:EP, 0:EP]).then_inc(tq, 1)
                pe.wait_ge(cr, a + 1)
                pe.transpose(pcar[:, :], carT[:, a, a:a + EP], C.ident[0:H, 0:H]).then_inc(cb, 1)



def load_step_table(k, S, sp, T, tab, sem):
    sp.dma_start(tab[0:1, :, :], T.steps.rearrange("a (b k) -> b a k", b=1)).then_inc(sem, 16)


def gat_edges(k, S, C, T, acc):
    nc = k.nc
    DEPTH = GAT_DEPTH
    H, HD, D, W = S.H, S.HD, S.D, S.D + S.H + 1
    tl = k.sem("gat_table_loaded")
    ld = k.sems("gat_step_loaded", DEPTH)
    ga = k.sems("gat_rows_gathered", DEPTH)
    oh = k.sem("gat_onehot_ready")
    ad = k.sem("gat_dst_terms_ready")
    ch = k.sem("gat_exponent_chain")
    ex = k.sem("gat_exp_ready")
    ms = k.sem("gat_messages_ready")
    sc = k.sem("gat_step_summed")
    dn = k.sem("gat_step_done")
    cl = k.sem("gat_acc_clear")
    with ExitStack() as ctx:
        tab = k.sb(ctx, "gat_table", [1, 2, P * S.KC], I32)
        idx = k.sb(ctx, "gat_idx", [P, DEPTH, SUB], I32)
        ed = k.sb(ctx, "gat_terms", [P, DEPTH, SUB, S.EW])
        row = k.sb(ctx, "gat_dst_row", [P, DEPTH, STEP])
        g = k.sb(ctx, "gat_rows", [P, DEPTH, SUB, D])
        oT = k.sb(ctx, "gat_onehot_T", [P, DEPTH, SUB, P])
        o = k.sb(ctx, "gat_onehot", [P, DEPTH, SUB, P])
        z = k.sb(ctx, "gat_z", [P, DEPTH, SUB, 2 * H])
        y = k.sb(ctx, "gat_leaky", [P, DEPTH, SUB, 2 * H])
        q = k.sb(ctx, "gat_exponent", [P, DEPTH, SUB, H])
        m = k.sb(ctx, "gat_messages", [P, DEPTH, SUB, W])
        pa = k.ps(ctx, "gat_dst_ps", [P, 2, 512])
        po = k.ps(ctx, "gat_sum_ps", [P, 2, 512])
        block = ctx.enter_context(nc.Block())

        @block.sync
        def _(sp):
            load_step_table(k, S, sp, T, tab, tl)
            sp.wait_ge(tl, 16)

            def load(i, b, t, first):
                base = sp.value_load(tab[0:1, 1, bass.ds(t, 1)], min_val=0, max_val=S.E)
                if not first:
                    sp.wait_ge(dn, t - (DEPTH - 1))
                    sp.nop(nofuse=True)
                sp.dma_start(idx[:, b, :], T.src_i[bass.ds(base, STEP)].rearrange("(p j) -> p j", j=SUB)).then_inc(ld[b], 16)
                sp.dma_start(ed[:, b, :, :], T.ea[bass.ds(base, STEP), :].rearrange("(p j) h -> p j h", j=SUB)).then_inc(ld[b], 16)
                sp.dma_start(row[:, b, :], T.dst_f[bass.ds(base, STEP)].partition_broadcast(P)).then_inc(ld[b], 16)
            staged(sp, S.STEPS, [load], DEPTH)

        @block.gpsimd
        def _(pool):
            def gather(i, b, t, first):
                pool.wait_ge(ld[b], i * 48 + 48)
                pool.nop(nofuse=True)
                for j in range(SUB):
                    pool.indirect_dma_start(
                        out=g[:, b, j, :], out_offset=None, in_=T.h[:, :],
                        in_offset=bass.IndirectOffsetOnAxis(ap=idx[:, b, j:j + 1], axis=0)).then_inc(ga[b], 16)
            staged(pool, S.STEPS, [gather], DEPTH)

        @block.vector
        def _(dve):
            dve.memset(acc[:, :, :], 0.0).then_inc(cl, 1)
            for b in range(DEPTH):
                dve.memset(m[:, b, :, W - 1:W], 1.0)
            dve.wait_ge(cl, 1)
            dve.wait_ge(tl, 16)

            def onehots(i, b, t, first):
                w = dve.value_load(tab[0:1, 0, bass.ds(t, 1)], min_val=0, max_val=S.NT - 1)
                dve.wait_ge(ld[b], i * 48 + 48)
                dve.tensor_scalar(oT[:, b, :, :], row[:, b, :].rearrange("p (e j) -> p j e", j=SUB),
                                  C.wiota[:, bass.ds(w, 1)], None, ALU.is_equal)
                for j in range(SUB):
                    last = dve.tensor_scalar(o[:, b, j, :], C.iota_n[:, bass.ds(w * P, P)],
                                             ed[:, b, j, 2 * H:2 * H + 1], None, ALU.is_equal)
                last.then_inc(oh, 1)

            def exponents(i, b, t, first):
                dve.wait_ge(ad, t + 1)
                dve.tensor_tensor(z[:, b, :, :].rearrange("p j (a h) -> p j a h", a=2),
                                  ed[:, b, :, 0:2 * H].rearrange("p j (a h) -> p j a h", a=2),
                                  pa[:, b % 2, 0:SUB * H].rearrange("p (j h) -> p j h", j=SUB).unsqueeze(2)
                                  .to_broadcast([P, SUB, 2, H]), ALU.add).then_inc(ch, 1)
                dve.wait_ge(ch, t * 3 + 1)
                dve.scalar_tensor_tensor(out=y[:, b, :, :], in0=z[:, b, :, :], scalar=0.2, in1=z[:, b, :, :],
                                         op0=ALU.mult, op1=ALU.max).then_inc(ch, 1)
                dve.wait_ge(ch, t * 3 + 2)
                dve.tensor_tensor(q[:, b, :, :], y[:, b, :, 0:H], y[:, b, :, H:2 * H], ALU.subtract).then_inc(ch, 1)

            def messages(i, b, t, first):
                dve.wait_ge(ex, t + 1)
                dve.wait_ge(ga[b], i * (16 * SUB) + 16 * SUB)
                for j in range(SUB):
                    last = dve.tensor_tensor(m[:, b, j, 0:D].rearrange("p (h d) -> p h d", h=H),
                                             g[:, b, j, :].rearrange("p (h d) -> p h d", h=H),
                                             m[:, b, j, D:D + H].unsqueeze(2).to_broadcast([P, H, HD]), ALU.mult)
                last.then_inc(ms, 1)

            def add(i, b, t, first):
                w = dve.value_load(tab[0:1, 0, bass.ds(t, 1)], min_val=0, max_val=S.NT - 1)
                dve.wait_ge(sc, t + 1)
                if not (first and b == 0):
                    dve.wait_ge(dn, t)
                a = acc[:, bass.ds(w, 1), :].rearrange("p a c -> p (a c)")
                dve.tensor_tensor(a, a, po[:, b % 2, 0:W], ALU.add).then_inc(dn, 1)
            staged(dve, S.STEPS, [onehots, exponents, messages, add], DEPTH)

        @block.scalar
        def _(act):
            def numerators(i, b, t, first):
                act.wait_ge(ch, t * 3 + 3)
                nc.scalar.activation(m[:, b, :, D:D + H], q[:, b, :, :], ACT.Exp).then_inc(ex, 1)
            staged(act, S.STEPS, [numerators], DEPTH)

        @block.tensor
        def _(pe):
            pe.wait_ge(tl, 16)

            def dst_terms(i, b, t, first):
                w = pe.value_load(tab[0:1, 0, bass.ds(t, 1)], min_val=0, max_val=S.NT - 1)
                pe.wait_ge(oh, t + 1)
                if not (first and b < 2):
                    pe.wait_ge(ch, t * 3 - 5)
                for j in range(SUB):
                    last = pe.matmul(pa[:, b % 2, j * H:(j + 1) * H], oT[:, b, j, :],
                                     C.adst[:, bass.ds(w, 1), :].rearrange("p a h -> p (a h)"), start=True, stop=True)
                last.then_inc(ad, 1)

            def scatter(i, b, t, first):
                pe.wait_ge(ms, t + 1)
                if not (first and b < 2):
                    pe.wait_ge(dn, t - 1)
                for j in range(SUB):
                    last = pe.matmul(po[:, b % 2, 0:W], o[:, b, j, :], m[:, b, j, :],
                                     start=j == 0, stop=j == SUB - 1)
                last.then_inc(sc, 1)
            staged(pe, S.STEPS, [dst_terms, None, scatter], DEPTH)


def gat_finish(k, S, C, acc, x_res, x_dram):
    nc = k.nc
    NT, H, D = S.NT, S.H, S.D
    xl = k.sem("residual_x_loaded")
    ch = k.sem("gat_finish_chain")
    with ExitStack() as ctx:
        den = k.sb(ctx, "gat_den", [P, NT, H])
        block = ctx.enter_context(nc.Block())

        @block.gpsimd
        def _(pool):
            pool.memset(x_res[:, NT - 1, :], 0.0).then_inc(xl, 1)

        @block.sync
        def _(sp):
            sp.wait_ge(xl, 1)
            full, tail = rows_of(x_dram, S)
            sp.dma_start(x_res[:, 0:NT - 1, :], full).then_inc(xl, 16)
            sp.dma_start(x_res[0:S.TAIL, NT - 1, :], tail).then_inc(xl, 16)

        @block.vector
        def _(dve):
            c = Chain(dve, ch)
            out = acc[:, :, 0:D]
            heads = out.rearrange("p n (h d) -> p n h d", h=H)
            c.mark(dve.tensor_scalar(C.out_deg[:, :], acc[:, :, D + H], 1.0, None, ALU.add))
            c.link(dve.tensor_scalar(den[:, :, :], acc[:, :, D:D + H], 1e-16, None, ALU.add))
            c.link(dve.reciprocal(den[:, :, :], den[:, :, :]))
            c.link(dve.tensor_tensor(heads, heads, den[:, :, :].unsqueeze(3).to_broadcast([P, NT, H, S.HD]), ALU.mult))
            c.link(dve.tensor_tensor(out, out, C.gat_bias[:, :].unsqueeze(1).to_broadcast([P, NT, D]), ALU.add))
            dve.wait_ge(xl, 33)
            c.link(dve.scalar_tensor_tensor(out=x_res[:, :, :], in0=out, scalar=0.0, in1=x_res[:, :, :],
                                            op0=ALU.max, op1=ALU.add))



def gnn_scale(k, S, C, T, z):
    nc = k.nc
    ch = k.sem("scale_chain")
    rt = k.sem("degree_roots")
    st = k.sem("zb_stored")
    with ExitStack() as ctx:
        sd = k.sb(ctx, "degree_root", [P, 2, S.NT])
        block = ctx.enter_context(nc.Block())

        @block.scalar
        def _(act):
            nc.scalar.activation(sd[:, 0, :], C.out_deg[:, :], ACT.Sqrt).then_inc(rt, 1)
            nc.scalar.activation(sd[:, 1, :], C.in_deg[:, :], ACT.Sqrt).then_inc(rt, 1)

        @block.vector
        def _(dve):
            c = Chain(dve, ch)
            dve.wait_ge(rt, 2)
            c.link(dve.reciprocal(C.dinv[:, :, :], sd[:, :, :]))
            for a in (1, 0):
                part = z[:, :, a * P:(a + 1) * P]
                c.mark(dve.tensor_tensor(part, part, C.dinv[:, a, :].unsqueeze(2).to_broadcast([P, S.NT, P]), ALU.mult))

        @block.sync
        def _(sp):
            sp.wait_ge(ch, 2)
            sp.dma_start(T.zb.rearrange("(i p) d -> p i d", p=P), z[:, :, P:2 * P]).then_inc(st, 16)
            sp.wait_ge(st, 16)


def gnn_edges(k, S, C, T, z, acc):
    nc = k.nc
    DEPTH = GNN_DEPTH
    DUP_OPS = 4
    SPARE = S.NT * P
    tl = k.sem("gnn_table_loaded")
    ld = k.sems("gnn_step_loaded", DEPTH)
    ga = k.sems("gnn_rows_gathered", DEPTH)
    oh = k.sem("gnn_onehot_ready")
    dp = k.sem("gnn_duplicate_chain")
    pc = k.sem("gnn_pair_ready")
    mc = k.sem("gnn_pair_copied")
    pm = k.sem("gnn_message_ready")
    ms = k.sem("gnn_message_copied")
    sc = k.sem("gnn_step_summed")
    dn = k.sem("gnn_step_done")
    sa = k.sems("gnn_rows_added", 2)
    cl = k.sem("gnn_acc_clear")
    with ExitStack() as ctx:
        tab = k.sb(ctx, "gnn_table", [1, 2, P * S.KC], I32)
        idx = k.sb(ctx, "gnn_idx", [P, DEPTH, SUB], I32)
        sd = k.sb(ctx, "gnn_src_dst", [P, DEPTH, SUB, 2])
        row = k.sb(ctx, "gnn_src_row", [P, DEPTH, STEP])
        g = k.sb(ctx, "gnn_rows", [P, DEPTH, SUB, P])
        o = k.sb(ctx, "gnn_onehot", [P, DEPTH, SUB, P])
        eq = k.sb(ctx, "gnn_same_src", [P, DEPTH, SUB, P])
        junk = k.sb(ctx, "gnn_junk", [P, 2, SUB, P])
        dup = k.sb(ctx, "gnn_earlier", [P, DEPTH, SUB])
        away = k.sb(ctx, "gnn_away", [P, DEPTH, SUB])
        to = k.sb(ctx, "gnn_add_idx", [P, DEPTH, SUB], I32)
        spare = k.sb(ctx, "gnn_spare", [P, 1])
        pr = k.sb(ctx, "gnn_pair", [P, DEPTH, SUB, P])
        m = k.sb(ctx, "gnn_message", [P, DEPTH, SUB, P])
        pp = k.ps(ctx, "gnn_pair_ps", [P, 2, 512])
        pq = k.ps(ctx, "gnn_message_ps", [P, 2, 512])
        po = k.ps(ctx, "gnn_sum_ps", [P, 2, 512])
        block = ctx.enter_context(nc.Block())

        @block.sync
        def _(sp):
            load_step_table(k, S, sp, T, tab, tl)
            sp.wait_ge(tl, 16)

            def load(i, b, t, first):
                base = sp.value_load(tab[0:1, 1, bass.ds(t, 1)], min_val=0, max_val=S.E)
                if not first:
                    sp.wait_ge(dn, t - (DEPTH - 1))
                    sp.nop(nofuse=True)
                    sp.wait_ge(dp, (t - (DEPTH - 1)) * DUP_OPS)
                    sp.nop(nofuse=True)
                sp.dma_start(idx[:, b, :], T.src_i[bass.ds(base, STEP)].rearrange("(p j) -> p j", j=SUB)).then_inc(ld[b], 16)
                sp.dma_start(sd[:, b, :, :], T.sd[bass.ds(base, STEP), :].rearrange("(p j) c -> p j c", j=SUB)).then_inc(ld[b], 16)
                sp.dma_start(row[:, b, :], T.src_f[bass.ds(base, STEP)].partition_broadcast(P)).then_inc(ld[b], 16)
            staged(sp, S.STEPS, [load], DEPTH)

        @block.gpsimd
        def _(pool):
            def gather(i, b, t, first):
                pool.wait_ge(ld[b], i * 48 + 48)
                pool.nop(nofuse=True)
                for j in range(SUB):
                    pool.indirect_dma_start(
                        out=g[:, b, j, :], out_offset=None, in_=T.zb[:, :],
                        in_offset=bass.IndirectOffsetOnAxis(ap=idx[:, b, j:j + 1], axis=0)).then_inc(ga[b], 16)

            def add_rows(i, b, t, first):
                pool.wait_ge(ms, t + 1)
                if not (first and b < 2):
                    pool.wait_ge(sa[b % 2], i * (16 * SUB * (DEPTH // 2)) + 16 * SUB * (b // 2))
                pool.nop(nofuse=True)
                for j in range(SUB):
                    pool.indirect_dma_start(
                        out=T.yf[SUB * (b % 2) + j][:, :],
                        out_offset=bass.IndirectOffsetOnAxis(ap=to[:, b, j:j + 1], axis=0),
                        in_=m[:, b, j, :], in_offset=None, compute_op=ALU.add).then_inc(sa[b % 2], 16)
            staged(pool, S.STEPS, [gather, None, add_rows], DEPTH)
            for b in range(2):
                pool.wait_ge(sa[b], 16 * SUB * (S.STEPS // 2))

        @block.vector
        def _(dve):
            dve.memset(acc[:, :, :], 0.0).then_inc(cl, 1)
            dve.tensor_scalar(spare[:, :], C.wiota[:, 0:1], float(SPARE), None, ALU.add).then_inc(cl, 1)
            dve.wait_ge(cl, 2)
            dve.wait_ge(tl, 16)

            def onehots(i, b, t, first):
                w = dve.value_load(tab[0:1, 0, bass.ds(t, 1)], min_val=0, max_val=S.NT - 1)
                dve.wait_ge(ld[b], i * 48 + 48)
                if not first:
                    dve.wait_ge(sa[b % 2], i * (16 * SUB * (DEPTH // 2)) + (16 * SUB * (b // 2) - 16 * SUB * (DEPTH // 2 - 1)))
                for j in range(SUB):
                    dve.tensor_scalar(o[:, b, j, :], C.iota_n[:, bass.ds(w * P, P)], sd[:, b, j, 1:2], None,
                                      ALU.is_equal)
                    last = dve.tensor_scalar(eq[:, b, j, :], row[:, b, :].rearrange("p (e j) -> p j e", j=SUB)[:, j, :],
                                             sd[:, b, j, 0:1], None, ALU.is_equal)
                last.then_inc(oh, 1)

            def row_numbers(i, b, t, first):
                dve.wait_ge(oh, t + 1)
                for j in range(SUB):
                    last = dve.tensor_tensor_reduce(out=junk[:, b % 2, j, :], in0=eq[:, b, j, :], in1=C.lower[:, :], scale=1.0,
                                                    scalar=0.0, op0=ALU.mult, op1=ALU.add,
                                                    accum_out=dup[:, b, j:j + 1])
                last.then_inc(dp, 1)
                dve.tensor_scalar(away[:, b, :], sd[:, b, :, 0], -1.0, spare[:, 0:1], ALU.mult, ALU.add).then_inc(dp, 1)
                dve.wait_ge(dp, t * DUP_OPS + 2)
                dve.scalar_tensor_tensor(out=away[:, b, :], in0=dup[:, b, :], scalar=0.5, in1=away[:, b, :],
                                         op0=ALU.is_gt, op1=ALU.mult).then_inc(dp, 1)
                dve.wait_ge(dp, t * DUP_OPS + 3)
                dve.tensor_tensor(to[:, b, :], away[:, b, :], sd[:, b, :, 0], ALU.add).then_inc(dp, 1)

            def add(i, b, t, first):
                w = dve.value_load(tab[0:1, 0, bass.ds(t, 1)], min_val=0, max_val=S.NT - 1)
                dve.wait_ge(sc, t + 1)
                if not (first and b == 0):
                    dve.wait_ge(dn, t)
                a = acc[:, bass.ds(w, 1), :].rearrange("p a c -> p (a c)")
                dve.tensor_tensor(a, a, po[:, b % 2, 0:P], ALU.add).then_inc(dn, 1)
            staged(dve, S.STEPS, [onehots, row_numbers, add], DEPTH)

        @block.scalar
        def _(act):
            def pairs(i, b, t, first):
                act.wait_ge(pc, t + 1)
                nc.scalar.copy(pr[:, b, :, :], pp[:, b % 2, 0:SUB * P].rearrange("p (j e) -> p j e", j=SUB)).then_inc(mc, 1)

            def messages(i, b, t, first):
                act.wait_ge(pm, t + 1)
                act.wait_ge(dp, t * DUP_OPS + DUP_OPS)
                if not first:
                    act.wait_ge(sa[b % 2], i * (16 * SUB * (DEPTH // 2)) + (16 * SUB * (b // 2) - 16 * SUB * (DEPTH // 2 - 1)))
                nc.scalar.copy(m[:, b, :, :], pq[:, b % 2, 0:SUB * P].rearrange("p (j e) -> p j e", j=SUB)).then_inc(ms, 1)
            staged(act, S.STEPS, [pairs, messages], DEPTH)

        @block.tensor
        def _(pe):
            pe.wait_ge(tl, 16)

            def pairs(i, b, t, first):
                pe.wait_ge(oh, t + 1)
                if not (first and b < 2):
                    pe.wait_ge(mc, t - 1)
                for j in range(SUB):
                    last = pe.matmul(pp[:, b % 2, j * P:(j + 1) * P], o[:, b, j, :], eq[:, b, j, :],
                                     start=True, stop=True)
                last.then_inc(pc, 1)

            def messages(i, b, t, first):
                w = pe.value_load(tab[0:1, 0, bass.ds(t, 1)], min_val=0, max_val=S.NT - 1)
                pe.wait_ge(mc, t + 1)
                if not (first and b < 2):
                    pe.wait_ge(ms, t - 1)
                for j in range(SUB):
                    last = pe.matmul(pq[:, b % 2, j * P:(j + 1) * P], pr[:, b, j, :],
                                     z[:, bass.ds(w, 1), 0:P].rearrange("p a c -> p (a c)"), start=True, stop=True)
                last.then_inc(pm, 1)
                pe.wait_ge(ga[b], i * (16 * SUB) + 16 * SUB)
                if not (first and b < 2):
                    pe.wait_ge(dn, t - 1)
                for j in range(SUB):
                    last = pe.matmul(po[:, b % 2, 0:P], o[:, b, j, :], g[:, b, j, :], start=j == 0, stop=j == SUB - 1)
                last.then_inc(sc, 1)
            staged(pe, S.STEPS, [pairs, messages], DEPTH)


def gnn_finish(k, S, C, T, z, acc, x_res):
    nc = k.nc
    NT = S.NT
    ld = k.sems("forward_sums_loaded", 2)
    us = k.sems("forward_sums_used", 2)
    ch = k.sem("gnn_finish_chain")
    HALF = 7
    with ExitStack() as ctx:
        f = k.sb(ctx, "forward_sums_sb", [P, 2, HALF, P])
        block = ctx.enter_context(nc.Block())
        parts = [(g, y) for g in range(NT // HALF) for y in range(2 * SUB)]

        @block.sync
        def _(sp):
            for n, (g, y) in enumerate(parts):
                if n >= 2:
                    sp.wait_ge(us[n % 2], n // 2)
                sp.dma_start(f[:, n % 2, :, :], T.yf[y][g * HALF * P:(g + 1) * HALF * P, :]
                             .rearrange("(i p) d -> p i d", p=P)).then_inc(ld[n % 2], 16)

        @block.vector
        def _(dve):
            c = Chain(dve, ch)
            for n, (g, y) in enumerate(parts):
                part = z[:, g * HALF:(g + 1) * HALF, 0:P]
                dve.wait_ge(ld[n % 2], 16 * (n // 2 + 1))
                dve.tensor_tensor(part, part, f[:, n % 2, :, :], ALU.add).then_inc(us[n % 2], 1)
                dve.wait_ge(us[n % 2], n // 2 + 1)
            back = z[:, :, P:2 * P]
            c.link(dve.tensor_tensor(back, back, acc[:, :, :], ALU.add))
            for a in range(2):
                part = z[:, :, a * P:(a + 1) * P]
                c.link(dve.tensor_tensor(part, part, C.dinv[:, 1 - a, :].unsqueeze(2).to_broadcast([P, NT, P]),
                                         ALU.mult))
            c.link(dve.tensor_tensor(z[:, :, :], z[:, :, :],
                                     C.gnn_bias[:, :].unsqueeze(1).to_broadcast([P, NT, S.D]), ALU.add))
            c.link(dve.tensor_tensor(x_res[:, :, :], x_res[:, :, :], z[:, :, :], ALU.add))



def route(k, S, C, tag, logits, bias, choices, n_exp, capacity, idx_put, idx_get, weight, gtab):
    nc = k.nc
    NT, X = S.NT, n_exp
    groups = S.G1 if capacity is None else S.G2
    ch = k.sem(f"{tag}_route_chain")
    ex = k.sem(f"{tag}_route_exp_in")
    eo = k.sem(f"{tag}_route_exp_out")
    mr = k.sem(f"{tag}_route_mask_ready")
    rk = k.sem(f"{tag}_route_ranks")
    io = k.sem(f"{tag}_route_iota")
    with ExitStack() as ctx:
        lg = k.sb(ctx, f"{tag}_logits", [P, NT, X])
        t0 = k.sb(ctx, f"{tag}_t0", [P, NT, X])
        pv = k.sb(ctx, f"{tag}_pv", [P, NT, X])
        mk = k.sb(ctx, f"{tag}_masks", [P, choices, NT, X])
        both = k.sb(ctx, f"{tag}_both", [P, NT, X])
        mx = k.sb(ctx, f"{tag}_mx", [P, choices, NT])
        ix = k.sb(ctx, f"{tag}_ix", [P, NT])
        dd = k.sb(ctx, f"{tag}_dd", [P, NT])
        valid = k.sb(ctx, f"{tag}_valid", [P, NT])
        pos = k.sb(ctx, f"{tag}_pos", [P, NT, X])
        tot = k.sb(ctx, f"{tag}_tot", [P, X, NT])
        car = k.sb(ctx, f"{tag}_car", [P, X, NT + 1])
        zero = k.sb(ctx, f"{tag}_zero", [P, max(NT, X)])
        ng = k.sb(ctx, f"{tag}_ng", [P, X])
        ng_i = k.sb(ctx, f"{tag}_ng_i", [P, X], I32)
        gend = k.sb(ctx, f"{tag}_gend", [P, X])
        base = k.sb(ctx, f"{tag}_base", [P, X])
        sl = k.sb(ctx, f"{tag}_slot", [P, NT])
        kp = k.sb(ctx, f"{tag}_kept", [P, NT])
        gc = k.sb(ctx, f"{tag}_gcmp", [P, groups, X])
        gw = k.sb(ctx, f"{tag}_gw", [P, groups])
        pk = k.ps(ctx, f"{tag}_rank_ps", [P, 512])
        pt = k.ps(ctx, f"{tag}_total_ps", [P, 512])
        block = ctx.enter_context(nc.Block())
        grid = [P, NT, X]

        def wide(v):
            return v.unsqueeze(2).to_broadcast(grid)

        def over(v):
            return v.unsqueeze(1).to_broadcast(grid)

        @block.vector
        def _(dve):
            c = Chain(dve, ch)
            tt, ts = dve.tensor_tensor, dve.tensor_scalar
            c.link(tt(lg[:, :, :], logits[:, :, :], over(bias[:, :]), ALU.add))
            c.link(dve.memset(zero[:, :], 0.0))
            c.link(ts(valid[:, :], C.wiota[:, :], float(S.N) - 0.5, None, ALU.is_lt))

            def first_of(values, m, out):
                c.link(tt(t0[:, :, :], values[:, :, :], wide(m), ALU.is_equal))
                c.link(ts(t0[:, :, :], t0[:, :, :], -float(X), float(X), ALU.mult, ALU.add))
                c.link(tt(t0[:, :, :], t0[:, :, :], over(C.iota[:, 0:X]), ALU.add))
                c.link(dve.tensor_reduce(ix[:, :], t0[:, :, :], AX.X, ALU.min))
                c.link(tt(out, over(C.iota[:, 0:X]), wide(ix[:, :]), ALU.is_equal))

            c.link(dve.tensor_reduce(mx[:, 0, :], lg[:, :, :], AX.X, ALU.max))
            if choices == 2:
                first_of(lg, mx[:, 0, :], mk[:, 0, :, :])
                c.link(dve.tensor_copy(pv[:, :, :], lg[:, :, :]))
                c.link(ts(t0[:, :, :], mk[:, 0, :, :], 2.0 * NEG_BIG, None, ALU.mult))
                c.link(tt(pv[:, :, :], pv[:, :, :], t0[:, :, :], ALU.add))
                c.link(dve.tensor_reduce(mx[:, 1, :], pv[:, :, :], AX.X, ALU.max))
                first_of(pv, mx[:, 1, :], mk[:, 1, :, :])
                c.link(tt(dd[:, :], mx[:, 1, :], mx[:, 0, :], ALU.subtract))
                dve.nop(nofuse=True).then_inc(ex, 1)
                dve.wait_ge(eo, 1)
                c.link(ts(sl[:, :], kp[:, :], 1.0, None, ALU.add))
                c.link(dve.reciprocal(weight[:, 0, :], sl[:, :]))
                c.link(tt(weight[:, 1, :], weight[:, 0, :], kp[:, :], ALU.mult))
                c.link(tt(both[:, :, :], mk[:, 0, :, :], mk[:, 1, :, :], ALU.add))
            else:
                c.link(tt(pv[:, :, :], lg[:, :, :], wide(mx[:, 0, :]), ALU.subtract))
                dve.nop(nofuse=True).then_inc(ex, 1)
                dve.wait_ge(eo, 1)
                c.link(dve.tensor_reduce(sl[:, :], pos[:, :, :], AX.X, ALU.add))
                c.link(dve.reciprocal(dd[:, :], sl[:, :]))
                c.link(tt(pv[:, :, :], pos[:, :, :], wide(dd[:, :]), ALU.mult))
                c.link(dve.tensor_reduce(mx[:, 0, :], pv[:, :, :], AX.X, ALU.max))
                first_of(pv, mx[:, 0, :], mk[:, 0, :, :])
                c.link(dve.tensor_copy(weight[:, 0, :], mx[:, 0, :]))
                c.link(dve.tensor_copy(both[:, :, :], mk[:, 0, :, :]))
            c.link(tt(both[:, :, :], both[:, :, :], wide(valid[:, :]), ALU.mult))
            dve.nop(nofuse=True).then_inc(mr, 1)
            dve.wait_ge(rk, 1)
            c.link(dve.tensor_copy(tot[:, :, :], pt[:, 0:NT * X].rearrange("p (n x) -> p x n", x=X)))
            c.link(dve.memset(car[:, :, 0:1], 0.0))
            for e in range(X):
                c.link(dve.tensor_tensor_scan(car[:, e, 1:NT + 1], zero[:, 0:NT], tot[:, e, :], 0.0, ALU.add, ALU.add))
            c.link(tt(pos[:, :, :], pk[:, 0:NT * X].rearrange("p (n x) -> p n x", x=X),
                      car[:, :, 0:NT].rearrange("p x n -> p n x"), ALU.add))
            if capacity is None:
                c.link(ts(ng_i[:, :], car[:, :, NT], float(TOK - 1), None, ALU.add))
                c.link(ts(ng_i[:, :], ng_i[:, :], TOK.bit_length() - 1, None, ALU.arith_shift_right))
                c.link(dve.tensor_copy(ng[:, :], ng_i[:, :]))
                c.link(dve.tensor_tensor_scan(gend[:, :], zero[:, 0:X], ng[:, :], 0.0, ALU.add, ALU.add))
                c.link(tt(base[:, :], gend[:, :], ng[:, :], ALU.subtract))
                c.link(ts(base[:, :], base[:, :], float(TOK), None, ALU.mult))
                gg = [P, groups, X]
                c.link(tt(gc[:, :, :], gend[:, :].unsqueeze(1).to_broadcast(gg),
                          C.iota[:, 0:groups].unsqueeze(2).to_broadcast(gg), ALU.is_le))
                c.link(dve.tensor_reduce(gw[:, :], gc[:, :, :], AX.X, ALU.add))
                c.link(ts(gtab[0:1, :], gw[0:1, :], float(X - 1), None, ALU.min))
            else:
                c.link(ts(base[:, :], C.iota[:, 0:X], float(groups * TOK // X), None, ALU.mult))
            for n in range(choices):
                def chosen(v, out):
                    c.link(tt(t0[:, :, :], mk[:, n, :, :], v, ALU.mult))
                    c.link(dve.tensor_reduce(out, t0[:, :, :], AX.X, ALU.add))
                chosen(pos[:, :, :], sl[:, :])
                chosen(over(base[:, :]), dd[:, :])
                if capacity is None:
                    c.link(dve.tensor_copy(kp[:, :], valid[:, :]))
                else:
                    c.link(ts(kp[:, :], sl[:, :], float(capacity) - 0.5, None, ALU.is_lt))
                    c.link(tt(weight[:, n, :], weight[:, n, :], kp[:, :], ALU.mult))
                    c.link(tt(kp[:, :], kp[:, :], valid[:, :], ALU.mult))
                    c.link(ts(sl[:, :], sl[:, :], float(capacity - 1), None, ALU.min))
                c.link(tt(sl[:, :], sl[:, :], dd[:, :], ALU.add))
                c.link(ts(idx_get[:, n, :], sl[:, :], float(groups * TOK - 1), None, ALU.min))
                c.link(ts(dd[:, :], C.wiota[:, :], float(groups * TOK + n * S.ROWS), None, ALU.add))
                c.link(tt(sl[:, :], sl[:, :], dd[:, :], ALU.subtract))
                c.link(tt(sl[:, :], sl[:, :], kp[:, :], ALU.mult))
                c.link(tt(idx_put[:, n, :], sl[:, :], dd[:, :], ALU.add))

        @block.scalar
        def _(act):
            act.wait_ge(ex, 1)
            if choices == 2:
                nc.scalar.activation(kp[:, :], dd[:, :], ACT.Exp).then_inc(eo, 1)
            else:
                nc.scalar.activation(pos[:, :, :], pv[:, :, :], ACT.Exp).then_inc(eo, 1)

        @block.tensor
        def _(pe):
            pe.wait_ge(mr, 1)
            flat = both[:, :, :].rearrange("p n x -> p (n x)")
            pe.matmul(pk[:, 0:NT * X], C.upper[:, :], flat, start=True, stop=True)
            pe.matmul(pt[:, 0:NT * X], C.ones[:, :], flat, start=True, stop=True).then_inc(rk, 1)


def put_rows(k, S, tag, xn_all, idx_put, choices, buf):
    nc = k.nc
    pt = k.sem(f"{tag}_rows_put")
    with ExitStack() as ctx:
        block = ctx.enter_context(nc.Block())

        @block.gpsimd
        def _(pool):
            for i in range(S.NT):
                for n in range(choices):
                    pool.indirect_dma_start(
                        out=buf[:, :], out_offset=bass.IndirectOffsetOnAxis(ap=idx_put[:, n, i:i + 1], axis=0),
                        in_=xn_all[:, i, :], in_offset=None).then_inc(pt, 16)
            pool.wait_ge(pt, 16 * S.NT * choices)


def experts(k, S, C, tag, groups, F, func, xb, yb, w1, b1, w2, b2, expert_of):
    nc = k.nc
    FC = F // P
    Q = TOK // P
    D = S.D
    wl = k.sems(f"{tag}_weights_loaded", 2)
    xl = k.sems(f"{tag}_rows_loaded", 2)
    tp = k.sem(f"{tag}_rows_turned")
    tc = k.sem(f"{tag}_turned_copied")
    hp = k.sem(f"{tag}_hidden_product")
    hc = k.sem(f"{tag}_hidden_ready")
    yp = k.sem(f"{tag}_out_product")
    yc = k.sem(f"{tag}_out_ready")
    ys = k.sems(f"{tag}_out_stored", 2)
    with ExitStack() as ctx:
        w1s = k.sb(ctx, f"{tag}_w1", [P, 2, 2, F])
        w2s = k.sb(ctx, f"{tag}_w2", [P, 2, FC, D])
        b1s = k.sb(ctx, f"{tag}_b1", [P, 2, FC])
        b2s = k.sb(ctx, f"{tag}_b2", [P, 2, D])
        xr = k.sb(ctx, f"{tag}_rows", [P, 2, Q, D])
        xT = k.sb(ctx, f"{tag}_rows_T", [P, 2, 2, TOK])
        hT = k.sb(ctx, f"{tag}_hidden", [P, FC, TOK])
        yo = k.sb(ctx, f"{tag}_out_rows", [P, 2, Q, D])
        px = k.ps(ctx, f"{tag}_turn_ps", [P, 2, TOK])
        ph = k.ps(ctx, f"{tag}_hidden_ps", [P, 2, TOK])
        py = k.ps(ctx, f"{tag}_out_ps", [P, 2, 512])
        block = ctx.enter_context(nc.Block())

        @block.sync
        def _(sp):
            def load(i, b, t, first):
                e = expert_of(sp, t)
                if not first:
                    sp.wait_ge(yc, (t - 1) * Q)
                    sp.nop(nofuse=True)
                at = t * TOK
                sp.dma_start(xr[:, b, :, :], xb[bass.ds(at, TOK), :].rearrange("(q p) d -> p q d", p=P)).then_inc(xl[b], 16)
                sp.dma_start(w1s[:, b, :, :], w1[bass.ds(e, 1), :, :].rearrange("a (c p) f -> p (a c) f", p=P)).then_inc(wl[b], 16)
                sp.dma_start(b1s[:, b, :], b1[bass.ds(e, 1), :].rearrange("a (p c) -> p (a c)", p=P)).then_inc(wl[b], 16)
                sp.dma_start(w2s[:, b, :, :], w2[bass.ds(e, 1), :, :].rearrange("a (p c) d -> p (a c) d", p=P)).then_inc(wl[b], 16)
                sp.dma_start(b2s[:, b, :], b2[bass.ds(e, 1), :].rearrange("a d -> (a d)").partition_broadcast(P)).then_inc(wl[b], 16)

            def store(i, b, t, first):
                sp.wait_ge(yc, t * Q + Q)
                sp.nop(nofuse=True)
                sp.dma_start(yb[bass.ds(t * TOK, TOK), :].rearrange("(q p) d -> p q d", p=P), yo[:, b, :, :]).then_inc(ys[b], 16)
            staged(sp, groups, [load, None, store], 2)
            for b in range(2):
                sp.wait_ge(ys[b], 16 * (groups // 2))

        @block.tensor
        def _(pe):
            def turn(i, b, t, first):
                pe.wait_ge(xl[b], i * 16 + 16)
                if not (first and b == 0):
                    pe.wait_ge(tc, t * 2)
                for c in range(2):
                    for q in range(Q):
                        last = pe.transpose(px[:, c, q * P:(q + 1) * P], xr[:, b, q, c * P:(c + 1) * P], C.ident[:, :])
                    last.then_inc(tp, 1)

            def products(i, b, t, first):
                pe.wait_ge(tc, t * 2 + 2)
                pe.wait_ge(wl[b], i * 64 + 64)
                for f in range(FC):
                    if not (first and b == 0 and f < 2):
                        pe.wait_ge(hc, t * FC + (f - 1))
                    for c in range(2):
                        last = pe.matmul(ph[:, f % 2, :], w1s[:, b, c, f:F:FC], xT[:, b, c, :],
                                         start=c == 0, stop=c == 1)
                    last.then_inc(hp, 1)
                pe.wait_ge(hc, t * FC + FC)
                for q in range(Q):
                    if not (first and b == 0 and q < 2):
                        pe.wait_ge(yc, t * Q + (q - 1))
                    for f in range(FC):
                        last = pe.matmul(py[:, q % 2, 0:D], hT[:, f, q * P:(q + 1) * P], w2s[:, b, f, :],
                                         start=f == 0, stop=f == FC - 1)
                    last.then_inc(yp, 1)
            staged(pe, groups, [turn, products], 2)

        @block.scalar
        def _(act):
            def hidden(i, b, t, first):
                for f in range(FC):
                    act.wait_ge(hp, t * FC + (f + 1))
                    if f == 0 and not (first and b == 0):
                        act.wait_ge(yp, t * Q)
                    nc.scalar.activation(hT[:, f, :], ph[:, f % 2, :], func, bias=b1s[:, b, f:f + 1]).then_inc(hc, 1)
            staged(act, groups, [hidden], 2)

        @block.vector
        def _(dve):
            def turned(i, b, t, first):
                for c in range(2):
                    dve.wait_ge(tp, t * 2 + (c + 1))
                    if not first:
                        dve.wait_ge(hp, (t - 1) * FC)
                    dve.tensor_copy(xT[:, b, c, :], px[:, c, :]).then_inc(tc, 1)

            def outs(i, b, t, first):
                if not first:
                    dve.wait_ge(ys[b], i * 16)
                for q in range(Q):
                    dve.wait_ge(yp, t * Q + (q + 1))
                    dve.tensor_tensor(yo[:, b, q, :], py[:, q % 2, 0:D], b2s[:, b, :], ALU.add).then_inc(yc, 1)
            staged(dve, groups, [turned, outs], 2)


def take_rows(k, S, C, tag, idx_get, choices, weight, buf, x_res, guard):
    nc = k.nc
    NT, D = S.NT, S.D
    gt = k.sem(f"{tag}_rows_taken")
    ch = k.sem(f"{tag}_take_chain")
    with ExitStack() as ctx:
        y = k.sb(ctx, f"{tag}_taken", [P, choices, NT, D])
        if guard:
            t = k.sb(ctx, f"{tag}_guarded", [P, GROUP, D])
            ok = k.sb(ctx, f"{tag}_in_range", [P, 3, GROUP, D], I32)
            lim = k.sb(ctx, f"{tag}_limits", [P, 3, 1])
        block = ctx.enter_context(nc.Block())

        @block.gpsimd
        def _(pool):
            for n in range(choices):
                for i in range(NT):
                    pool.indirect_dma_start(
                        out=y[:, n, i, :], out_offset=None, in_=buf[:, :],
                        in_offset=bass.IndirectOffsetOnAxis(ap=idx_get[:, n, i:i + 1], axis=0)).then_inc(gt, 16)

        @block.vector
        def _(dve):
            c = Chain(dve, ch)
            if guard:
                c.link(dve.memset(lim[:, 0, :], 0.0))
                c.link(dve.memset(lim[:, 1, :], 1e4))
                c.link(dve.memset(lim[:, 2, :], -1e4))
            for n in range(choices):
                dve.wait_ge(gt, 16 * NT * choices)
                c.link(dve.tensor_tensor(y[:, n, :, :], y[:, n, :, :],
                                         weight[:, n, :].unsqueeze(2).to_broadcast([P, NT, D]), ALU.mult))
                if guard:
                    for g in range(NT // GROUP):
                        v = y[:, n, g * GROUP:(g + 1) * GROUP, :]
                        shape = [P, GROUP, D]
                        c.mark(dve.tensor_tensor(ok[:, 0, :, :], v, v, ALU.not_equal))
                        c.mark(dve.tensor_scalar(ok[:, 1, :, :], v, 3.4028234663852886e38, None, ALU.is_gt))
                        c.link(dve.tensor_scalar(ok[:, 2, :, :], v, -3.4028234663852886e38, None, ALU.is_lt))
                        for m in range(3):
                            c.link(dve.copy_predicated(v, ok[:, m, :, :], lim[:, m, :].unsqueeze(1).to_broadcast(shape)))
                c.link(dve.tensor_tensor(x_res[:, :, :], x_res[:, :, :], y[:, n, :, :], ALU.add))


class Namespace:
    pass


def store_rows(k, S, x_res, out):
    nc = k.nc
    st = k.sem("output_stored")
    with ExitStack() as ctx:
        block = ctx.enter_context(nc.Block())

        @block.sync
        def _(sp):
            full, tail = rows_of(out, S)
            sp.dma_start(full, x_res[:, 0:S.NT - 1, :]).then_inc(st, 16)
            sp.dma_start(tail, x_res[0:S.TAIL, S.NT - 1, :]).then_inc(st, 16)
            sp.wait_ge(st, 32)


def gnn_moe_kernel(nc, ins, out):
    S = Shapes(ins["x"], ins["src"], ins["L0_gnn_W"], ins["L0_ffn_W1"], ins["L1_ffn_w1"])
    NT, D, H = S.NT, S.D, S.H
    with ExitStack() as top:
        k = Core(nc, top)
        C, T = Namespace(), Namespace()
        C.ident = k.sb(top, "ident", [P, P])
        C.ones = k.sb(top, "ones", [P, P])
        C.iota = k.sb(top, "iota", [P, P])
        C.upper = k.sb(top, "upper", [P, P])
        C.lower = k.sb(top, "lower", [P, P])
        C.wiota = k.sb(top, "wiota", [P, NT])
        C.eps = k.sb(top, "eps", [P, 1])
        C.waug = k.sb(top, "w_aug", [P, 2, D + 2 * H])
        C.wfb = k.sb(top, "w_fb", [P, 2, D])
        C.wr = k.sb(top, "w_router", [P, 2, S.NX1])
        C.wg = k.sb(top, "w_gate", [P, 2, S.NX2])
        C.br = k.sb(top, "b_router", [P, S.NX1])
        C.bg = k.sb(top, "b_gate", [P, S.NX2])
        C.gat_bias = k.sb(top, "gat_bias", [P, D])
        C.gnn_bias = k.sb(top, "gnn_bias", [P, D])
        C.gamma = k.sb(top, "gamma", [P, D])
        C.beta = k.sb(top, "beta", [P, D])
        C.adst = k.sb(top, "a_dst", [P, NT, H])
        C.in_deg = k.sb(top, "in_deg", [P, NT])
        C.out_deg = k.sb(top, "out_deg", [P, NT])
        C.dinv = k.sb(top, "inv_root_degrees", [P, 2, NT])
        T.h = k.dram("h_rows", [NT * P, D])
        T.zb = k.dram("zb_rows", [NT * P, P])
        T.yf = [k.dram(f"forward_sums_{n}", [(NT + 1) * P, P]) for n in range(2 * SUB)]
        T.xb1 = k.dram("moe1_slots_in", [S.G1 * TOK + 2 * S.ROWS, D])
        T.xb2 = k.dram("moe2_slots_in", [S.G2 * TOK + S.ROWS, D])
        T.yb1 = k.dram("moe1_slots_out", [S.G1 * TOK, D])
        T.yb2 = k.dram("moe2_slots_out", [S.G2 * TOK, D])
        T.src_f = k.dram("edge_src_f", [S.E + STEP])
        T.sd = k.dram("edge_src_dst", [S.E + STEP, 2])
        T.asrc = k.dram("a_src_rows", [NT * P, H])
        T.ea = k.dram("edge_terms", [S.E + STEP, S.EW])
        T.src_i = k.dram("edge_src", [S.E + STEP], I32)
        T.dst_f = k.dram("edge_dst", [S.E + STEP])
        T.steps = k.dram("step_table_dram", [2, P * S.KC], I32)

        setup(k, S, ins, C)
        with ExitStack() as ctx:
            x0 = k.sb(ctx, "x_in", [P, NT, D])
            pr = k.sb(ctx, "gat_products", [P, NT, D + 2 * H])
            project_nodes(k, S, C, "gat", x0, C.waug, D + 2 * H, pr, load_x=ins["x"])
            store_gat_tables(k, S, C, pr, T)
        with ExitStack() as ctx:
            ea = k.sb(ctx, "edge_terms_sb", [S.EP, S.ET, S.EW])
            gather_source_terms(k, S, C, ins, T, ea)
            edge_maxima(k, S, C, ins, T, ea)
        x_res = k.sb(top, "x_res", [P, NT, D])
        with ExitStack() as ctx:
            C.iota_n = k.sb(ctx, "iota_n", [P, NT * P])
            acc = k.sb(ctx, "gat_acc", [P, NT, D + H + 1])
            node_numbers(k, S, C, "gat")
            gat_edges(k, S, C, T, acc)
            gat_finish(k, S, C, acc, x_res, ins["x"])

        def moe(tag, rhs, bias, choices, X, capacity, affine, groups, F, func, xb, yb, w, guard):
            with ExitStack() as ctx:
                put = k.sb(ctx, f"{tag}_put_idx", [P, choices, NT], I32)
                get = k.sb(ctx, f"{tag}_get_idx", [P, choices, NT], I32)
                weight = k.sb(ctx, f"{tag}_weight", [P, choices, NT])
                gtab = k.sb(ctx, f"{tag}_group_expert", [1, groups], I32)
                with ExitStack() as inner:
                    xn = k.sb(inner, f"{tag}_xn_all", [P, NT, D])
                    logits = k.sb(inner, f"{tag}_raw_logits", [P, NT, X])
                    project_nodes(k, S, C, tag, x_res, rhs, X, logits, xn_all=xn, affine=affine)
                    route(k, S, C, tag, logits, bias, choices, X, capacity, put, get, weight, gtab)
                    put_rows(k, S, tag, xn, put, choices, xb)
                per = groups // X
                if capacity is None:
                    def expert_of(eng, t):
                        return eng.value_load(gtab[0:1, bass.ds(t, 1)], min_val=0, max_val=X - 1)
                else:
                    def expert_of(eng, t):
                        assert per == 2
                        return t // 2
                experts(k, S, C, tag, groups, F, func, xb, yb, *w, expert_of)
                take_rows(k, S, C, tag, get, choices, weight, yb, x_res, guard)

        moe("moe1", C.wr, C.br, 2, S.NX1, None, (C.gamma, C.beta), S.G1, S.F1, ACT.Gelu, T.xb1, T.yb1,
            (ins["L0_ffn_W1"], ins["L0_ffn_b1"], ins["L0_ffn_W2"], ins["L0_ffn_b2"]), False)
        with ExitStack() as ctx:
            z = k.sb(ctx, "gnn_z", [P, NT, D])
            project_nodes(k, S, C, "gnn", x_res, C.wfb, D, z)
            gnn_scale(k, S, C, T, z)
            acc = k.sb(ctx, "gnn_acc", [P, NT, P])
            with ExitStack() as inner:
                C.iota_n = k.sb(inner, "iota_n2", [P, NT * P])
                node_numbers(k, S, C, "gnn")
                gnn_edges(k, S, C, T, z, acc)
            gnn_finish(k, S, C, T, z, acc, x_res)
        k.recycle()
        moe("moe2", C.wg, C.bg, 1, S.NX2, S.CAP, None, S.G2, S.F2, ACT.Relu, T.xb2, T.yb2,
            (ins["L1_ffn_w1"], ins["L1_ffn_b1"], ins["L1_ffn_w2"], ins["L1_ffn_b2"]), True)
        store_rows(k, S, x_res, out)


def node_numbers(k, S, C, tag):
    io = k.sem(f"{tag}_node_numbers_ready")
    with ExitStack() as ctx:
        block = ctx.enter_context(k.nc.Block())

        @block.gpsimd
        def _(pool):
            pool.iota(C.iota_n[:, :], pattern=[[1, S.NT * P]], base=0, channel_multiplier=0,
                      allow_small_or_imprecise_dtypes=True).then_inc(io, 1)


_INS = ["x", "src", "dst", "L0_gnn_W", "L0_gnn_att_src", "L0_gnn_att_dst", "L0_gnn_bias", "L0_ffn_gamma",
        "L0_ffn_beta", "L0_ffn_Wr", "L0_ffn_br", "L0_ffn_W1", "L0_ffn_b1", "L0_ffn_W2", "L0_ffn_b2", "L1_gnn_W_f",
        "L1_gnn_W_b", "L1_gnn_bias_param", "L1_ffn_gate_w", "L1_ffn_gate_b", "L1_ffn_w1", "L1_ffn_b1", "L1_ffn_w2",
        "L1_ffn_b2"]


def kernel(**inputs):
    import numpy as np
    import concourse.bacc as bacc
    from concourse.bass_utils import run_bass_kernel_spmd

    nc = bacc.Bacc("TRN2", target_bir_lowering=False, num_devices=1)
    arrays, ins = {}, {}
    for name in _INS:
        a = np.ascontiguousarray(inputs[name])
        arrays["in_" + name] = a
        ins[name] = nc.dram_tensor("in_" + name, a.shape, mybir.dt.from_np(a.dtype), kind="ExternalInput").ap()
    shape = inputs["x"].shape
    out = nc.dram_tensor("out", shape, F32, kind="ExternalOutput").ap()
    gnn_moe_kernel(nc, ins, out)
    r = run_bass_kernel_spmd(nc, [arrays], core_ids=[0])
    return r.results[0]["out"]
```

```python
from contextlib import ExitStack

import concourse.bass as bass
from concourse import mybir

F32 = mybir.dt.float32
BF16 = mybir.dt.bfloat16
I32 = mybir.dt.int32
ALU = mybir.AluOpType
ACT = mybir.ActivationFunctionType
AX = mybir.AxisListType

P = 128
EPS = 1e-5
NEG_BIG = -1.0e38
FAR = -2.0 ** 100
CH = 16
ZCOLS = 1024
SUB = 2
STEP = SUB * P
POOL_SHARE = 51
GAT_DEPTH = 8
GNN_DEPTH = 4
BIG_DEPTH = max(GAT_DEPTH, GNN_DEPTH)
TOK = 512
GROUP = 7


class Shapes:

    def __init__(self, x, src, gat_W, w1, w2):
        self.N, self.D = x.shape
        self.E = src.shape[0]
        self.H = gat_W.shape[1]
        self.HD = gat_W.shape[2]
        self.NT = -(-self.N // P)
        self.TAIL = self.N - (self.NT - 1) * P
        self.EP = next(p for p in range(P, 0, -1) if self.E % p == 0)
        self.ET = self.E // self.EP
        self.STEPS = -(-(-(-self.E // STEP) + self.NT) // BIG_DEPTH) * BIG_DEPTH
        self.NX1, self.F1 = w1.shape[0], w1.shape[2]
        self.NX2, self.F2 = w2.shape[0], w2.shape[2]
        self.CAP = -(-5 * self.N // (4 * self.NX2))
        self.CT = -(-self.CAP // P)
        self.KC = -(-self.STEPS // P)
        self.EW = 2 * self.H + 2
        self.G1 = (2 * self.N + self.NX1 * (TOK - 1)) // TOK
        self.G2 = self.NX2 * -(-self.CAP // TOK)
        self.ROWS = self.NT * P
        self.G1 += self.G1 % 2
        self.G2 += self.G2 % 2
        assert self.D == 2 * P and self.NT % GROUP == 0


class Core:

    def __init__(self, nc, ctx):
        self.nc, self.ctx = nc, ctx
        self.used = []

    def sem(self, name):
        self.used.append(self.nc.alloc_semaphore(name))
        return self.used[-1]

    def recycle(self):
        self.nc.clear_and_free_semaphores(self.used)
        self.nc.all_engine_barrier()
        self.used = []

    def sems(self, name, n):
        return [self.sem(f"{name}_{j}") for j in range(n)]

    def sb(self, ctx, name, shape, dt=F32):
        return ctx.enter_context(self.nc.sbuf_tensor(name, shape, dt))

    def ps(self, ctx, name, shape, dt=F32):
        return ctx.enter_context(self.nc.psum_tensor(name, shape, dt))

    def dram(self, name, shape, dt=F32):
        return self.nc.dram_tensor(name, shape, dt, kind="Internal").ap()


class Chain:

    def __init__(self, eng, sem, start=0):
        self.eng, self.sem, self.n = eng, sem, start

    def mark(self, ins):
        ins.then_inc(self.sem, 1)
        self.n = self.n + 1

    def link(self, ins):
        self.mark(ins)
        self.eng.wait_ge(self.sem, self.n)

    def join(self):
        self.eng.wait_ge(self.sem, self.n)


def staged(eng, steps, stages, depth):
    def tick(i, j):
        for s, stage in stages:
            back, slot = (0, j - s) if j >= s else (1, j - s + depth)
            if not isinstance(i, int):
                stage(i - back, slot, i * depth + (j - s), False)
            elif 0 <= i * depth + j - s < steps:
                stage(i - back, slot, i * depth + j - s, i == back)

    rounds = steps // depth
    for i in range(2):
        for j in range(depth):
            tick(i, j)
    with eng.Fori(2, rounds) as i:
        for j in range(depth):
            tick(i, j)
    for j in range(max(lag for lag, _ in stages)):
        tick(rounds, j)


def rows_of(dram, S):
    full = dram[0:(S.NT - 1) * P, :].rearrange("(i p) d -> p i d", p=P)
    tail = dram[(S.NT - 1) * P:S.N, :]
    return full, tail



def setup(k, S, ins, C):
    nc = k.nc
    ld = k.sem("weights_loaded")
    io = k.sem("iota_written")
    ch = k.sem("setup_chain")
    tr = k.sem("wfb_transposed")
    with ExitStack() as ctx:
        att = k.sb(ctx, "att_rows", [P, 2, S.D])
        tmp = k.sb(ctx, "w_times_att", [P, S.D])
        wraw = k.sb(ctx, "wfb_raw", [P, 2, S.D])
        ii = k.sb(ctx, "iota_int", [P, P], I32)
        tri_i = k.sb(ctx, "diff_int", [P, P], I32)
        wi = k.sb(ctx, "window_int", [P, S.NT], I32)
        pt = k.ps(ctx, "wfb_ps", [P, 4, P])
        block = ctx.enter_context(nc.Block())

        def row(v):
            return v.rearrange("(a d) -> a d", a=1).partition_broadcast(P) if len(v.shape) == 1 else v

        loads = [
            (C.waug[:, :, 0:S.D], ins["L0_gnn_W"].rearrange("(c p) h d -> p c (h d)", p=P)),
            (att[:, 0, :], ins["L0_gnn_att_src"].rearrange("h d -> (h d)").partition_broadcast(P)),
            (att[:, 1, :], ins["L0_gnn_att_dst"].rearrange("h d -> (h d)").partition_broadcast(P)),
            (C.gat_bias[:, :], ins["L0_gnn_bias"].partition_broadcast(P)),
            (C.gamma[:, :], ins["L0_ffn_gamma"].partition_broadcast(P)),
            (C.beta[:, :], ins["L0_ffn_beta"].partition_broadcast(P)),
            (C.wr[:, :, :], ins["L0_ffn_Wr"].rearrange("(c p) n -> p c n", p=P)),
            (C.br[:, :], ins["L0_ffn_br"].partition_broadcast(P)),
            (wraw[:, 0, :], ins["L1_gnn_W_f"]),
            (wraw[:, 1, :], ins["L1_gnn_W_b"]),
            (C.gnn_bias[:, :], ins["L1_gnn_bias_param"].partition_broadcast(P)),
            (C.wg[:, :, :], ins["L1_ffn_gate_w"].rearrange("(c p) n -> p c n", p=P)),
            (C.bg[:, :], ins["L1_ffn_gate_b"].partition_broadcast(P)),
        ]

        @block.sync
        def _(sp):
            for out, src in loads:
                sp.dma_start(out, src).then_inc(ld, 16)

        @block.gpsimd
        def _(pool):
            pool.iota(ii[:, :], pattern=[[1, P]], base=0, channel_multiplier=0).then_inc(io, 1)
            pool.iota(tri_i[:, :], pattern=[[1, P]], base=0, channel_multiplier=-1).then_inc(io, 1)
            pool.iota(wi[:, :], pattern=[[P, S.NT]], base=0, channel_multiplier=1).then_inc(io, 1)

        @block.vector
        def _(dve):
            c = Chain(dve, ch)
            dve.wait_ge(io, 3)
            c.mark(dve.tensor_copy(C.iota[:, :], ii[:, :]))
            c.mark(dve.tensor_scalar(C.ident[:, :], tri_i[:, :], 0.0, None, ALU.is_equal))
            c.mark(dve.tensor_scalar(C.upper[:, :], tri_i[:, :], 0.0, None, ALU.is_gt))
            c.mark(dve.tensor_scalar(C.lower[:, :], tri_i[:, :], 0.0, None, ALU.is_lt))
            c.mark(dve.tensor_copy(C.wiota[:, :], wi[:, :]))
            c.mark(dve.memset(C.ones[:, :], 1.0))
            c.mark(dve.memset(C.eps[:, :], EPS))
            c.mark(dve.memset(C.one[:, :], 1.0))
            dve.wait_ge(ld, 16 * len(loads))
            for a in range(2):
                for t in range(2):
                    c.link(dve.tensor_tensor(tmp[:, :], C.waug[:, t, 0:S.D], att[:, a, :], ALU.mult))
                    c.link(dve.tensor_reduce(C.waug[:, t, S.D + a * S.H:S.D + (a + 1) * S.H],
                                             tmp[:, :].rearrange("p (h d) -> p h d", h=S.H), AX.X, ALU.add))
            dve.wait_ge(tr, 1)
            c.link(dve.tensor_copy(C.wfb[:, :, :], pt[:, :, :].rearrange("p (c a) n -> p c (a n)", c=2)))

        @block.tensor
        def _(pe):
            pe.wait_ge(ch, 7)
            pe.wait_ge(ld, 16 * len(loads))
            for t in range(2):
                for a in range(2):
                    last = pe.transpose(pt[:, 2 * t + a, :], wraw[:, a, t * P:(t + 1) * P], C.ident[:, :])
            last.then_inc(tr, 1)



def project_nodes(k, S, C, tag, x_res, rhs, n_out, out_sb, xn_all=None, xnT_all=None, load_x=None, affine=None):
    nc = k.nc
    passes = 2 if affine else 1
    per_row = 3 if affine else 1
    head = 2 * GROUP + 1
    before_last = (passes - 1) * (head + GROUP)
    ops = before_last + head + GROUP * per_row
    ln = k.sem(f"{tag}_ln_steps")
    rt = k.sem(f"{tag}_root_ready")
    xl = k.sem(f"{tag}_x_loaded")
    tp = k.sem(f"{tag}_rows_transposed")
    tc = k.sem(f"{tag}_transpose_copied")
    pj = k.sem(f"{tag}_product_ready")
    ev = k.sem(f"{tag}_product_copied")
    gf = k.sem(f"{tag}_row_slots_free")
    with ExitStack() as ctx:
        st = k.sb(ctx, f"{tag}_stats", [P, GROUP, 6])
        mv = k.sb(ctx, f"{tag}_meanvar", [P, 2, GROUP, 2])
        sd = k.sb(ctx, f"{tag}_std", [P, 2, GROUP])
        rs = k.sb(ctx, f"{tag}_rstd", [P, 2, GROUP])
        xn = k.sb(ctx, f"{tag}_xn", [P, GROUP, S.D])
        xm = k.sb(ctx, f"{tag}_xm", [P, GROUP, S.D]) if affine else None
        xT = k.sb(ctx, f"{tag}_xT", [P, GROUP, 2, P])
        pt = k.ps(ctx, f"{tag}_pt", [P, 2, 512])
        po = k.ps(ctx, f"{tag}_po", [P, 2, 512])
        block = ctx.enter_context(nc.Block())

        def tile_of(t, g, j):
            return t[:, bass.ds(g * GROUP + j, 1), :].rearrange("p a d -> p (a d)")

        @block.sync
        def _(sp):
            if load_x is None:
                return
            sp.wait_ge(xl, 1)
            full, tail = rows_of(load_x, S)
            for g in range(S.NT // GROUP):
                hi = min((g + 1) * GROUP, S.NT - 1)
                sp.dma_start(x_res[:, g * GROUP:hi, :], full[:, g * GROUP:hi, :]).then_inc(xl, 16)
            sp.dma_start(x_res[0:S.TAIL, S.NT - 1, :], tail).then_inc(xl, 16)

        @block.gpsimd
        def _(pool):
            if load_x is not None:
                pool.memset(x_res[:, S.NT - 1, :], 0.0).then_inc(xl, 1)

        @block.vector
        def _(dve):
            if load_x is not None:
                dve.wait_ge(xl, 1 + 16 * (S.NT // GROUP + 1))
            with dve.Fori(0, S.NT // GROUP) as g:
                for r in range(passes):
                    last = r == passes - 1
                    at = g * ops + r * (head + GROUP)
                    src = [xm[:, j, :] if r else tile_of(x_res, g, j) for j in range(GROUP)]
                    for j in range(GROUP):
                        if r:
                            dve.wait_ge(ln, at - GROUP + j + 1)
                        dve.bn_stats(st[:, j, :], src[j]).then_inc(ln, 1)
                    for j in range(GROUP):
                        dve.wait_ge(ln, at + (j + 1))
                        dve.nop(nofuse=True)
                        dve.bn_aggr(mv[:, r, j, :], st[:, j, :]).then_inc(ln, 1)
                    dve.wait_ge(rt, g * passes + (r + 1))
                    dve.reciprocal(rs[:, r, :], sd[:, r, :]).then_inc(ln, 1)
                    dve.wait_ge(ln, at + head)
                    if last:
                        dve.wait_ge(gf, g + 1)
                    for j in range(GROUP):
                        dst = xn[:, j, :] if last else xm[:, j, :]
                        dve.tensor_scalar(dst, src[j], mv[:, r, j, 0:1], rs[:, r, j:j + 1],
                                          ALU.subtract, ALU.mult).then_inc(ln, 1)
                        if last and affine:
                            dve.wait_ge(ln, at + (head + 3 * j + 1))
                            dve.tensor_tensor(dst, dst, affine[0][:, :], ALU.mult).then_inc(ln, 1)
                            dve.wait_ge(ln, at + (head + 3 * j + 2))
                            dve.tensor_tensor(dst, dst, affine[1][:, :], ALU.add).then_inc(ln, 1)

        @block.scalar
        def _(act):
            with act.Fori(0, S.NT // GROUP) as g:
                for r in range(passes):
                    act.wait_ge(ln, g * ops + (r * (head + GROUP) + 2 * GROUP))
                    nc.scalar.activation(sd[:, r, :], mv[:, r, :, 1], ACT.Sqrt, bias=C.eps[:, 0:1]).then_inc(rt, 1)

                def copy_transposed(j):
                    act.wait_ge(tp, g * GROUP + (j + 1))
                    last = nc.scalar.copy(xT[:, j, :, :], pt[:, j % 2, 0:2 * P].rearrange("p (c n) -> p c n", c=2))
                    if xnT_all is not None:
                        for c in range(2):
                            last = nc.scalar.copy(xnT_all[:, c, bass.ds((g * GROUP + j) * P, P)],
                                                  pt[:, j % 2, c * P:(c + 1) * P])
                    last.then_inc(tc, 1)

                copy_transposed(0)
                for j in range(GROUP):
                    if j + 1 < GROUP:
                        copy_transposed(j + 1)
                    if xn_all is not None:
                        nc.scalar.copy(tile_of(xn_all, g, j), xn[:, j, :])
                    act.wait_ge(pj, g * GROUP + (j + 1))
                    nc.scalar.copy(tile_of(out_sb, g, j), po[:, j % 2, 0:n_out]).then_inc(ev, 1)

        @block.tensor
        def _(pe):
            pe.nop(nofuse=True).then_inc(gf, 1)
            with pe.Fori(0, S.NT // GROUP) as g:
                def transpose(j):
                    pe.wait_ge(ln, g * ops + (before_last + head + (j + 1) * per_row))
                    if j >= 2:
                        pe.wait_ge(tc, g * GROUP + (j - 1))
                    for c in range(2):
                        last = pe.transpose(pt[:, j % 2, c * P:(c + 1) * P], xn[:, j, c * P:(c + 1) * P],
                                            C.ident[:, :])
                    last.then_inc(tp, 1)

                transpose(0)
                for j in range(GROUP):
                    if j + 1 < GROUP:
                        transpose(j + 1)
                    pe.wait_ge(tc, g * GROUP + (j + 1))
                    if j >= 2:
                        pe.wait_ge(ev, g * GROUP + (j - 1))
                    for c in range(2):
                        last = pe.matmul(po[:, j % 2, 0:n_out], xT[:, j, c, :], rhs[:, c, :],
                                         start=c == 0, stop=c == 1)
                    last.then_inc(pj, 1)
                pe.wait_ge(ev, g * GROUP + GROUP)
                pe.nop(nofuse=True).then_inc(gf, 1)



def store_gat_tables(k, S, C, pr, T):
    nc = k.nc
    st = k.sem("gat_tables_stored")
    ca = k.sem("dst_terms_kept")
    with ExitStack() as ctx:
        rest = k.sb(ctx, "terms_rest", [P, S.NT, S.H])
        far = k.sb(ctx, "far", [S.NT, S.NT])
        block = ctx.enter_context(nc.Block())

        @block.sync
        def _(sp):
            for i in range(S.NT // GROUP):
                a, b = i * GROUP, (i + 1) * GROUP
                sp.dma_start(T.h[a * P:b * P, :].rearrange("(i p) d -> p i d", p=P), pr[:, a:b, 0:S.D]).then_inc(st, 16)
            sp.dma_start(T.asrc.rearrange("(i p) h -> p i h", p=P), pr[:, :, S.D:S.D + S.H]).then_inc(st, 16)
            sp.wait_ge(st, 16 * (S.NT // GROUP + 1))

        @block.vector
        def _(dve):
            c = Chain(dve, ca)
            c.mark(dve.tensor_copy(C.adst[:, :, :], pr[:, :, S.D + S.H:S.D + 2 * S.H]))
            part = C.asplit[:, :, :].rearrange("p s (n h) -> p s n h", h=S.H)
            c.link(dve.tensor_copy(part[:, 0, :, :], pr[:, :, S.D:S.D + S.H]))
            c.link(dve.tensor_tensor(rest[:, :, :], pr[:, :, S.D:S.D + S.H], part[:, 0, :, :], ALU.subtract))
            c.link(dve.tensor_copy(part[:, 1, :, :], rest[:, :, :]))
            c.link(dve.tensor_tensor(rest[:, :, :], rest[:, :, :], part[:, 1, :, :], ALU.subtract))
            c.link(dve.tensor_copy(part[:, 2, :, :], rest[:, :, :]))
            c.link(dve.tensor_scalar(far[:, :], C.iota[0:S.NT, 0:S.NT], C.wiota[0:S.NT, 0:1], FAR,
                                     ALU.is_equal, ALU.mult))
            c.link(dve.tensor_copy(C.farpat[:, :].rearrange("p (n h) -> p n h", h=S.H),
                                   far[:, :].unsqueeze(2).to_broadcast([S.NT, S.NT, S.H])))


def edge_lists(k, S, ins, T):
    nc = k.nc
    EP, ET = S.EP, S.ET
    ld = k.sem("edge_lists_loaded")
    ch = k.sem("edge_lists_chain")
    tl = k.sem("edge_tails_ready")
    st = k.sem("edge_lists_stored")
    with ExitStack() as ctx:
        si = k.sb(ctx, "src_int", [EP, ET], I32)
        di = k.sb(ctx, "dst_int", [EP, ET], I32)
        hi_i = k.sb(ctx, "src_hi_int", [EP, ET], I32)
        sf = k.sb(ctx, "src_float", [EP, ET])
        df = k.sb(ctx, "dst_float", [EP, ET])
        hi = k.sb(ctx, "src_hi", [EP, ET], BF16)
        lo = k.sb(ctx, "src_lo", [EP, ET], BF16)
        sd = k.sb(ctx, "src_dst_rows", [EP, ET, 3])
        tz = k.sb(ctx, "tail_src", [P, SUB])
        tm = k.sb(ctx, "tail_dst", [P, SUB])
        tsd = k.sb(ctx, "tail_src_dst", [P, SUB, 3])
        block = ctx.enter_context(nc.Block())
        lists = [(T.src_f, sf), (T.dst_f, df), (T.src_hi, hi), (T.src_lo, lo)]

        @block.sync
        def _(sp):
            sp.dma_start(si[:, :], ins["src"].rearrange("(p t) -> p t", t=ET)).then_inc(ld, 16)
            sp.dma_start(di[:, :], ins["dst"].rearrange("(p t) -> p t", t=ET)).then_inc(ld, 16)
            sp.wait_ge(tl, 4)
            sp.dma_start(T.src_f[S.E:S.E + STEP].rearrange("(p j) -> p j", j=SUB), tz[:, :]).then_inc(st, 16)
            sp.dma_start(T.dst_f[S.E:S.E + STEP].rearrange("(p j) -> p j", j=SUB), tm[:, :]).then_inc(st, 16)
            sp.dma_start(T.sd[S.E:S.E + STEP, :].rearrange("(p j) c -> p j c", j=SUB), tsd[:, :, :]).then_inc(st, 16)
            sp.wait_ge(ch, 8)
            for dram, own in lists:
                sp.dma_start(dram[0:S.E].rearrange("(p t) -> p t", t=ET), own[:, :]).then_inc(st, 16)
            sp.dma_start(T.sd[0:S.E, :].rearrange("(p t) c -> p (t c)", t=ET),
                         sd[:, :, :].rearrange("p t c -> p (t c)")).then_inc(st, 16)
            sp.wait_ge(st, 16 * 8)

        @block.gpsimd
        def _(pool):
            pool.memset(tz[:, :], 0.0).then_inc(tl, 1)
            pool.memset(tm[:, :], -1.0).then_inc(tl, 1)
            pool.memset(tsd[:, :, :], 0.0).then_inc(tl, 1)
            pool.wait_ge(tl, 3)
            pool.memset(tsd[:, :, 1], -1.0).then_inc(tl, 1)

        @block.vector
        def _(dve):
            c = Chain(dve, ch)
            dve.wait_ge(ld, 32)
            c.link(dve.tensor_scalar(hi_i[:, :], si[:, :], P.bit_length() - 1, None, ALU.arith_shift_right))
            c.mark(dve.tensor_copy(hi[:, :], hi_i[:, :]))
            c.mark(dve.scalar_tensor_tensor(out=lo[:, :], in0=hi_i[:, :], scalar=-float(P), in1=si[:, :],
                                            op0=ALU.mult, op1=ALU.add))
            c.mark(dve.tensor_copy(sf[:, :], si[:, :]))
            c.mark(dve.tensor_copy(df[:, :], di[:, :]))
            c.mark(dve.tensor_copy(sd[:, :, 0], si[:, :]))
            c.mark(dve.tensor_copy(sd[:, :, 1], di[:, :]))
            c.mark(dve.tensor_copy(sd[:, :, 2].bitcast(I32), si[:, :]))


def source_terms(k, S, C, ins, T):
    nc = k.nc
    NT, H, EP, ET = S.NT, S.H, S.EP, S.ET
    CE = P * CH
    full = S.E // CE
    rest = S.E - full * CE
    NPOOL = full * POOL_SHARE // 100 // 2 * 2
    NPE = (full - NPOOL) // 2 * 2
    extra = list(range(NPE + NPOOL, full)) + ([full] if rest else [])
    assert rest % CH == 0 and ET % (2 * CH) == 0
    counts = ET // CH
    BANKS = 4
    il = k.sems("src_chunk_loaded", 2)
    ga = k.sems("terms_gathered", 2)
    gs = k.sems("gathered_terms_stored", 2)
    rl = k.sems("src_rows_loaded", 2)
    oh = k.sem("pick_onehots_ready")
    pk = k.sem("candidates_ready")
    rd = k.sem("candidates_reduced")
    ps = k.sems("picked_terms_stored", 2)
    cl = k.sem("count_lists_loaded")
    co = k.sem("count_onehots_ready")
    cu = k.sem("count_onehots_used")
    ch = k.sem("count_chain")
    with ExitStack() as ctx:
        idx = k.sb(ctx, "src_chunk", [P, 2, CH], I32)
        rows = k.sb(ctx, "gathered_terms", [P, 2, CH * H])
        lo_r = k.sb(ctx, "src_lo_row", [P, 2, CE], BF16)
        hi_r = k.sb(ctx, "src_hi_row", [NT, 2, CE], BF16)
        olo = k.sb(ctx, "pick_lo", [P, 2, CE], BF16)
        nhi = k.sb(ctx, "pick_not_hi", [NT, 2, CE], BF16)
        res = k.sb(ctx, "picked_terms", [P, 2, CH, H])
        iob = k.sb(ctx, "iota_bf", [P, P], BF16)
        hi = k.sb(ctx, "count_hi", [EP, ET], BF16)
        lo = k.sb(ctx, "count_lo", [EP, ET], BF16)
        ohl = k.sb(ctx, "count_onehot_lo", [EP, 2, CH, P], BF16)
        ohh = k.sb(ctx, "count_onehot_hi", [EP, 2, CH, NT], BF16)
        zz = k.sb(ctx, "zeros_bf", [EP, P], BF16)
        pc = k.ps(ctx, "candidates_ps", [P, BANKS, 512])
        pd = k.ps(ctx, "source_counts", [P, NT])
        block = ctx.enter_context(nc.Block())
        src = ins["src"]

        def edges(c, n=1):
            return bass.ds(c * CE, CE) if n == 1 else None

        def put(c):
            return T.terms[bass.ds(c * CE, CE), :].rearrange("(p t) h -> p (t h)", t=CH)

        @block.sync
        def _(sp):
            sp.dma_start(hi[:, :], T.src_hi[0:S.E].rearrange("(p t) -> p t", t=ET)).then_inc(cl, 16)
            sp.dma_start(lo[:, :], T.src_lo[0:S.E].rearrange("(p t) -> p t", t=ET)).then_inc(cl, 16)

            def load(i, b, t, first):
                if not first:
                    sp.wait_ge(oh, t - 1)
                    sp.nop(nofuse=True)
                sp.dma_start(lo_r[:, b, :], T.src_lo[edges(t)].partition_broadcast(P)).then_inc(rl[b], 16)
                sp.dma_start(hi_r[:, b, :], T.src_hi[edges(t)].partition_broadcast(NT)).then_inc(rl[b], 16)

            def store(i, b, t, first):
                sp.wait_ge(rd, t * CH + CH)
                sp.nop(nofuse=True)
                sp.dma_start(put(t), res[:, b, :, :].rearrange("p t h -> p (t h)")).then_inc(ps[b], 16)
            staged(sp, NPE, [(0, load), (2, store)], 2)
            for b in range(2):
                sp.wait_ge(ps[b], 16 * (NPE // 2))

        @block.scalar
        def _(act):
            def load(i, b, t, first):
                if not first:
                    act.wait_ge(ga[b], i * (16 * CH))
                    act.nop(nofuse=True)
                act.dma_start(idx[:, b, :], src[bass.ds((t + NPE) * CE, CE)].rearrange("(p t) -> p t", t=CH))\
                   .then_inc(il[b], 16)

            def store(i, b, t, first):
                act.wait_ge(ga[b], i * (16 * CH) + 16 * CH)
                act.nop(nofuse=True)
                act.dma_start(put(t + NPE), rows[:, b, :]).then_inc(gs[b], 16)
            staged(act, NPOOL, [(0, load), (1, store)], 2)
            n = NPOOL // 2
            for x, c in enumerate(extra):
                b, r = x % 2, n + x // 2
                parts = P if c < full else rest // CH
                act.wait_ge(ga[b], 16 * CH * r)
                act.dma_start(idx[0:parts, b, :],
                              src[c * CE:c * CE + parts * CH].rearrange("(p t) -> p t", t=CH)).then_inc(il[b], 16)
                act.wait_ge(ga[b], 16 * CH * (r + 1))
                act.dma_start(T.terms[c * CE:c * CE + parts * CH, :].rearrange("(p t) h -> p (t h)", t=CH),
                              rows[0:parts, b, :]).then_inc(gs[b], 16)
            for b in range(2):
                act.wait_ge(gs[b], 16 * (n + len(range(b, len(extra), 2))))

        @block.gpsimd
        def _(pool):
            def fetch(b, parts):
                for t in range(CH):
                    pool.indirect_dma_start(
                        out=rows[0:parts, b, t * H:(t + 1) * H], out_offset=None, in_=T.asrc[:, :],
                        in_offset=bass.IndirectOffsetOnAxis(ap=idx[0:parts, b, t:t + 1], axis=0)).then_inc(ga[b], 16)

            def gather(i, b, t, first):
                pool.wait_ge(il[b], i * 16 + 16)
                pool.nop(nofuse=True)
                if not first:
                    pool.wait_ge(gs[b], i * 16)
                    pool.nop(nofuse=True)
                fetch(b, P)
            staged(pool, NPOOL, [(0, gather)], 2)
            for x, c in enumerate(extra):
                b, r = x % 2, NPOOL // 2 + x // 2
                pool.wait_ge(il[b], 16 * (r + 1))
                pool.wait_ge(gs[b], 16 * r)
                fetch(b, P if c < full else rest // CH)

        @block.vector
        def _(dve):
            c = Chain(dve, ch)
            c.mark(dve.memset(zz[:, :], 0.0))
            c.link(dve.tensor_copy(iob[:, :], C.iota[:, :]))

            def onehots(i, b, t, first):
                dve.wait_ge(rl[b], i * 32 + 32)
                if not first:
                    dve.wait_ge(pk, (t - 1) * CH)
                dve.tensor_scalar(olo[:, b, :], lo_r[:, b, :], C.wiota[:, 0:1], None, ALU.is_equal)
                dve.tensor_scalar(nhi[:, b, :], hi_r[:, b, :], C.wiota[0:NT, 0:1], None, ALU.not_equal).then_inc(oh, 1)

            def reduce(i, b, t, first):
                if not first:
                    dve.wait_ge(ps[b], i * 16)
                for j in range(CH):
                    dve.wait_ge(pk, t * CH + (j + 1))
                    dve.tensor_reduce(res[:, b, j, :], pc[:, j % BANKS, 0:NT * H].rearrange("p (n h) -> p h n", h=H),
                                      AX.X, ALU.max).then_inc(rd, 1)
            staged(dve, NPE, [(0, onehots), (1, reduce)], 2)

            def count(i, b, t, first):
                if not first:
                    dve.wait_ge(cu, t - 1)
                at = bass.ds(t * CH, CH)
                dve.tensor_tensor(ohl[:, b, :, :], lo[:, at].unsqueeze(2).to_broadcast([EP, CH, P]),
                                  iob[0:EP, :].unsqueeze(1).to_broadcast([EP, CH, P]), ALU.is_equal)
                dve.tensor_tensor(ohh[:, b, :, :], hi[:, at].unsqueeze(2).to_broadcast([EP, CH, NT]),
                                  iob[0:EP, 0:NT].unsqueeze(1).to_broadcast([EP, CH, NT]), ALU.is_equal).then_inc(co, 1)
            dve.wait_ge(cl, 32)
            staged(dve, counts, [(0, count)], 2)
            dve.wait_ge(cu, counts + 1)
            dve.tensor_scalar(C.in_deg[:, :], pd[:, :], 1.0, None, ALU.add).then_inc(ch, 1)

        @block.tensor
        def _(pe):
            def pick(i, b, t, first):
                pe.wait_ge(oh, t + 1)
                for j in range(CH):
                    if not (first and b == 0 and j < BANKS):
                        pe.wait_ge(rd, t * CH + (j + 1 - BANKS))
                    out = pc[:, j % BANKS, 0:NT * H]
                    for s in range(3):
                        pe.matmul(out, olo[:, b, j:CE:CH], C.asplit[:, s, :], start=s == 0, stop=False)
                    pe.matmul(out, nhi[:, b, j:CE:CH], C.farpat[:, :], start=False, stop=True).then_inc(pk, 1)
            staged(pe, NPE, [(0, pick)], 2)

            pe.wait_ge(ch, 1)
            pe.matmul(pd[:, :], zz[:, :], zz[:, 0:NT], start=True, stop=False, skip_group_check=True)

            def count(i, b, t, first):
                pe.wait_ge(co, t + 1)
                for j in range(CH):
                    last = pe.matmul(pd[:, :], ohl[:, b, j, :], ohh[:, b, j, :], start=False, stop=False,
                                     skip_group_check=True)
                last.then_inc(cu, 1)
            staged(pe, counts, [(0, count)], 2)
            pe.matmul(pd[:, :], zz[:, :], zz[:, 0:NT], start=False, stop=True, skip_group_check=True).then_inc(cu, 1)


def edge_maxima(k, S, C, ins, T, ea):
    nc = k.nc
    EP, ET, H, NT = S.EP, S.ET, S.H, S.NT
    KC = S.KC
    ld = k.sem("dst_loaded")
    ch = k.sem("maxima_chain")
    tr = k.sem("totals_ready")
    tq = k.sem("totals_transposed")
    cr = k.sem("carry_ready")
    cb = k.sem("carry_back")
    cn = k.sem("window_counts_ready")
    cs = k.sem("window_counts_summed")
    sm = k.sem("term_tails_ready")
    fl = k.sem("dst_edge_column_blank")
    el = k.sem("terms_loaded")
    zm = k.sem("zeros_ready")
    zs = k.sem("buffers_zeroed")
    tb = k.sem("step_table_ready")
    mx = k.sem("maxima_ready")
    st = k.sem("edge_arrays_saved")
    io = k.sem("step_numbers")
    with ExitStack() as ctx:
        di = k.sb(ctx, "dst_int_wide", [EP, 1 + ET + 1], I32)
        sf = k.sb(ctx, "dst_float_list", [EP, ET])
        fs = k.sb(ctx, "starts_flag", [EP, ET])
        fe = k.sb(ctx, "ends_flag", [EP, ET])
        run = k.sb(ctx, "running", [EP, ET])
        fmin = k.sb(ctx, "flag_min", [EP, 2])
        tot = k.sb(ctx, "totals", [EP, 2, 2 * H])
        totT = k.sb(ctx, "totals_T", [H, 2, 2, EP])
        carT = k.sb(ctx, "carry_T", [H, 2, EP + 1])
        car = k.sb(ctx, "carry", [EP, 2, H])
        cnt = k.sb(ctx, "below_count", [P, NT])
        ends = k.sb(ctx, "window_end", [P, NT])
        wst = k.sb(ctx, "window_start", [P, NT])
        wn = k.sb(ctx, "window_steps", [P, NT])
        wn_i = k.sb(ctx, "window_steps_int", [P, NT], I32)
        kend = k.sb(ctx, "window_last_step", [P, NT])
        wbase = k.sb(ctx, "window_base", [P, NT])
        zero = k.sb(ctx, "window_zero", [P, NT])
        kg_i = k.sb(ctx, "step_number_int", [P, KC], I32)
        kg = k.sb(ctx, "step_number", [P, KC])
        cmp = k.sb(ctx, "step_compare", [P, KC, NT])
        ww = k.sb(ctx, "step_window", [P, KC])
        bb = k.sb(ctx, "step_base", [P, KC])
        tab = k.sb(ctx, "step_table", [P, 2, KC], I32)
        tail = k.sb(ctx, "tail_edges", [P, SUB * S.EW])
        si = k.sb(ctx, "src_int_list", [EP, ET], I32)
        zf = k.sb(ctx, "zeros_f", [P, ZCOLS])
        ptot = k.ps(ctx, "totals_ps", [H, 2, P])
        pcar = k.ps(ctx, "carry_ps", [EP, H])
        pc = k.ps(ctx, "window_ps", [P, NT])
        block = ctx.enter_context(nc.Block())
        dst = ins["dst"]
        dst_pt = dst.rearrange("(p t) -> p t", t=ET)

        @block.sync
        def _(sp):
            sp.dma_start(di[:, 1:1 + ET], dst_pt).then_inc(ld, 16)
            sp.dma_start(si[:, :], ins["src"].rearrange("(p t) -> p t", t=ET)).then_inc(ld, 16)
            sp.wait_ge(fl, 2)
            sp.dma_start(di[1:EP, 0:1], dst_pt[0:EP - 1, ET - 1:ET], allow_slow_non_contiguous=True).then_inc(ld, 16)
            sp.dma_start(di[0:EP - 1, 1 + ET:2 + ET], dst_pt[1:EP, 0:1], allow_slow_non_contiguous=True).then_inc(ld, 16)
            terms = T.terms.rearrange("(p t) h -> p t h", t=ET)
            QUARTER = ET // 4
            for q in range(0, ET, QUARTER):
                sp.dma_start(ea[:, q:q + QUARTER, 0:H], terms[:, q:q + QUARTER, :]).then_inc(el, 16)
            sp.wait_ge(sm, 2)
            sp.dma_start(T.ea[S.E:S.E + STEP, :].rearrange("(p j) h -> p (j h)", j=SUB), tail[:, :]).then_inc(st, 16)
            sp.wait_ge(tb, 1)
            for a in range(2):
                sp.dma_start(T.steps[a, :].rearrange("(p c) -> p c", c=KC), tab[:, a, :]).then_inc(st, 16)
            sp.wait_ge(mx, 1)
            sp.dma_start(T.ea[0:S.E, :].rearrange("(p t) h -> p (t h)", t=ET),
                         ea[:, :, :].rearrange("p t h -> p (t h)")).then_inc(st, 16)
            sp.wait_ge(st, 16 * 4)

        @block.gpsimd
        def _(pool):
            pool.memset(tail[:, :], 0.0).then_inc(sm, 1)
            pool.wait_ge(sm, 1)
            for j in range(SUB):
                last = pool.memset(tail[:, j * S.EW + 2 * H:j * S.EW + 2 * H + 1], -1.0)
            last.then_inc(sm, 1)
            pool.memset(zf[:, :], 0.0).then_inc(zm, 1)
            pool.iota(kg_i[:, :], pattern=[[1, KC]], base=0, channel_multiplier=KC).then_inc(io, 1)

        @block.vector
        def _(dve):
            c = Chain(dve, ch)
            dve.memset(di[:, 0:1], -1).then_inc(fl, 1)
            dve.memset(di[:, 1 + ET:2 + ET], -1).then_inc(fl, 1)
            c.mark(dve.memset(carT[:, :, :], NEG_BIG))
            c.mark(dve.memset(zero[:, :], 0.0))
            c.link(dve.memset(cnt[:, :], 0.0))
            dve.wait_ge(ld, 64)
            c.mark(dve.tensor_tensor(fs[:, :], di[:, 1:1 + ET], di[:, 0:ET], ALU.not_equal))
            c.mark(dve.tensor_tensor(fe[:, :], di[:, 1:1 + ET], di[:, 2:2 + ET], ALU.not_equal))
            c.link(dve.tensor_copy(sf[:, :], di[:, 1:1 + ET]))
            c.mark(dve.tensor_copy(ea[:, :, 2 * H + 1].bitcast(I32), si[:, :]))
            c.mark(dve.tensor_copy(ea[:, :, 2 * H], sf[:, :]))
            c.mark(dve.tensor_scalar(fs[:, :], fs[:, :], NEG_BIG, None, ALU.mult))
            c.link(dve.tensor_scalar(fe[:, :], fe[:, :], NEG_BIG, None, ALU.mult))
            for w in range(NT):
                c.link(dve.tensor_scalar(run[:, :], sf[:, :], float((w + 1) * P), 0.0, ALU.is_lt, ALU.add,
                                         accum_out=cnt[0:EP, w:w + 1]))
            dve.nop(nofuse=True).then_inc(cn, 1)
            c.mark(dve.tensor_reduce(fmin[:, 0:1], fs[:, :], AX.X, ALU.min))
            c.link(dve.tensor_reduce(fmin[:, 1:2], fe[:, :], AX.X, ALU.min))
            for a in range(2):
                c.link(dve.tensor_copy(tot[:, a, H:2 * H], fmin[:, a:a + 1].to_broadcast([EP, H])))
            dve.wait_ge(el, 16 * 4)
            for a in range(2):
                forward = a == 0

                def scan(h, out, initial):
                    data = ea[:, :, h] if forward else ea[:, ::-1, H + h]
                    flag = fs[:, :] if forward else fe[:, ::-1]
                    c.link(dve.tensor_tensor_scan(out, flag, data, initial, ALU.add, ALU.max))
                for h in range(H):
                    scan(h, run[:, :], NEG_BIG)
                    c.link(dve.tensor_copy(tot[:, a, h:h + 1], run[:, ET - 1:ET]))
                dve.nop(nofuse=True).then_inc(tr, 1)
                dve.wait_ge(tq, a + 1)
                c.link(dve.tensor_copy(totT[:, a, :, :], ptot[:, :, 0:EP]))
                if forward:
                    c.link(dve.tensor_tensor_scan(carT[:, a, 1:EP + 1], totT[:, a, 1, :], totT[:, a, 0, :], NEG_BIG,
                                                  ALU.add, ALU.max))
                else:
                    c.link(dve.tensor_tensor_scan(carT[:, a, 0:EP][:, ::-1], totT[:, a, 1, ::-1],
                                                  totT[:, a, 0, ::-1], NEG_BIG, ALU.add, ALU.max))
                dve.nop(nofuse=True).then_inc(cr, 1)
                dve.wait_ge(cb, a + 1)
                c.link(dve.tensor_copy(car[:, a, :], pcar[:, :]))
                for h in range(H):
                    scan(h, ea[:, :, H + h] if forward else ea[:, ::-1, H + h], car[:, a, h:h + 1])
            dve.nop(nofuse=True).then_inc(mx, 1)
            dve.wait_ge(cs, 1)
            dve.wait_ge(io, 1)
            c.link(dve.tensor_copy(kg[:, :], kg_i[:, :]))
            c.link(dve.memset(wst[:, 0:1], 0.0))
            c.link(dve.tensor_copy(ends[:, :], pc[:, :]))
            c.link(dve.tensor_copy(wst[:, 1:NT], ends[:, 0:NT - 1]))
            c.link(dve.tensor_tensor(wn[:, :], ends[:, :], wst[:, :], ALU.subtract))
            c.link(dve.tensor_scalar(wn_i[:, :], wn[:, :], float(STEP - 1), None, ALU.add))
            c.link(dve.tensor_scalar(wn_i[:, :], wn_i[:, :], STEP.bit_length() - 1, None, ALU.arith_shift_right))
            c.link(dve.tensor_copy(wn[:, :], wn_i[:, :]))
            c.link(dve.tensor_tensor_scan(kend[:, :], zero[:, :], wn[:, :], 0.0, ALU.add, ALU.add))
            c.link(dve.tensor_tensor(wbase[:, :], kend[:, :], wn[:, :], ALU.subtract))
            c.link(dve.scalar_tensor_tensor(out=wbase[:, :], in0=wbase[:, :], scalar=-float(STEP), in1=wst[:, :],
                                            op0=ALU.mult, op1=ALU.add))
            grid = [P, KC, NT]
            c.link(dve.tensor_tensor(cmp[:, :, :], kend[:, :].unsqueeze(1).to_broadcast(grid),
                                     kg[:, :].unsqueeze(2).to_broadcast(grid), ALU.is_le))
            c.link(dve.tensor_reduce(ww[:, :], cmp[:, :, :], AX.X, ALU.add))
            c.link(dve.tensor_tensor(cmp[:, :, :], C.iota[:, 0:NT].unsqueeze(1).to_broadcast(grid),
                                     ww[:, :].unsqueeze(2).to_broadcast(grid), ALU.is_equal))
            c.link(dve.tensor_tensor(cmp[:, :, :], cmp[:, :, :], wbase[:, :].unsqueeze(1).to_broadcast(grid),
                                     ALU.mult))
            c.link(dve.tensor_reduce(bb[:, :], cmp[:, :, :], AX.X, ALU.add))
            c.link(dve.scalar_tensor_tensor(out=bb[:, :], in0=kg[:, :], scalar=float(STEP), in1=bb[:, :],
                                            op0=ALU.mult, op1=ALU.add))
            c.link(dve.tensor_scalar(tab[:, 0, :], ww[:, :], float(NT - 1), None, ALU.min))
            c.link(dve.tensor_scalar(tab[:, 1, :], bb[:, :], float(S.E), None, ALU.min))
            dve.nop(nofuse=True).then_inc(tb, 1)

        @block.scalar
        def _(act):
            n = 0
            act.wait_ge(zm, 1)
            for buf in [*T.yf, T.xb1[0:S.G1 * TOK, :], T.xb2[0:S.G2 * TOK, :]]:
                flat = buf.rearrange("(p r) d -> p (r d)", p=P)
                for at in range(0, flat.shape[1], ZCOLS):
                    w = min(ZCOLS, flat.shape[1] - at)
                    act.dma_start(flat[:, at:at + w], zf[:, 0:w]).then_inc(zs, 16)
                    n += 16
            act.wait_ge(zs, n)

        @block.tensor
        def _(pe):
            pe.wait_ge(cn, 1)
            pe.matmul(pc[:, :], C.ones[:, :], cnt[:, :], start=True, stop=True).then_inc(cs, 1)
            for a in range(2):
                pe.wait_ge(tr, a + 1)
                pe.transpose(ptot[:, 0, 0:EP], tot[:, a, 0:H], C.ident[0:EP, 0:EP])
                pe.transpose(ptot[:, 1, 0:EP], tot[:, a, H:2 * H], C.ident[0:EP, 0:EP]).then_inc(tq, 1)
                pe.wait_ge(cr, a + 1)
                pe.transpose(pcar[:, :], carT[:, a, a:a + EP], C.ident[0:H, 0:H]).then_inc(cb, 1)



def load_step_table(k, S, sp, T, tab, sem):
    sp.dma_start(tab[0:1, :, :], T.steps.rearrange("a (b k) -> b a k", b=1)).then_inc(sem, 16)


def gat_edges(k, S, C, T, acc):
    nc = k.nc
    DEPTH = GAT_DEPTH
    H, HD, D, W = S.H, S.HD, S.D, S.D + S.H + 1
    tl = k.sem("gat_table_loaded")
    ld = k.sems("gat_step_loaded", DEPTH)
    ga = k.sems("gat_rows_gathered", DEPTH)
    oh = k.sem("gat_onehot_ready")
    ad = k.sem("gat_dst_terms_ready")
    df = k.sem("gat_difference_ready")
    ch = k.sem("gat_exponent_chain")
    ex = k.sem("gat_exp_ready")
    ms = k.sem("gat_messages_ready")
    sc = k.sem("gat_step_summed")
    dn = k.sem("gat_step_done")
    cl = k.sem("gat_acc_clear")
    with ExitStack() as ctx:
        tab = k.sb(ctx, "gat_table", [1, 2, P * S.KC], I32)
        ed = k.sb(ctx, "gat_terms", [P, DEPTH, SUB, S.EW])
        row = k.sb(ctx, "gat_dst_row", [P, DEPTH, STEP])
        g = k.sb(ctx, "gat_rows", [P, DEPTH, SUB, D])
        oT = k.sb(ctx, "gat_onehot_T", [P, DEPTH, SUB, P])
        o = k.sb(ctx, "gat_onehot", [P, DEPTH, SUB, P])
        z = k.sb(ctx, "gat_z", [P, DEPTH, SUB, 2 * H])
        y = k.sb(ctx, "gat_leaky", [P, DEPTH, SUB, 2 * H])
        q = k.sb(ctx, "gat_exponent", [P, DEPTH, SUB, H])
        m = k.sb(ctx, "gat_messages", [P, DEPTH, SUB, W])
        pa = k.ps(ctx, "gat_dst_ps", [P, 2, 512])
        po = k.ps(ctx, "gat_sum_ps", [P, 2, 512])
        block = ctx.enter_context(nc.Block())

        @block.sync
        def _(sp):
            load_step_table(k, S, sp, T, tab, tl)
            sp.wait_ge(tl, 16)

            def load(i, b, t, first):
                base = sp.value_load(tab[0:1, 1, bass.ds(t, 1)], min_val=0, max_val=S.E)
                if not first:
                    sp.wait_ge(dn, t - (DEPTH - 1))
                    sp.nop(nofuse=True)
                sp.dma_start(ed[:, b, :, :], T.ea[bass.ds(base, STEP), :].rearrange("(p j) h -> p j h", j=SUB)).then_inc(ld[b], 16)
                sp.dma_start(row[:, b, :], T.dst_f[bass.ds(base, STEP)].partition_broadcast(P)).then_inc(ld[b], 16)
            staged(sp, S.STEPS, [(0, load)], DEPTH)

        @block.gpsimd
        def _(pool):
            def gather(i, b, t, first):
                pool.wait_ge(ld[b], i * 32 + 32)
                pool.nop(nofuse=True)
                for j in range(SUB):
                    pool.indirect_dma_start(
                        out=g[:, b, j, :], out_offset=None, in_=T.h[:, :],
                        in_offset=bass.IndirectOffsetOnAxis(ap=ed[:, b, j, 2 * H + 1:2 * H + 2].bitcast(I32), axis=0)).then_inc(ga[b], 16)
            staged(pool, S.STEPS, [(0, gather)], DEPTH)

        @block.scalar
        def _(act):
            act.wait_ge(tl, 16)

            def onehots(i, b, t, first):
                w = act.value_load(tab[0:1, 0, bass.ds(t, 1)], min_val=0, max_val=S.NT - 1)
                act.wait_ge(ld[b], i * 32 + 32)
                nc.scalar.activation(oT[:, b, :, :], row[:, b, :].rearrange("p (e j) -> p j e", j=SUB), ACT.Abs,
                                     bias=C.wiota[:, bass.ds(w, 1)], scale=-1.0)
                for j in range(SUB):
                    last = nc.scalar.activation(o[:, b, j, :], C.iota_n[:, bass.ds(w * P, P)], ACT.Abs,
                                                bias=ed[:, b, j, 2 * H:2 * H + 1], scale=-1.0)
                last.then_inc(df, 1)
                act.wait_ge(df, t + 1)
                nc.scalar.activation(oT[:, b, :, :], oT[:, b, :, :], ACT.Relu, bias=C.one[:, 0:1],
                                     scale=-1.0).then_inc(oh, 1)
                nc.scalar.activation(o[:, b, :, :], o[:, b, :, :], ACT.Relu, bias=C.one[:, 0:1], scale=-1.0)

            def numerators(i, b, t, first):
                act.wait_ge(ch, t * 3 + 3)
                nc.scalar.activation(m[:, b, :, D:D + H], q[:, b, :, :], ACT.Exp).then_inc(ex, 1)
            staged(act, S.STEPS, [(0, onehots), (1, numerators)], DEPTH)

        @block.vector
        def _(dve):
            dve.memset(acc[:, :, :], 0.0).then_inc(cl, 1)
            for b in range(DEPTH):
                dve.memset(m[:, b, :, W - 1:W], 1.0)
            dve.wait_ge(cl, 1)
            dve.wait_ge(tl, 16)

            def terms(i, b, t, first):
                dve.wait_ge(ad, t + 1)
                dve.tensor_tensor(z[:, b, :, :].rearrange("p j (a h) -> p j a h", a=2),
                                  ed[:, b, :, 0:2 * H].rearrange("p j (a h) -> p j a h", a=2),
                                  pa[:, b % 2, 0:SUB * H].rearrange("p (j h) -> p j h", j=SUB).unsqueeze(2)
                                  .to_broadcast([P, SUB, 2, H]), ALU.add).then_inc(ch, 1)

            def leaky(i, b, t, first):
                dve.wait_ge(ch, t * 3 + 1)
                dve.scalar_tensor_tensor(out=y[:, b, :, :], in0=z[:, b, :, :], scalar=0.2, in1=z[:, b, :, :],
                                         op0=ALU.mult, op1=ALU.max).then_inc(ch, 1)

            def exponents(i, b, t, first):
                dve.wait_ge(ch, t * 3 + 2)
                dve.tensor_tensor(q[:, b, :, :], y[:, b, :, 0:H], y[:, b, :, H:2 * H], ALU.subtract).then_inc(ch, 1)

            def message(j):
                def stage(i, b, t, first):
                    if j == 0:
                        dve.wait_ge(ex, t + 1)
                        dve.wait_ge(ga[b], i * (16 * SUB) + 16 * SUB)
                    ins = dve.tensor_tensor(m[:, b, j, 0:D].rearrange("p (h d) -> p h d", h=H),
                                            g[:, b, j, :].rearrange("p (h d) -> p h d", h=H),
                                            m[:, b, j, D:D + H].unsqueeze(2).to_broadcast([P, H, HD]), ALU.mult)
                    if j == SUB - 1:
                        ins.then_inc(ms, 1)
                return stage

            def add(i, b, t, first):
                w = dve.value_load(tab[0:1, 0, bass.ds(t, 1)], min_val=0, max_val=S.NT - 1)
                dve.wait_ge(sc, t + 1)
                if not (first and b == 0):
                    dve.wait_ge(dn, t)
                a = acc[:, bass.ds(w, 1), :].rearrange("p a c -> p (a c)")
                dve.tensor_tensor(a, a, po[:, b % 2, 0:W], ALU.add).then_inc(dn, 1)
            staged(dve, S.STEPS, [(1, terms), (2, message(0)), (1, leaky), (2, message(1)), (1, exponents), (3, add)],
                   DEPTH)

        @block.tensor
        def _(pe):
            pe.wait_ge(tl, 16)

            def dst_terms(i, b, t, first):
                w = pe.value_load(tab[0:1, 0, bass.ds(t, 1)], min_val=0, max_val=S.NT - 1)
                pe.wait_ge(oh, t + 1)
                if not (first and b < 2):
                    pe.wait_ge(ch, t * 3 - 5)
                for j in range(SUB):
                    last = pe.matmul(pa[:, b % 2, j * H:(j + 1) * H], oT[:, b, j, :],
                                     C.adst[:, bass.ds(w, 1), :].rearrange("p a h -> p (a h)"), start=True, stop=True)
                last.then_inc(ad, 1)

            def scatter(i, b, t, first):
                pe.wait_ge(ms, t + 1)
                if not (first and b < 2):
                    pe.wait_ge(dn, t - 1)
                for j in range(SUB):
                    last = pe.matmul(po[:, b % 2, 0:W], o[:, b, j, :], m[:, b, j, :],
                                     start=j == 0, stop=j == SUB - 1)
                last.then_inc(sc, 1)
            staged(pe, S.STEPS, [(0, dst_terms), (2, scatter)], DEPTH)


def gat_finish(k, S, C, acc, x_res, x_dram):
    nc = k.nc
    NT, H, D = S.NT, S.H, S.D
    xl = k.sem("residual_x_loaded")
    ch = k.sem("gat_finish_chain")
    with ExitStack() as ctx:
        den = k.sb(ctx, "gat_den", [P, NT, H])
        block = ctx.enter_context(nc.Block())

        @block.gpsimd
        def _(pool):
            pool.memset(x_res[:, NT - 1, :], 0.0).then_inc(xl, 1)

        @block.sync
        def _(sp):
            sp.wait_ge(xl, 1)
            full, tail = rows_of(x_dram, S)
            sp.dma_start(x_res[:, 0:NT - 1, :], full).then_inc(xl, 16)
            sp.dma_start(x_res[0:S.TAIL, NT - 1, :], tail).then_inc(xl, 16)

        @block.vector
        def _(dve):
            c = Chain(dve, ch)
            out = acc[:, :, 0:D]
            heads = out.rearrange("p n (h d) -> p n h d", h=H)
            c.mark(dve.tensor_scalar(C.out_deg[:, :], acc[:, :, D + H], 1.0, None, ALU.add))
            c.link(dve.tensor_scalar(den[:, :, :], acc[:, :, D:D + H], 1e-16, None, ALU.add))
            c.link(dve.reciprocal(den[:, :, :], den[:, :, :]))
            c.link(dve.tensor_tensor(heads, heads, den[:, :, :].unsqueeze(3).to_broadcast([P, NT, H, S.HD]), ALU.mult))
            c.link(dve.tensor_tensor(out, out, C.gat_bias[:, :].unsqueeze(1).to_broadcast([P, NT, D]), ALU.add))
            dve.wait_ge(xl, 33)
            c.link(dve.scalar_tensor_tensor(out=x_res[:, :, :], in0=out, scalar=0.0, in1=x_res[:, :, :],
                                            op0=ALU.max, op1=ALU.add))



def gnn_scale(k, S, C, T, z):
    nc = k.nc
    ch = k.sem("scale_chain")
    rt = k.sem("degree_roots")
    st = k.sem("zb_stored")
    with ExitStack() as ctx:
        sd = k.sb(ctx, "degree_root", [P, 2, S.NT])
        block = ctx.enter_context(nc.Block())

        @block.scalar
        def _(act):
            nc.scalar.activation(sd[:, 0, :], C.out_deg[:, :], ACT.Sqrt).then_inc(rt, 1)
            nc.scalar.activation(sd[:, 1, :], C.in_deg[:, :], ACT.Sqrt).then_inc(rt, 1)

        @block.vector
        def _(dve):
            c = Chain(dve, ch)
            dve.wait_ge(rt, 2)
            c.link(dve.reciprocal(C.dinv[:, :, :], sd[:, :, :]))
            for a in (1, 0):
                part = z[:, :, a * P:(a + 1) * P]
                c.mark(dve.tensor_tensor(part, part, C.dinv[:, a, :].unsqueeze(2).to_broadcast([P, S.NT, P]), ALU.mult))

        @block.sync
        def _(sp):
            sp.wait_ge(ch, 2)
            sp.dma_start(T.zb.rearrange("(i p) d -> p i d", p=P), z[:, :, P:2 * P]).then_inc(st, 16)
            sp.wait_ge(st, 16)


def gnn_edges(k, S, C, T, z, acc):
    nc = k.nc
    DEPTH = GNN_DEPTH
    DUP_OPS = 4
    SPARE = S.NT * P
    tl = k.sem("gnn_table_loaded")
    ld = k.sems("gnn_step_loaded", DEPTH)
    ga = k.sems("gnn_rows_gathered", DEPTH)
    oh = k.sem("gnn_onehot_ready")
    dp = k.sem("gnn_duplicate_chain")
    pc = k.sem("gnn_pair_ready")
    mc = k.sem("gnn_pair_copied")
    pm = k.sem("gnn_message_ready")
    ms = k.sem("gnn_message_copied")
    sc = k.sem("gnn_step_summed")
    dn = k.sem("gnn_step_done")
    sa = k.sems("gnn_rows_added", 2)
    cl = k.sem("gnn_acc_clear")
    with ExitStack() as ctx:
        tab = k.sb(ctx, "gnn_table", [1, 2, P * S.KC], I32)
        sd = k.sb(ctx, "gnn_src_dst", [P, DEPTH, SUB, 3])
        row = k.sb(ctx, "gnn_src_row", [P, DEPTH, STEP])
        g = k.sb(ctx, "gnn_rows", [P, DEPTH, SUB, P])
        o = k.sb(ctx, "gnn_onehot", [P, DEPTH, SUB, P])
        eq = k.sb(ctx, "gnn_same_src", [P, DEPTH, SUB, P])
        junk = k.sb(ctx, "gnn_junk", [P, 2, SUB, P])
        dup = k.sb(ctx, "gnn_earlier", [P, DEPTH, SUB])
        away = k.sb(ctx, "gnn_away", [P, DEPTH, SUB])
        to = k.sb(ctx, "gnn_add_idx", [P, DEPTH, SUB], I32)
        spare = k.sb(ctx, "gnn_spare", [P, 1])
        pr = k.sb(ctx, "gnn_pair", [P, DEPTH, SUB, P])
        m = k.sb(ctx, "gnn_message", [P, DEPTH, SUB, P])
        pp = k.ps(ctx, "gnn_pair_ps", [P, 2, 512])
        pq = k.ps(ctx, "gnn_message_ps", [P, 2, 512])
        po = k.ps(ctx, "gnn_sum_ps", [P, 2, 512])
        block = ctx.enter_context(nc.Block())

        @block.sync
        def _(sp):
            load_step_table(k, S, sp, T, tab, tl)
            sp.wait_ge(tl, 16)

            def load(i, b, t, first):
                base = sp.value_load(tab[0:1, 1, bass.ds(t, 1)], min_val=0, max_val=S.E)
                if not first:
                    sp.wait_ge(dn, t - (DEPTH - 1))
                    sp.nop(nofuse=True)
                    sp.wait_ge(dp, (t - (DEPTH - 1)) * DUP_OPS)
                    sp.nop(nofuse=True)
                sp.dma_start(sd[:, b, :, :], T.sd[bass.ds(base, STEP), :].rearrange("(p j) c -> p j c", j=SUB)).then_inc(ld[b], 16)
                sp.dma_start(row[:, b, :], T.src_f[bass.ds(base, STEP)].partition_broadcast(P)).then_inc(ld[b], 16)
            staged(sp, S.STEPS, [(0, load)], DEPTH)

        @block.gpsimd
        def _(pool):
            def gather(i, b, t, first):
                pool.wait_ge(ld[b], i * 32 + 32)
                pool.nop(nofuse=True)
                for j in range(SUB):
                    pool.indirect_dma_start(
                        out=g[:, b, j, :], out_offset=None, in_=T.zb[:, :],
                        in_offset=bass.IndirectOffsetOnAxis(ap=sd[:, b, j, 2:3].bitcast(I32), axis=0)).then_inc(ga[b], 16)

            def add_rows(i, b, t, first):
                pool.wait_ge(ms, t + 1)
                if not (first and b < 2):
                    pool.wait_ge(sa[b % 2], i * (16 * SUB * (DEPTH // 2)) + 16 * SUB * (b // 2))
                pool.nop(nofuse=True)
                for j in range(SUB):
                    pool.indirect_dma_start(
                        out=T.yf[SUB * (b % 2) + j][:, :],
                        out_offset=bass.IndirectOffsetOnAxis(ap=to[:, b, j:j + 1], axis=0),
                        in_=m[:, b, j, :], in_offset=None, compute_op=ALU.add).then_inc(sa[b % 2], 16)
            staged(pool, S.STEPS, [(0, gather), (2, add_rows)], DEPTH)
            for b in range(2):
                pool.wait_ge(sa[b], 16 * SUB * (S.STEPS // 2))

        @block.vector
        def _(dve):
            dve.memset(acc[:, :, :], 0.0).then_inc(cl, 1)
            dve.tensor_scalar(spare[:, :], C.wiota[:, 0:1], float(SPARE), None, ALU.add).then_inc(cl, 1)
            dve.wait_ge(cl, 2)
            dve.wait_ge(tl, 16)

            def onehots(i, b, t, first):
                w = dve.value_load(tab[0:1, 0, bass.ds(t, 1)], min_val=0, max_val=S.NT - 1)
                dve.wait_ge(ld[b], i * 32 + 32)
                if not first:
                    dve.wait_ge(sa[b % 2], i * (16 * SUB * (DEPTH // 2)) + (16 * SUB * (b // 2) - 16 * SUB * (DEPTH // 2 - 1)))
                for j in range(SUB):
                    dve.tensor_scalar(o[:, b, j, :], C.iota_n[:, bass.ds(w * P, P)], sd[:, b, j, 1:2], None,
                                      ALU.is_equal)
                    last = dve.tensor_scalar(eq[:, b, j, :], row[:, b, :].rearrange("p (e j) -> p j e", j=SUB)[:, j, :],
                                             sd[:, b, j, 0:1], None, ALU.is_equal)
                last.then_inc(oh, 1)

            def row_numbers(i, b, t, first):
                dve.wait_ge(oh, t + 1)
                for j in range(SUB):
                    last = dve.tensor_tensor_reduce(out=junk[:, b % 2, j, :], in0=eq[:, b, j, :], in1=C.lower[:, :], scale=1.0,
                                                    scalar=0.0, op0=ALU.mult, op1=ALU.add,
                                                    accum_out=dup[:, b, j:j + 1])
                last.then_inc(dp, 1)
                dve.tensor_scalar(away[:, b, :], sd[:, b, :, 0], -1.0, spare[:, 0:1], ALU.mult, ALU.add).then_inc(dp, 1)
                dve.wait_ge(dp, t * DUP_OPS + 2)
                dve.scalar_tensor_tensor(out=away[:, b, :], in0=dup[:, b, :], scalar=0.5, in1=away[:, b, :],
                                         op0=ALU.is_gt, op1=ALU.mult).then_inc(dp, 1)
                dve.wait_ge(dp, t * DUP_OPS + 3)
                dve.tensor_tensor(to[:, b, :], away[:, b, :], sd[:, b, :, 0], ALU.add).then_inc(dp, 1)

            def add(i, b, t, first):
                w = dve.value_load(tab[0:1, 0, bass.ds(t, 1)], min_val=0, max_val=S.NT - 1)
                dve.wait_ge(sc, t + 1)
                if not (first and b == 0):
                    dve.wait_ge(dn, t)
                a = acc[:, bass.ds(w, 1), :].rearrange("p a c -> p (a c)")
                dve.tensor_tensor(a, a, po[:, b % 2, 0:P], ALU.add).then_inc(dn, 1)
            staged(dve, S.STEPS, [(0, onehots), (1, row_numbers), (2, add)], DEPTH)

        @block.scalar
        def _(act):
            def pairs(i, b, t, first):
                act.wait_ge(pc, t + 1)
                nc.scalar.copy(pr[:, b, :, :], pp[:, b % 2, 0:SUB * P].rearrange("p (j e) -> p j e", j=SUB)).then_inc(mc, 1)

            def messages(i, b, t, first):
                act.wait_ge(pm, t + 1)
                act.wait_ge(dp, t * DUP_OPS + DUP_OPS)
                if not first:
                    act.wait_ge(sa[b % 2], i * (16 * SUB * (DEPTH // 2)) + (16 * SUB * (b // 2) - 16 * SUB * (DEPTH // 2 - 1)))
                nc.scalar.copy(m[:, b, :, :], pq[:, b % 2, 0:SUB * P].rearrange("p (j e) -> p j e", j=SUB)).then_inc(ms, 1)
            staged(act, S.STEPS, [(0, pairs), (1, messages)], DEPTH)

        @block.tensor
        def _(pe):
            pe.wait_ge(tl, 16)

            def pairs(i, b, t, first):
                pe.wait_ge(oh, t + 1)
                if not (first and b < 2):
                    pe.wait_ge(mc, t - 1)
                for j in range(SUB):
                    last = pe.matmul(pp[:, b % 2, j * P:(j + 1) * P], o[:, b, j, :], eq[:, b, j, :],
                                     start=True, stop=True)
                last.then_inc(pc, 1)

            def messages(i, b, t, first):
                w = pe.value_load(tab[0:1, 0, bass.ds(t, 1)], min_val=0, max_val=S.NT - 1)
                pe.wait_ge(mc, t + 1)
                if not (first and b < 2):
                    pe.wait_ge(ms, t - 1)
                for j in range(SUB):
                    last = pe.matmul(pq[:, b % 2, j * P:(j + 1) * P], pr[:, b, j, :],
                                     z[:, bass.ds(w, 1), 0:P].rearrange("p a c -> p (a c)"), start=True, stop=True)
                last.then_inc(pm, 1)
                pe.wait_ge(ga[b], i * (16 * SUB) + 16 * SUB)
                if not (first and b < 2):
                    pe.wait_ge(dn, t - 1)
                for j in range(SUB):
                    last = pe.matmul(po[:, b % 2, 0:P], o[:, b, j, :], g[:, b, j, :], start=j == 0, stop=j == SUB - 1)
                last.then_inc(sc, 1)
            staged(pe, S.STEPS, [(0, pairs), (1, messages)], DEPTH)


def gnn_finish(k, S, C, T, z, acc, x_res):
    nc = k.nc
    NT = S.NT
    ld = k.sems("forward_sums_loaded", 2)
    us = k.sems("forward_sums_used", 2)
    ch = k.sem("gnn_finish_chain")
    HALF = 7
    with ExitStack() as ctx:
        f = k.sb(ctx, "forward_sums_sb", [P, 2, HALF, P])
        block = ctx.enter_context(nc.Block())
        parts = [(g, y) for g in range(NT // HALF) for y in range(2 * SUB)]

        @block.sync
        def _(sp):
            for n, (g, y) in enumerate(parts):
                if n >= 2:
                    sp.wait_ge(us[n % 2], n // 2)
                sp.dma_start(f[:, n % 2, :, :], T.yf[y][g * HALF * P:(g + 1) * HALF * P, :]
                             .rearrange("(i p) d -> p i d", p=P)).then_inc(ld[n % 2], 16)

        @block.vector
        def _(dve):
            c = Chain(dve, ch)
            for n, (g, y) in enumerate(parts):
                part = z[:, g * HALF:(g + 1) * HALF, 0:P]
                dve.wait_ge(ld[n % 2], 16 * (n // 2 + 1))
                dve.tensor_tensor(part, part, f[:, n % 2, :, :], ALU.add).then_inc(us[n % 2], 1)
                dve.wait_ge(us[n % 2], n // 2 + 1)
            back = z[:, :, P:2 * P]
            c.link(dve.tensor_tensor(back, back, acc[:, :, :], ALU.add))
            for a in range(2):
                part = z[:, :, a * P:(a + 1) * P]
                c.link(dve.tensor_tensor(part, part, C.dinv[:, 1 - a, :].unsqueeze(2).to_broadcast([P, NT, P]),
                                         ALU.mult))
            c.link(dve.tensor_tensor(z[:, :, :], z[:, :, :],
                                     C.gnn_bias[:, :].unsqueeze(1).to_broadcast([P, NT, S.D]), ALU.add))
            c.link(dve.tensor_tensor(x_res[:, :, :], x_res[:, :, :], z[:, :, :], ALU.add))



def route(k, S, C, tag, logits, bias, choices, n_exp, capacity, idx_put, idx_get, weight, gtab):
    nc = k.nc
    NT, X = S.NT, n_exp
    groups = S.G1 if capacity is None else S.G2
    ch = k.sem(f"{tag}_route_chain")
    ex = k.sem(f"{tag}_route_exp_in")
    eo = k.sem(f"{tag}_route_exp_out")
    mr = k.sem(f"{tag}_route_mask_ready")
    rk = k.sem(f"{tag}_route_ranks")
    io = k.sem(f"{tag}_route_iota")
    with ExitStack() as ctx:
        lg = k.sb(ctx, f"{tag}_logits", [P, NT, X])
        t0 = k.sb(ctx, f"{tag}_t0", [P, NT, X])
        pv = k.sb(ctx, f"{tag}_pv", [P, NT, X])
        mk = k.sb(ctx, f"{tag}_masks", [P, choices, NT, X])
        both = k.sb(ctx, f"{tag}_both", [P, NT, X])
        mx = k.sb(ctx, f"{tag}_mx", [P, choices, NT])
        ix = k.sb(ctx, f"{tag}_ix", [P, NT])
        dd = k.sb(ctx, f"{tag}_dd", [P, NT])
        valid = k.sb(ctx, f"{tag}_valid", [P, NT])
        pos = k.sb(ctx, f"{tag}_pos", [P, NT, X])
        tot = k.sb(ctx, f"{tag}_tot", [P, X, NT])
        car = k.sb(ctx, f"{tag}_car", [P, X, NT + 1])
        zero = k.sb(ctx, f"{tag}_zero", [P, max(NT, X)])
        ng = k.sb(ctx, f"{tag}_ng", [P, X])
        ng_i = k.sb(ctx, f"{tag}_ng_i", [P, X], I32)
        gend = k.sb(ctx, f"{tag}_gend", [P, X])
        base = k.sb(ctx, f"{tag}_base", [P, X])
        sl = k.sb(ctx, f"{tag}_slot", [P, NT])
        kp = k.sb(ctx, f"{tag}_kept", [P, NT])
        gc = k.sb(ctx, f"{tag}_gcmp", [P, groups, X])
        gw = k.sb(ctx, f"{tag}_gw", [P, groups])
        pk = k.ps(ctx, f"{tag}_rank_ps", [P, 512])
        pt = k.ps(ctx, f"{tag}_total_ps", [P, 512])
        block = ctx.enter_context(nc.Block())
        grid = [P, NT, X]

        def wide(v):
            return v.unsqueeze(2).to_broadcast(grid)

        def over(v):
            return v.unsqueeze(1).to_broadcast(grid)

        @block.vector
        def _(dve):
            c = Chain(dve, ch)
            tt, ts = dve.tensor_tensor, dve.tensor_scalar
            c.link(tt(lg[:, :, :], logits[:, :, :], over(bias[:, :]), ALU.add))
            c.link(dve.memset(zero[:, :], 0.0))
            c.link(ts(valid[:, :], C.wiota[:, :], float(S.N) - 0.5, None, ALU.is_lt))

            def first_of(values, m, out):
                c.link(tt(t0[:, :, :], values[:, :, :], wide(m), ALU.is_equal))
                c.link(ts(t0[:, :, :], t0[:, :, :], -float(X), float(X), ALU.mult, ALU.add))
                c.link(tt(t0[:, :, :], t0[:, :, :], over(C.iota[:, 0:X]), ALU.add))
                c.link(dve.tensor_reduce(ix[:, :], t0[:, :, :], AX.X, ALU.min))
                c.link(tt(out, over(C.iota[:, 0:X]), wide(ix[:, :]), ALU.is_equal))

            c.link(dve.tensor_reduce(mx[:, 0, :], lg[:, :, :], AX.X, ALU.max))
            if choices == 2:
                first_of(lg, mx[:, 0, :], mk[:, 0, :, :])
                c.link(dve.tensor_copy(pv[:, :, :], lg[:, :, :]))
                c.link(ts(t0[:, :, :], mk[:, 0, :, :], 2.0 * NEG_BIG, None, ALU.mult))
                c.link(tt(pv[:, :, :], pv[:, :, :], t0[:, :, :], ALU.add))
                c.link(dve.tensor_reduce(mx[:, 1, :], pv[:, :, :], AX.X, ALU.max))
                first_of(pv, mx[:, 1, :], mk[:, 1, :, :])
                c.link(tt(dd[:, :], mx[:, 1, :], mx[:, 0, :], ALU.subtract))
                dve.nop(nofuse=True).then_inc(ex, 1)
                dve.wait_ge(eo, 1)
                c.link(ts(sl[:, :], kp[:, :], 1.0, None, ALU.add))
                c.link(dve.reciprocal(weight[:, 0, :], sl[:, :]))
                c.link(tt(weight[:, 1, :], weight[:, 0, :], kp[:, :], ALU.mult))
                c.link(tt(both[:, :, :], mk[:, 0, :, :], mk[:, 1, :, :], ALU.add))
            else:
                c.link(tt(pv[:, :, :], lg[:, :, :], wide(mx[:, 0, :]), ALU.subtract))
                dve.nop(nofuse=True).then_inc(ex, 1)
                dve.wait_ge(eo, 1)
                c.link(dve.tensor_reduce(sl[:, :], pos[:, :, :], AX.X, ALU.add))
                c.link(dve.reciprocal(dd[:, :], sl[:, :]))
                c.link(tt(pv[:, :, :], pos[:, :, :], wide(dd[:, :]), ALU.mult))
                c.link(dve.tensor_reduce(mx[:, 0, :], pv[:, :, :], AX.X, ALU.max))
                first_of(pv, mx[:, 0, :], mk[:, 0, :, :])
                c.link(dve.tensor_copy(weight[:, 0, :], mx[:, 0, :]))
                c.link(dve.tensor_copy(both[:, :, :], mk[:, 0, :, :]))
            c.link(tt(both[:, :, :], both[:, :, :], wide(valid[:, :]), ALU.mult))
            dve.nop(nofuse=True).then_inc(mr, 1)
            dve.wait_ge(rk, 1)
            c.link(dve.tensor_copy(tot[:, :, :], pt[:, 0:NT * X].rearrange("p (n x) -> p x n", x=X)))
            c.link(dve.memset(car[:, :, 0:1], 0.0))
            for e in range(X):
                c.link(dve.tensor_tensor_scan(car[:, e, 1:NT + 1], zero[:, 0:NT], tot[:, e, :], 0.0, ALU.add, ALU.add))
            c.link(tt(pos[:, :, :], pk[:, 0:NT * X].rearrange("p (n x) -> p n x", x=X),
                      car[:, :, 0:NT].rearrange("p x n -> p n x"), ALU.add))
            if capacity is None:
                c.link(ts(ng_i[:, :], car[:, :, NT], float(TOK - 1), None, ALU.add))
                c.link(ts(ng_i[:, :], ng_i[:, :], TOK.bit_length() - 1, None, ALU.arith_shift_right))
                c.link(dve.tensor_copy(ng[:, :], ng_i[:, :]))
                c.link(dve.tensor_tensor_scan(gend[:, :], zero[:, 0:X], ng[:, :], 0.0, ALU.add, ALU.add))
                c.link(tt(base[:, :], gend[:, :], ng[:, :], ALU.subtract))
                c.link(ts(base[:, :], base[:, :], float(TOK), None, ALU.mult))
                gg = [P, groups, X]
                c.link(tt(gc[:, :, :], gend[:, :].unsqueeze(1).to_broadcast(gg),
                          C.iota[:, 0:groups].unsqueeze(2).to_broadcast(gg), ALU.is_le))
                c.link(dve.tensor_reduce(gw[:, :], gc[:, :, :], AX.X, ALU.add))
                c.link(ts(gtab[0:1, :], gw[0:1, :], float(X - 1), None, ALU.min))
            else:
                c.link(ts(base[:, :], C.iota[:, 0:X], float(groups * TOK // X), None, ALU.mult))
            for n in range(choices):
                def chosen(v, out):
                    c.link(tt(t0[:, :, :], mk[:, n, :, :], v, ALU.mult))
                    c.link(dve.tensor_reduce(out, t0[:, :, :], AX.X, ALU.add))
                chosen(pos[:, :, :], sl[:, :])
                chosen(over(base[:, :]), dd[:, :])
                if capacity is None:
                    c.link(dve.tensor_copy(kp[:, :], valid[:, :]))
                else:
                    c.link(ts(kp[:, :], sl[:, :], float(capacity) - 0.5, None, ALU.is_lt))
                    c.link(tt(weight[:, n, :], weight[:, n, :], kp[:, :], ALU.mult))
                    c.link(tt(kp[:, :], kp[:, :], valid[:, :], ALU.mult))
                    c.link(ts(sl[:, :], sl[:, :], float(capacity - 1), None, ALU.min))
                c.link(tt(sl[:, :], sl[:, :], dd[:, :], ALU.add))
                c.link(ts(idx_get[:, n, :], sl[:, :], float(groups * TOK - 1), None, ALU.min))
                c.link(ts(dd[:, :], C.wiota[:, :], float(groups * TOK + n * S.ROWS), None, ALU.add))
                c.link(tt(sl[:, :], sl[:, :], dd[:, :], ALU.subtract))
                c.link(tt(sl[:, :], sl[:, :], kp[:, :], ALU.mult))
                c.link(tt(idx_put[:, n, :], sl[:, :], dd[:, :], ALU.add))

        @block.scalar
        def _(act):
            act.wait_ge(ex, 1)
            if choices == 2:
                nc.scalar.activation(kp[:, :], dd[:, :], ACT.Exp).then_inc(eo, 1)
            else:
                nc.scalar.activation(pos[:, :, :], pv[:, :, :], ACT.Exp).then_inc(eo, 1)

        @block.tensor
        def _(pe):
            pe.wait_ge(mr, 1)
            flat = both[:, :, :].rearrange("p n x -> p (n x)")
            pe.matmul(pk[:, 0:NT * X], C.upper[:, :], flat, start=True, stop=True)
            pe.matmul(pt[:, 0:NT * X], C.ones[:, :], flat, start=True, stop=True).then_inc(rk, 1)


def put_rows(k, S, tag, xn_all, idx_put, choices, buf):
    nc = k.nc
    pt = k.sem(f"{tag}_rows_put")
    with ExitStack() as ctx:
        block = ctx.enter_context(nc.Block())

        @block.gpsimd
        def _(pool):
            for i in range(S.NT):
                for n in range(choices):
                    pool.indirect_dma_start(
                        out=buf[:, :], out_offset=bass.IndirectOffsetOnAxis(ap=idx_put[:, n, i:i + 1], axis=0),
                        in_=xn_all[:, i, :], in_offset=None).then_inc(pt, 16)
            pool.wait_ge(pt, 16 * S.NT * choices)


def experts(k, S, C, tag, groups, F, func, xb, yb, w1, b1, w2, b2, expert_of):
    nc = k.nc
    FC = F // P
    Q = TOK // P
    D = S.D
    wl = k.sems(f"{tag}_weights_loaded", 2)
    xl = k.sems(f"{tag}_rows_loaded", 2)
    tp = k.sem(f"{tag}_rows_turned")
    tc = k.sem(f"{tag}_turned_copied")
    hp = k.sem(f"{tag}_hidden_product")
    hc = k.sem(f"{tag}_hidden_ready")
    yp = k.sem(f"{tag}_out_product")
    yc = k.sem(f"{tag}_out_ready")
    ys = k.sems(f"{tag}_out_stored", 2)
    with ExitStack() as ctx:
        w1s = k.sb(ctx, f"{tag}_w1", [P, 2, 2, F])
        w2s = k.sb(ctx, f"{tag}_w2", [P, 2, FC, D])
        b1s = k.sb(ctx, f"{tag}_b1", [P, 2, FC])
        b2s = k.sb(ctx, f"{tag}_b2", [P, 2, D])
        xr = k.sb(ctx, f"{tag}_rows", [P, 2, Q, D])
        xT = k.sb(ctx, f"{tag}_rows_T", [P, 2, 2, TOK])
        hT = k.sb(ctx, f"{tag}_hidden", [P, FC, TOK])
        yo = k.sb(ctx, f"{tag}_out_rows", [P, 2, Q, D])
        px = k.ps(ctx, f"{tag}_turn_ps", [P, 2, TOK])
        ph = k.ps(ctx, f"{tag}_hidden_ps", [P, 2, TOK])
        py = k.ps(ctx, f"{tag}_out_ps", [P, 2, 512])
        block = ctx.enter_context(nc.Block())

        @block.sync
        def _(sp):
            def load(i, b, t, first):
                e = expert_of(sp, t)
                if not first:
                    sp.wait_ge(yc, (t - 1) * Q)
                    sp.nop(nofuse=True)
                at = t * TOK
                sp.dma_start(xr[:, b, :, :], xb[bass.ds(at, TOK), :].rearrange("(q p) d -> p q d", p=P)).then_inc(xl[b], 16)
                sp.dma_start(w1s[:, b, :, :], w1[bass.ds(e, 1), :, :].rearrange("a (c p) f -> p (a c) f", p=P)).then_inc(wl[b], 16)
                sp.dma_start(b1s[:, b, :], b1[bass.ds(e, 1), :].rearrange("a (p c) -> p (a c)", p=P)).then_inc(wl[b], 16)
                sp.dma_start(w2s[:, b, :, :], w2[bass.ds(e, 1), :, :].rearrange("a (p c) d -> p (a c) d", p=P)).then_inc(wl[b], 16)
                sp.dma_start(b2s[:, b, :], b2[bass.ds(e, 1), :].rearrange("a d -> (a d)").partition_broadcast(P)).then_inc(wl[b], 16)

            def store(i, b, t, first):
                sp.wait_ge(yc, t * Q + Q)
                sp.nop(nofuse=True)
                sp.dma_start(yb[bass.ds(t * TOK, TOK), :].rearrange("(q p) d -> p q d", p=P), yo[:, b, :, :]).then_inc(ys[b], 16)
            staged(sp, groups, [(0, load), (2, store)], 2)
            for b in range(2):
                sp.wait_ge(ys[b], 16 * (groups // 2))

        @block.tensor
        def _(pe):
            def turn(i, b, t, first):
                pe.wait_ge(xl[b], i * 16 + 16)
                if not (first and b == 0):
                    pe.wait_ge(tc, t * 2)
                for c in range(2):
                    for q in range(Q):
                        last = pe.transpose(px[:, c, q * P:(q + 1) * P], xr[:, b, q, c * P:(c + 1) * P], C.ident[:, :])
                    last.then_inc(tp, 1)

            def hidden(i, b, t, first):
                pe.wait_ge(tc, t * 2 + 2)
                pe.wait_ge(wl[b], i * 64 + 64)
                for f in range(FC):
                    if not (first and b == 0 and f < 2):
                        pe.wait_ge(hc, t * FC + (f - 1))
                    for c in range(2):
                        last = pe.matmul(ph[:, f % 2, :], w1s[:, b, c, f:F:FC], xT[:, b, c, :],
                                         start=c == 0, stop=c == 1)
                    last.then_inc(hp, 1)

            def outs(i, b, t, first):
                pe.wait_ge(hc, t * FC + FC)
                for q in range(Q):
                    if not (first and b == 0 and q < 2):
                        pe.wait_ge(yc, t * Q + (q - 1))
                    for f in range(FC):
                        last = pe.matmul(py[:, q % 2, 0:D], hT[:, f, q * P:(q + 1) * P], w2s[:, b, f, :],
                                         start=f == 0, stop=f == FC - 1)
                    last.then_inc(yp, 1)
            staged(pe, groups, [(1, hidden), (0, turn), (1, outs)], 2)

        @block.scalar
        def _(act):
            def hidden(i, b, t, first):
                for f in range(FC):
                    act.wait_ge(hp, t * FC + (f + 1))
                    if f == 0 and not (first and b == 0):
                        act.wait_ge(yp, t * Q)
                    nc.scalar.activation(hT[:, f, :], ph[:, f % 2, :], func, bias=b1s[:, b, f:f + 1]).then_inc(hc, 1)
            staged(act, groups, [(0, hidden)], 2)

        @block.vector
        def _(dve):
            def turned(i, b, t, first):
                for c in range(2):
                    dve.wait_ge(tp, t * 2 + (c + 1))
                    if not first:
                        dve.wait_ge(hp, (t - 1) * FC)
                    dve.tensor_copy(xT[:, b, c, :], px[:, c, :]).then_inc(tc, 1)

            def outs(i, b, t, first):
                if not first:
                    dve.wait_ge(ys[b], i * 16)
                for q in range(Q):
                    dve.wait_ge(yp, t * Q + (q + 1))
                    dve.tensor_tensor(yo[:, b, q, :], py[:, q % 2, 0:D], b2s[:, b, :], ALU.add).then_inc(yc, 1)
            staged(dve, groups, [(0, turned), (1, outs)], 2)


def take_rows(k, S, C, tag, idx_get, choices, weight, buf, x_res, guard):
    nc = k.nc
    NT, D = S.NT, S.D
    gt = k.sem(f"{tag}_rows_taken")
    ch = k.sem(f"{tag}_take_chain")
    with ExitStack() as ctx:
        y = k.sb(ctx, f"{tag}_taken", [P, choices, NT, D])
        if guard:
            t = k.sb(ctx, f"{tag}_guarded", [P, GROUP, D])
            ok = k.sb(ctx, f"{tag}_in_range", [P, 3, GROUP, D], I32)
            lim = k.sb(ctx, f"{tag}_limits", [P, 3, 1])
        block = ctx.enter_context(nc.Block())

        @block.gpsimd
        def _(pool):
            for n in range(choices):
                for i in range(NT):
                    pool.indirect_dma_start(
                        out=y[:, n, i, :], out_offset=None, in_=buf[:, :],
                        in_offset=bass.IndirectOffsetOnAxis(ap=idx_get[:, n, i:i + 1], axis=0)).then_inc(gt, 16)

        @block.vector
        def _(dve):
            c = Chain(dve, ch)
            if guard:
                c.link(dve.memset(lim[:, 0, :], 0.0))
                c.link(dve.memset(lim[:, 1, :], 1e4))
                c.link(dve.memset(lim[:, 2, :], -1e4))
            for n in range(choices):
                dve.wait_ge(gt, 16 * NT * choices)
                c.link(dve.tensor_tensor(y[:, n, :, :], y[:, n, :, :],
                                         weight[:, n, :].unsqueeze(2).to_broadcast([P, NT, D]), ALU.mult))
                if guard:
                    for g in range(NT // GROUP):
                        v = y[:, n, g * GROUP:(g + 1) * GROUP, :]
                        shape = [P, GROUP, D]
                        c.mark(dve.tensor_tensor(ok[:, 0, :, :], v, v, ALU.not_equal))
                        c.mark(dve.tensor_scalar(ok[:, 1, :, :], v, 3.4028234663852886e38, None, ALU.is_gt))
                        c.link(dve.tensor_scalar(ok[:, 2, :, :], v, -3.4028234663852886e38, None, ALU.is_lt))
                        for m in range(3):
                            c.link(dve.copy_predicated(v, ok[:, m, :, :], lim[:, m, :].unsqueeze(1).to_broadcast(shape)))
                c.link(dve.tensor_tensor(x_res[:, :, :], x_res[:, :, :], y[:, n, :, :], ALU.add))


class Namespace:
    pass


def store_rows(k, S, x_res, out):
    nc = k.nc
    st = k.sem("output_stored")
    with ExitStack() as ctx:
        block = ctx.enter_context(nc.Block())

        @block.sync
        def _(sp):
            full, tail = rows_of(out, S)
            sp.dma_start(full, x_res[:, 0:S.NT - 1, :]).then_inc(st, 16)
            sp.dma_start(tail, x_res[0:S.TAIL, S.NT - 1, :]).then_inc(st, 16)
            sp.wait_ge(st, 32)


def gnn_moe_kernel(nc, ins, out):
    S = Shapes(ins["x"], ins["src"], ins["L0_gnn_W"], ins["L0_ffn_W1"], ins["L1_ffn_w1"])
    NT, D, H = S.NT, S.D, S.H
    with ExitStack() as top:
        k = Core(nc, top)
        C, T = Namespace(), Namespace()
        C.ident = k.sb(top, "ident", [P, P])
        C.ones = k.sb(top, "ones", [P, P])
        C.iota = k.sb(top, "iota", [P, P])
        C.upper = k.sb(top, "upper", [P, P])
        C.lower = k.sb(top, "lower", [P, P])
        C.wiota = k.sb(top, "wiota", [P, NT])
        C.eps = k.sb(top, "eps", [P, 1])
        C.one = k.sb(top, "one", [P, 1])
        C.waug = k.sb(top, "w_aug", [P, 2, D + 2 * H])
        C.wfb = k.sb(top, "w_fb", [P, 2, D])
        C.wr = k.sb(top, "w_router", [P, 2, S.NX1])
        C.wg = k.sb(top, "w_gate", [P, 2, S.NX2])
        C.br = k.sb(top, "b_router", [P, S.NX1])
        C.bg = k.sb(top, "b_gate", [P, S.NX2])
        C.gat_bias = k.sb(top, "gat_bias", [P, D])
        C.gnn_bias = k.sb(top, "gnn_bias", [P, D])
        C.gamma = k.sb(top, "gamma", [P, D])
        C.beta = k.sb(top, "beta", [P, D])
        C.adst = k.sb(top, "a_dst", [P, NT, H])
        C.in_deg = k.sb(top, "in_deg", [P, NT])
        C.out_deg = k.sb(top, "out_deg", [P, NT])
        C.dinv = k.sb(top, "inv_root_degrees", [P, 2, NT])
        T.h = k.dram("h_rows", [NT * P, D])
        T.zb = k.dram("zb_rows", [NT * P, P])
        T.yf = [k.dram(f"forward_sums_{n}", [(NT + 1) * P, P]) for n in range(2 * SUB)]
        T.xb1 = k.dram("moe1_slots_in", [S.G1 * TOK + 2 * S.ROWS, D])
        T.xb2 = k.dram("moe2_slots_in", [S.G2 * TOK + S.ROWS, D])
        T.yb1 = k.dram("moe1_slots_out", [S.G1 * TOK, D])
        T.yb2 = k.dram("moe2_slots_out", [S.G2 * TOK, D])
        T.src_f = k.dram("edge_src_f", [S.E + STEP])
        T.src_hi = k.dram("edge_src_hi", [S.E], BF16)
        T.src_lo = k.dram("edge_src_lo", [S.E], BF16)
        T.terms = k.dram("edge_src_terms", [S.E, H])
        T.sd = k.dram("edge_src_dst", [S.E + STEP, 3])
        T.asrc = k.dram("a_src_rows", [NT * P, H])
        T.ea = k.dram("edge_terms", [S.E + STEP, S.EW])
        T.dst_f = k.dram("edge_dst", [S.E + STEP])
        T.steps = k.dram("step_table_dram", [2, P * S.KC], I32)

        setup(k, S, ins, C)
        edge_lists(k, S, ins, T)
        with ExitStack() as outer:
            C.asplit = k.sb(outer, "a_src_split", [P, 3, NT * H], BF16)
            C.farpat = k.sb(outer, "far_pattern", [NT, NT * H], BF16)
            with ExitStack() as ctx:
                x0 = k.sb(ctx, "x_in", [P, NT, D])
                pr = k.sb(ctx, "gat_products", [P, NT, D + 2 * H])
                project_nodes(k, S, C, "gat", x0, C.waug, D + 2 * H, pr, load_x=ins["x"])
                store_gat_tables(k, S, C, pr, T)
            with ExitStack() as ctx:
                source_terms(k, S, C, ins, T)
                ea = k.sb(ctx, "edge_terms_sb", [S.EP, S.ET, S.EW])
                edge_maxima(k, S, C, ins, T, ea)
        x_res = k.sb(top, "x_res", [P, NT, D])
        with ExitStack() as ctx:
            C.iota_n = k.sb(ctx, "iota_n", [P, NT * P])
            acc = k.sb(ctx, "gat_acc", [P, NT, D + H + 1])
            node_numbers(k, S, C, "gat")
            gat_edges(k, S, C, T, acc)
            gat_finish(k, S, C, acc, x_res, ins["x"])

        def moe(tag, rhs, bias, choices, X, capacity, affine, groups, F, func, xb, yb, w, guard):
            with ExitStack() as ctx:
                put = k.sb(ctx, f"{tag}_put_idx", [P, choices, NT], I32)
                get = k.sb(ctx, f"{tag}_get_idx", [P, choices, NT], I32)
                weight = k.sb(ctx, f"{tag}_weight", [P, choices, NT])
                gtab = k.sb(ctx, f"{tag}_group_expert", [1, groups], I32)
                with ExitStack() as inner:
                    xn = k.sb(inner, f"{tag}_xn_all", [P, NT, D])
                    logits = k.sb(inner, f"{tag}_raw_logits", [P, NT, X])
                    project_nodes(k, S, C, tag, x_res, rhs, X, logits, xn_all=xn, affine=affine)
                    route(k, S, C, tag, logits, bias, choices, X, capacity, put, get, weight, gtab)
                    put_rows(k, S, tag, xn, put, choices, xb)
                per = groups // X
                if capacity is None:
                    def expert_of(eng, t):
                        return eng.value_load(gtab[0:1, bass.ds(t, 1)], min_val=0, max_val=X - 1)
                else:
                    def expert_of(eng, t):
                        assert per == 2
                        return t // 2
                experts(k, S, C, tag, groups, F, func, xb, yb, *w, expert_of)
                take_rows(k, S, C, tag, get, choices, weight, yb, x_res, guard)

        moe("moe1", C.wr, C.br, 2, S.NX1, None, (C.gamma, C.beta), S.G1, S.F1, ACT.Gelu, T.xb1, T.yb1,
            (ins["L0_ffn_W1"], ins["L0_ffn_b1"], ins["L0_ffn_W2"], ins["L0_ffn_b2"]), False)
        with ExitStack() as ctx:
            z = k.sb(ctx, "gnn_z", [P, NT, D])
            project_nodes(k, S, C, "gnn", x_res, C.wfb, D, z)
            gnn_scale(k, S, C, T, z)
            acc = k.sb(ctx, "gnn_acc", [P, NT, P])
            with ExitStack() as inner:
                C.iota_n = k.sb(inner, "iota_n2", [P, NT * P])
                node_numbers(k, S, C, "gnn")
                gnn_edges(k, S, C, T, z, acc)
            gnn_finish(k, S, C, T, z, acc, x_res)
        k.recycle()
        moe("moe2", C.wg, C.bg, 1, S.NX2, S.CAP, None, S.G2, S.F2, ACT.Relu, T.xb2, T.yb2,
            (ins["L1_ffn_w1"], ins["L1_ffn_b1"], ins["L1_ffn_w2"], ins["L1_ffn_b2"]), True)
        store_rows(k, S, x_res, out)


def node_numbers(k, S, C, tag):
    io = k.sem(f"{tag}_node_numbers_ready")
    with ExitStack() as ctx:
        block = ctx.enter_context(k.nc.Block())

        @block.gpsimd
        def _(pool):
            pool.iota(C.iota_n[:, :], pattern=[[1, S.NT * P]], base=0, channel_multiplier=0,
                      allow_small_or_imprecise_dtypes=True).then_inc(io, 1)


_INS = ["x", "src", "dst", "L0_gnn_W", "L0_gnn_att_src", "L0_gnn_att_dst", "L0_gnn_bias", "L0_ffn_gamma",
        "L0_ffn_beta", "L0_ffn_Wr", "L0_ffn_br", "L0_ffn_W1", "L0_ffn_b1", "L0_ffn_W2", "L0_ffn_b2", "L1_gnn_W_f",
        "L1_gnn_W_b", "L1_gnn_bias_param", "L1_ffn_gate_w", "L1_ffn_gate_b", "L1_ffn_w1", "L1_ffn_b1", "L1_ffn_w2",
        "L1_ffn_b2"]


def kernel(**inputs):
    import numpy as np
    import concourse.bacc as bacc
    from concourse.bass_utils import run_bass_kernel_spmd

    nc = bacc.Bacc("TRN2", target_bir_lowering=False, num_devices=1)
    arrays, ins = {}, {}
    for name in _INS:
        a = np.ascontiguousarray(inputs[name])
        arrays["in_" + name] = a
        ins[name] = nc.dram_tensor("in_" + name, a.shape, mybir.dt.from_np(a.dtype), kind="ExternalInput").ap()
    shape = inputs["x"].shape
    out = nc.dram_tensor("out", shape, F32, kind="ExternalOutput").ap()
    gnn_moe_kernel(nc, ins, out)
    r = run_bass_kernel_spmd(nc, [arrays], core_ids=[0])
    return r.results[0]["out"]
```

```python
from contextlib import ExitStack

import concourse.bass as bass
from concourse import mybir

F32 = mybir.dt.float32
BF16 = mybir.dt.bfloat16
I32 = mybir.dt.int32
ALU = mybir.AluOpType
ACT = mybir.ActivationFunctionType
AX = mybir.AxisListType

P = 128
EPS = 1e-5
NEG_BIG = -1.0e38
FAR = -2.0 ** 100
CH = 16
ZCOLS = 1024
SUB = 2
STEP = SUB * P
POOL_SHARE = 51
GAT_DEPTH = 8
GNN_DEPTH = 4
BIG_DEPTH = max(GAT_DEPTH, GNN_DEPTH)
TOK1 = 256
TOK2 = 512
GROUP = 7


class Shapes:

    def __init__(self, x, src, gat_W, w1, w2):
        self.N, self.D = x.shape
        self.E = src.shape[0]
        self.H = gat_W.shape[1]
        self.HD = gat_W.shape[2]
        self.NT = -(-self.N // P)
        self.TAIL = self.N - (self.NT - 1) * P
        self.EP = next(p for p in range(P, 0, -1) if self.E % p == 0)
        self.ET = self.E // self.EP
        self.STEPS = -(-(-(-self.E // STEP) + self.NT) // BIG_DEPTH) * BIG_DEPTH
        self.NX1, self.F1 = w1.shape[0], w1.shape[2]
        self.NX2, self.F2 = w2.shape[0], w2.shape[2]
        self.CAP = -(-5 * self.N // (4 * self.NX2))
        self.CT = -(-self.CAP // P)
        self.KC = -(-self.STEPS // P)
        self.EW = 2 * self.H + 2
        self.G1 = (2 * self.N + self.NX1 * (TOK1 - 1)) // TOK1
        self.G2 = self.NX2 * -(-self.CAP // TOK2)
        self.ROWS = self.NT * P
        self.G1 += self.G1 % 2
        self.G2 += self.G2 % 2
        assert self.D == 2 * P and self.NT % GROUP == 0


class Core:

    def __init__(self, nc, ctx):
        self.nc, self.ctx = nc, ctx
        self.used = []

    def sem(self, name):
        self.used.append(self.nc.alloc_semaphore(name))
        return self.used[-1]

    def recycle(self):
        self.nc.clear_and_free_semaphores(self.used)
        self.nc.all_engine_barrier()
        self.used = []

    def sems(self, name, n):
        return [self.sem(f"{name}_{j}") for j in range(n)]

    def sb(self, ctx, name, shape, dt=F32):
        return ctx.enter_context(self.nc.sbuf_tensor(name, shape, dt))

    def ps(self, ctx, name, shape, dt=F32):
        return ctx.enter_context(self.nc.psum_tensor(name, shape, dt))

    def dram(self, name, shape, dt=F32):
        return self.nc.dram_tensor(name, shape, dt, kind="Internal").ap()


class Chain:

    def __init__(self, eng, sem, start=0):
        self.eng, self.sem, self.n = eng, sem, start

    def mark(self, ins):
        ins.then_inc(self.sem, 1)
        self.n = self.n + 1

    def link(self, ins):
        self.mark(ins)
        self.eng.wait_ge(self.sem, self.n)

    def join(self):
        self.eng.wait_ge(self.sem, self.n)


class RoundTable:

    def __init__(self, nc, engine, row, depth, lag, top):
        self.nc, self.engine, self.row, self.depth, self.lag, self.top = nc, engine, row, depth, lag, top
        self.at = {}

    def fetch(self, i):
        start = i * self.depth - self.lag
        skip = -start if isinstance(start, int) and start < 0 else 0
        n = self.depth - skip
        _, values = self.nc.values_load_multi_w_load_instructions(
            self.row[:, bass.ds(start + skip, n)], engines=(self.engine,), min_val=0, max_val=self.top,
            skip_runtime_bounds_check_because="the table's rows were clamped to their range when they were built")
        for j in range(n):
            self.at[(skip + j - self.lag) % self.depth] = values[j]


def staged(eng, steps, stages, depth, tables=()):
    def tick(i, j):
        for s, stage in stages:
            back, slot = (0, j - s) if j >= s else (1, j - s + depth)
            if not isinstance(i, int):
                stage(i - back, slot, i * depth + (j - s), False)
            elif 0 <= i * depth + j - s < steps:
                stage(i - back, slot, i * depth + j - s, i == back)

    def fetch(i):
        for table in tables:
            table.fetch(i)

    rounds = steps // depth
    for i in range(2):
        fetch(i)
        for j in range(depth):
            tick(i, j)
    with eng.Fori(2, rounds) as i:
        fetch(i)
        for j in range(depth):
            tick(i, j)
    if any(lag for lag, _ in stages):
        fetch(rounds)
    for j in range(max(lag for lag, _ in stages)):
        tick(rounds, j)


def rows_of(dram, S):
    full = dram[0:(S.NT - 1) * P, :].rearrange("(i p) d -> p i d", p=P)
    tail = dram[(S.NT - 1) * P:S.N, :]
    return full, tail



def setup(k, S, ins, C):
    nc = k.nc
    ld = k.sem("weights_loaded")
    io = k.sem("iota_written")
    ch = k.sem("setup_chain")
    tr = k.sem("wfb_transposed")
    with ExitStack() as ctx:
        att = k.sb(ctx, "att_rows", [P, 2, S.D])
        tmp = k.sb(ctx, "w_times_att", [P, S.D])
        wraw = k.sb(ctx, "wfb_raw", [P, 2, S.D])
        ii = k.sb(ctx, "iota_int", [P, P], I32)
        tri_i = k.sb(ctx, "diff_int", [P, P], I32)
        wi = k.sb(ctx, "window_int", [P, S.NT], I32)
        pt = k.ps(ctx, "wfb_ps", [P, 4, P])
        block = ctx.enter_context(nc.Block())

        def row(v):
            return v.rearrange("(a d) -> a d", a=1).partition_broadcast(P) if len(v.shape) == 1 else v

        loads = [
            (C.waug[:, :, 0:S.D], ins["L0_gnn_W"].rearrange("(c p) h d -> p c (h d)", p=P)),
            (att[:, 0, :], ins["L0_gnn_att_src"].rearrange("h d -> (h d)").partition_broadcast(P)),
            (att[:, 1, :], ins["L0_gnn_att_dst"].rearrange("h d -> (h d)").partition_broadcast(P)),
            (C.gat_bias[:, :], ins["L0_gnn_bias"].partition_broadcast(P)),
            (C.gamma[:, :], ins["L0_ffn_gamma"].partition_broadcast(P)),
            (C.beta[:, :], ins["L0_ffn_beta"].partition_broadcast(P)),
            (C.wr[:, :, :], ins["L0_ffn_Wr"].rearrange("(c p) n -> p c n", p=P)),
            (C.br[:, :], ins["L0_ffn_br"].partition_broadcast(P)),
            (wraw[:, 0, :], ins["L1_gnn_W_f"]),
            (wraw[:, 1, :], ins["L1_gnn_W_b"]),
            (C.gnn_bias[:, :], ins["L1_gnn_bias_param"].partition_broadcast(P)),
            (C.wg[:, :, :], ins["L1_ffn_gate_w"].rearrange("(c p) n -> p c n", p=P)),
            (C.bg[:, :], ins["L1_ffn_gate_b"].partition_broadcast(P)),
        ]

        @block.sync
        def _(sp):
            for out, src in loads:
                sp.dma_start(out, src).then_inc(ld, 16)

        @block.gpsimd
        def _(pool):
            pool.iota(ii[:, :], pattern=[[1, P]], base=0, channel_multiplier=0).then_inc(io, 1)
            pool.iota(tri_i[:, :], pattern=[[1, P]], base=0, channel_multiplier=-1).then_inc(io, 1)
            pool.iota(wi[:, :], pattern=[[P, S.NT]], base=0, channel_multiplier=1).then_inc(io, 1)

        @block.vector
        def _(dve):
            c = Chain(dve, ch)
            dve.wait_ge(io, 3)
            c.mark(dve.tensor_copy(C.iota[:, :], ii[:, :]))
            c.mark(dve.tensor_scalar(C.ident[:, :], tri_i[:, :], 0.0, None, ALU.is_equal))
            c.mark(dve.tensor_scalar(C.upper[:, :], tri_i[:, :], 0.0, None, ALU.is_gt))
            c.mark(dve.tensor_scalar(C.lower[:, :], tri_i[:, :], 0.0, None, ALU.is_lt))
            c.mark(dve.tensor_copy(C.wiota[:, :], wi[:, :]))
            c.mark(dve.memset(C.ones[:, :], 1.0))
            c.mark(dve.memset(C.eps[:, :], EPS))
            c.mark(dve.memset(C.one[:, :], 1.0))
            dve.wait_ge(ld, 16 * len(loads))
            for a in range(2):
                for t in range(2):
                    c.link(dve.tensor_tensor(tmp[:, :], C.waug[:, t, 0:S.D], att[:, a, :], ALU.mult))
                    c.link(dve.tensor_reduce(C.waug[:, t, S.D + a * S.H:S.D + (a + 1) * S.H],
                                             tmp[:, :].rearrange("p (h d) -> p h d", h=S.H), AX.X, ALU.add))
            dve.wait_ge(tr, 1)
            c.link(dve.tensor_copy(C.wfb[:, :, :], pt[:, :, :].rearrange("p (c a) n -> p c (a n)", c=2)))

        @block.tensor
        def _(pe):
            pe.wait_ge(ch, 7)
            pe.wait_ge(ld, 16 * len(loads))
            for t in range(2):
                for a in range(2):
                    last = pe.transpose(pt[:, 2 * t + a, :], wraw[:, a, t * P:(t + 1) * P], C.ident[:, :])
            last.then_inc(tr, 1)



def project_nodes(k, S, C, tag, x_res, rhs, n_out, out_sb, xn_all=None, load_x=None, affine=None):
    nc = k.nc
    passes = 2 if affine else 1
    per_row = 3 if affine else 1
    head = 2 * GROUP + 1
    before_last = (passes - 1) * (head + GROUP)
    ops = before_last + head + GROUP * per_row
    ln = k.sem(f"{tag}_ln_steps")
    rt = k.sem(f"{tag}_root_ready")
    xl = k.sem(f"{tag}_x_loaded")
    tp = k.sem(f"{tag}_rows_transposed")
    tc = k.sem(f"{tag}_transpose_copied")
    pj = k.sem(f"{tag}_product_ready")
    ev = k.sem(f"{tag}_product_copied")
    with ExitStack() as ctx:
        st = k.sb(ctx, f"{tag}_stats", [P, GROUP, 6])
        mv = k.sb(ctx, f"{tag}_meanvar", [P, 2, GROUP, 2])
        sd = k.sb(ctx, f"{tag}_std", [P, 2, GROUP])
        rs = k.sb(ctx, f"{tag}_rstd", [P, 2, GROUP])
        xn = k.sb(ctx, f"{tag}_xn", [P, GROUP, S.D])
        xm = k.sb(ctx, f"{tag}_xm", [P, GROUP, S.D]) if affine else None
        xT = k.sb(ctx, f"{tag}_xT", [P, GROUP, 2, P])
        pt = k.ps(ctx, f"{tag}_pt", [P, 2, 512])
        po = k.ps(ctx, f"{tag}_po", [P, 2, 512])
        block = ctx.enter_context(nc.Block())

        def tile_of(t, g, j):
            return t[:, bass.ds(g * GROUP + j, 1), :].rearrange("p a d -> p (a d)")

        @block.sync
        def _(sp):
            if load_x is None:
                return
            sp.wait_ge(xl, 1)
            full, tail = rows_of(load_x, S)
            for g in range(S.NT // GROUP):
                hi = min((g + 1) * GROUP, S.NT - 1)
                sp.dma_start(x_res[:, g * GROUP:hi, :], full[:, g * GROUP:hi, :]).then_inc(xl, 16)
            sp.dma_start(x_res[0:S.TAIL, S.NT - 1, :], tail).then_inc(xl, 16)

        @block.gpsimd
        def _(pool):
            if load_x is not None:
                pool.memset(x_res[:, S.NT - 1, :], 0.0).then_inc(xl, 1)

        @block.vector
        def _(dve):
            if load_x is not None:
                dve.wait_ge(xl, 1 + 16 * (S.NT // GROUP + 1))

            def group(g, first):
                for r in range(passes):
                    last = r == passes - 1
                    at = g * ops + r * (head + GROUP)
                    src = [xm[:, j, :] if r else tile_of(x_res, g, j) for j in range(GROUP)]
                    for j in range(GROUP):
                        if r:
                            dve.wait_ge(ln, at - GROUP + j + 1)
                        dve.bn_stats(st[:, j, :], src[j]).then_inc(ln, 1)
                    for j in range(GROUP):
                        dve.wait_ge(ln, at + (j + 1))
                        dve.nop(nofuse=True)
                        dve.bn_aggr(mv[:, r, j, :], st[:, j, :]).then_inc(ln, 1)
                    dve.wait_ge(rt, g * passes + (r + 1))
                    dve.reciprocal(rs[:, r, :], sd[:, r, :]).then_inc(ln, 1)
                    dve.wait_ge(ln, at + head)
                    for j in range(GROUP):
                        if last and not first:
                            dve.wait_ge(tp, g * GROUP + (j + 1 - GROUP))
                            if xn_all is not None:
                                dve.wait_ge(ev, g * GROUP + (j + 1 - GROUP))
                        dst = xn[:, j, :] if last else xm[:, j, :]
                        dve.tensor_scalar(dst, src[j], mv[:, r, j, 0:1], rs[:, r, j:j + 1],
                                          ALU.subtract, ALU.mult).then_inc(ln, 1)
                        if last and affine:
                            dve.wait_ge(ln, at + (head + 3 * j + 1))
                            dve.tensor_tensor(dst, dst, affine[0][:, :], ALU.mult).then_inc(ln, 1)
                            dve.wait_ge(ln, at + (head + 3 * j + 2))
                            dve.tensor_tensor(dst, dst, affine[1][:, :], ALU.add).then_inc(ln, 1)
            group(0, True)
            with dve.Fori(1, S.NT // GROUP) as g:
                group(g, False)

        @block.scalar
        def _(act):
            def root(g, r):
                act.wait_ge(ln, g * ops + (r * (head + GROUP) + 2 * GROUP))
                nc.scalar.activation(sd[:, r, :], mv[:, r, :, 1], ACT.Sqrt, bias=C.eps[:, 0:1]).then_inc(rt, 1)

            def copy_transposed(g, j):
                act.wait_ge(tp, g * GROUP + (j + 1))
                nc.scalar.copy(xT[:, j, :, :], pt[:, j % 2, 0:2 * P].rearrange("p (c n) -> p c n", c=2)).then_inc(tc, 1)

            def group(g, last):
                copy_transposed(g, 0)
                for j in range(GROUP):
                    if not last and (j - 1) % 3 == 0 and (j - 1) // 3 < passes:
                        root(g + 1, (j - 1) // 3)
                    if j + 1 < GROUP:
                        copy_transposed(g, j + 1)
                    if xn_all is not None:
                        nc.scalar.copy(tile_of(xn_all, g, j), xn[:, j, :])
                    act.wait_ge(pj, g * GROUP + (j + 1))
                    nc.scalar.copy(tile_of(out_sb, g, j), po[:, j % 2, 0:n_out]).then_inc(ev, 1)
            for r in range(passes):
                root(0, r)
            with act.Fori(0, S.NT // GROUP - 1) as g:
                group(g, False)
            group(S.NT // GROUP - 1, True)

        @block.tensor
        def _(pe):
            def group(g, first):
                def transpose(j):
                    pe.wait_ge(ln, g * ops + (before_last + head + (j + 1) * per_row))
                    if j >= 2:
                        pe.wait_ge(tc, g * GROUP + (j - 1))
                    for c in range(2):
                        last = pe.transpose(pt[:, j % 2, c * P:(c + 1) * P], xn[:, j, c * P:(c + 1) * P],
                                            C.ident[:, :])
                    last.then_inc(tp, 1)

                transpose(0)
                for j in range(GROUP):
                    if j + 1 < GROUP:
                        transpose(j + 1)
                    pe.wait_ge(tc, g * GROUP + (j + 1))
                    if j >= 2:
                        pe.wait_ge(ev, g * GROUP + (j - 1))
                    elif j == 0 and not first:
                        pe.wait_ge(ev, g * GROUP)
                    for c in range(2):
                        last = pe.matmul(po[:, j % 2, 0:n_out], xT[:, j, c, :], rhs[:, c, :],
                                         start=c == 0, stop=c == 1)
                    last.then_inc(pj, 1)
            group(0, True)
            with pe.Fori(1, S.NT // GROUP) as g:
                group(g, False)



def store_gat_tables(k, S, C, pr, T):
    nc = k.nc
    st = k.sem("gat_tables_stored")
    ca = k.sem("dst_terms_kept")
    with ExitStack() as ctx:
        rest = k.sb(ctx, "terms_rest", [P, S.NT, S.H])
        far = k.sb(ctx, "far", [S.NT, S.NT])
        block = ctx.enter_context(nc.Block())

        @block.sync
        def _(sp):
            for i in range(S.NT // GROUP):
                a, b = i * GROUP, (i + 1) * GROUP
                sp.dma_start(T.h[a * P:b * P, :].rearrange("(i p) d -> p i d", p=P), pr[:, a:b, 0:S.D]).then_inc(st, 16)
            sp.dma_start(T.asrc.rearrange("(i p) h -> p i h", p=P), pr[:, :, S.D:S.D + S.H]).then_inc(st, 16)
            sp.wait_ge(st, 16 * (S.NT // GROUP + 1))

        @block.vector
        def _(dve):
            c = Chain(dve, ca)
            c.mark(dve.tensor_copy(C.adst[:, :, :], pr[:, :, S.D + S.H:S.D + 2 * S.H]))
            part = C.asplit[:, :, :].rearrange("p s (n h) -> p s n h", h=S.H)
            c.link(dve.tensor_copy(part[:, 0, :, :], pr[:, :, S.D:S.D + S.H]))
            c.link(dve.tensor_tensor(rest[:, :, :], pr[:, :, S.D:S.D + S.H], part[:, 0, :, :], ALU.subtract))
            c.link(dve.tensor_copy(part[:, 1, :, :], rest[:, :, :]))
            c.link(dve.tensor_tensor(rest[:, :, :], rest[:, :, :], part[:, 1, :, :], ALU.subtract))
            c.link(dve.tensor_copy(part[:, 2, :, :], rest[:, :, :]))
            c.link(dve.tensor_scalar(far[:, :], C.iota[0:S.NT, 0:S.NT], C.wiota[0:S.NT, 0:1], FAR,
                                     ALU.is_equal, ALU.mult))
            c.link(dve.tensor_copy(C.farpat[:, :].rearrange("p (n h) -> p n h", h=S.H),
                                   far[:, :].unsqueeze(2).to_broadcast([S.NT, S.NT, S.H])))


def edge_lists(k, S, ins, T):
    nc = k.nc
    EP, ET = S.EP, S.ET
    ld = k.sem("edge_lists_loaded")
    ch = k.sem("edge_lists_chain")
    tl = k.sem("edge_tails_ready")
    st = k.sem("edge_lists_stored")
    with ExitStack() as ctx:
        si = k.sb(ctx, "src_int", [EP, ET], I32)
        di = k.sb(ctx, "dst_int", [EP, ET], I32)
        hi_i = k.sb(ctx, "src_hi_int", [EP, ET], I32)
        sf = k.sb(ctx, "src_float", [EP, ET])
        df = k.sb(ctx, "dst_float", [EP, ET])
        hi = k.sb(ctx, "src_hi", [EP, ET], BF16)
        lo = k.sb(ctx, "src_lo", [EP, ET], BF16)
        sd = k.sb(ctx, "src_dst_rows", [EP, ET, 3])
        tz = k.sb(ctx, "tail_src", [P, SUB])
        tm = k.sb(ctx, "tail_dst", [P, SUB])
        tsd = k.sb(ctx, "tail_src_dst", [P, SUB, 3])
        block = ctx.enter_context(nc.Block())
        lists = [(T.src_f, sf), (T.dst_f, df), (T.src_hi, hi), (T.src_lo, lo)]

        @block.sync
        def _(sp):
            sp.dma_start(si[:, :], ins["src"].rearrange("(p t) -> p t", t=ET)).then_inc(ld, 16)
            sp.dma_start(di[:, :], ins["dst"].rearrange("(p t) -> p t", t=ET)).then_inc(ld, 16)
            sp.wait_ge(tl, 4)
            sp.dma_start(T.src_f[S.E:S.E + STEP].rearrange("(p j) -> p j", j=SUB), tz[:, :]).then_inc(st, 16)
            sp.dma_start(T.dst_f[S.E:S.E + STEP].rearrange("(p j) -> p j", j=SUB), tm[:, :]).then_inc(st, 16)
            sp.dma_start(T.sd[S.E:S.E + STEP, :].rearrange("(p j) c -> p j c", j=SUB), tsd[:, :, :]).then_inc(st, 16)
            sp.wait_ge(ch, 8)
            for dram, own in lists:
                sp.dma_start(dram[0:S.E].rearrange("(p t) -> p t", t=ET), own[:, :]).then_inc(st, 16)
            sp.dma_start(T.sd[0:S.E, :].rearrange("(p t) c -> p (t c)", t=ET),
                         sd[:, :, :].rearrange("p t c -> p (t c)")).then_inc(st, 16)
            sp.wait_ge(st, 16 * 8)

        @block.gpsimd
        def _(pool):
            pool.memset(tz[:, :], 0.0).then_inc(tl, 1)
            pool.memset(tm[:, :], -1.0).then_inc(tl, 1)
            pool.memset(tsd[:, :, :], 0.0).then_inc(tl, 1)
            pool.wait_ge(tl, 3)
            pool.memset(tsd[:, :, 1], -1.0).then_inc(tl, 1)

        @block.vector
        def _(dve):
            c = Chain(dve, ch)
            dve.wait_ge(ld, 32)
            c.link(dve.tensor_scalar(hi_i[:, :], si[:, :], P.bit_length() - 1, None, ALU.arith_shift_right))
            c.mark(dve.tensor_copy(hi[:, :], hi_i[:, :]))
            c.mark(dve.scalar_tensor_tensor(out=lo[:, :], in0=hi_i[:, :], scalar=-float(P), in1=si[:, :],
                                            op0=ALU.mult, op1=ALU.add))
            c.mark(dve.tensor_copy(sf[:, :], si[:, :]))
            c.mark(dve.tensor_copy(df[:, :], di[:, :]))
            c.mark(dve.tensor_copy(sd[:, :, 0], si[:, :]))
            c.mark(dve.tensor_copy(sd[:, :, 1], di[:, :]))
            c.mark(dve.tensor_copy(sd[:, :, 2].bitcast(I32), si[:, :]))


def source_terms(k, S, C, ins, T):
    nc = k.nc
    NT, H, EP, ET = S.NT, S.H, S.EP, S.ET
    CE = P * CH
    full = S.E // CE
    rest = S.E - full * CE
    NPOOL = full * POOL_SHARE // 100 // 2 * 2
    NPE = (full - NPOOL) // 2 * 2
    extra = list(range(NPE + NPOOL, full)) + ([full] if rest else [])
    assert rest % CH == 0 and ET % (2 * CH) == 0
    counts = ET // CH
    BANKS = 4
    il = k.sems("src_chunk_loaded", 2)
    ga = k.sems("terms_gathered", 2)
    gs = k.sems("gathered_terms_stored", 2)
    rl = k.sems("src_rows_loaded", 2)
    oh = k.sem("pick_onehots_ready")
    pk = k.sem("candidates_ready")
    rd = k.sem("candidates_reduced")
    ps = k.sems("picked_terms_stored", 2)
    cl = k.sem("count_lists_loaded")
    co = k.sem("count_onehots_ready")
    cu = k.sem("count_onehots_used")
    ch = k.sem("count_chain")
    with ExitStack() as ctx:
        idx = k.sb(ctx, "src_chunk", [P, 2, CH], I32)
        rows = k.sb(ctx, "gathered_terms", [P, 2, CH * H])
        lo_r = k.sb(ctx, "src_lo_row", [P, 2, CE], BF16)
        hi_r = k.sb(ctx, "src_hi_row", [NT, 2, CE], BF16)
        olo = k.sb(ctx, "pick_lo", [P, 2, CE], BF16)
        nhi = k.sb(ctx, "pick_not_hi", [NT, 2, CE], BF16)
        res = k.sb(ctx, "picked_terms", [P, 2, CH, H])
        iob = k.sb(ctx, "iota_bf", [P, P], BF16)
        hi = k.sb(ctx, "count_hi", [EP, ET], BF16)
        lo = k.sb(ctx, "count_lo", [EP, ET], BF16)
        ohl = k.sb(ctx, "count_onehot_lo", [EP, 2, CH, P], BF16)
        ohh = k.sb(ctx, "count_onehot_hi", [EP, 2, CH, NT], BF16)
        zz = k.sb(ctx, "zeros_bf", [EP, P], BF16)
        pc = k.ps(ctx, "candidates_ps", [P, BANKS, 512])
        pd = k.ps(ctx, "source_counts", [P, NT])
        block = ctx.enter_context(nc.Block())
        src = ins["src"]

        def edges(c, n=1):
            return bass.ds(c * CE, CE) if n == 1 else None

        def put(c):
            return T.terms[bass.ds(c * CE, CE), :].rearrange("(p t) h -> p (t h)", t=CH)

        @block.sync
        def _(sp):
            sp.dma_start(hi[:, :], T.src_hi[0:S.E].rearrange("(p t) -> p t", t=ET)).then_inc(cl, 16)
            sp.dma_start(lo[:, :], T.src_lo[0:S.E].rearrange("(p t) -> p t", t=ET)).then_inc(cl, 16)

            def load(i, b, t, first):
                if not first:
                    sp.wait_ge(oh, t - 1)
                    sp.nop(nofuse=True)
                sp.dma_start(lo_r[:, b, :], T.src_lo[edges(t)].partition_broadcast(P)).then_inc(rl[b], 16)
                sp.dma_start(hi_r[:, b, :], T.src_hi[edges(t)].partition_broadcast(NT)).then_inc(rl[b], 16)

            def store(i, b, t, first):
                sp.wait_ge(rd, t * CH + CH)
                sp.nop(nofuse=True)
                sp.dma_start(put(t), res[:, b, :, :].rearrange("p t h -> p (t h)")).then_inc(ps[b], 16)
            staged(sp, NPE, [(0, load), (2, store)], 2)
            for b in range(2):
                sp.wait_ge(ps[b], 16 * (NPE // 2))

        @block.scalar
        def _(act):
            def load(i, b, t, first):
                if not first:
                    act.wait_ge(ga[b], i * (16 * CH))
                    act.nop(nofuse=True)
                act.dma_start(idx[:, b, :], src[bass.ds((t + NPE) * CE, CE)].rearrange("(p t) -> p t", t=CH))\
                   .then_inc(il[b], 16)

            def store(i, b, t, first):
                act.wait_ge(ga[b], i * (16 * CH) + 16 * CH)
                act.nop(nofuse=True)
                act.dma_start(put(t + NPE), rows[:, b, :]).then_inc(gs[b], 16)
            staged(act, NPOOL, [(0, load), (1, store)], 2)
            n = NPOOL // 2
            for x, c in enumerate(extra):
                b, r = x % 2, n + x // 2
                parts = P if c < full else rest // CH
                act.wait_ge(ga[b], 16 * CH * r)
                act.dma_start(idx[0:parts, b, :],
                              src[c * CE:c * CE + parts * CH].rearrange("(p t) -> p t", t=CH)).then_inc(il[b], 16)
                act.wait_ge(ga[b], 16 * CH * (r + 1))
                act.dma_start(T.terms[c * CE:c * CE + parts * CH, :].rearrange("(p t) h -> p (t h)", t=CH),
                              rows[0:parts, b, :]).then_inc(gs[b], 16)
            for b in range(2):
                act.wait_ge(gs[b], 16 * (n + len(range(b, len(extra), 2))))

        @block.gpsimd
        def _(pool):
            def fetch(b, parts):
                for t in range(CH):
                    pool.indirect_dma_start(
                        out=rows[0:parts, b, t * H:(t + 1) * H], out_offset=None, in_=T.asrc[:, :],
                        in_offset=bass.IndirectOffsetOnAxis(ap=idx[0:parts, b, t:t + 1], axis=0)).then_inc(ga[b], 16)

            def gather(i, b, t, first):
                pool.wait_ge(il[b], i * 16 + 16)
                pool.nop(nofuse=True)
                if not first:
                    pool.wait_ge(gs[b], i * 16)
                    pool.nop(nofuse=True)
                fetch(b, P)
            staged(pool, NPOOL, [(0, gather)], 2)
            for x, c in enumerate(extra):
                b, r = x % 2, NPOOL // 2 + x // 2
                pool.wait_ge(il[b], 16 * (r + 1))
                pool.wait_ge(gs[b], 16 * r)
                fetch(b, P if c < full else rest // CH)

        @block.vector
        def _(dve):
            c = Chain(dve, ch)
            c.mark(dve.memset(zz[:, :], 0.0))
            c.link(dve.tensor_copy(iob[:, :], C.iota[:, :]))

            def onehots(i, b, t, first):
                dve.wait_ge(rl[b], i * 32 + 32)
                if not first:
                    dve.wait_ge(pk, (t - 1) * CH)
                dve.tensor_scalar(olo[:, b, :], lo_r[:, b, :], C.wiota[:, 0:1], None, ALU.is_equal)
                dve.tensor_scalar(nhi[:, b, :], hi_r[:, b, :], C.wiota[0:NT, 0:1], None, ALU.not_equal).then_inc(oh, 1)

            def reduce(i, b, t, first):
                if not first:
                    dve.wait_ge(ps[b], i * 16)
                for j in range(CH):
                    dve.wait_ge(pk, t * CH + (j + 1))
                    dve.tensor_reduce(res[:, b, j, :], pc[:, j % BANKS, 0:NT * H].rearrange("p (n h) -> p h n", h=H),
                                      AX.X, ALU.max).then_inc(rd, 1)
            staged(dve, NPE, [(0, onehots), (1, reduce)], 2)

            def count(i, b, t, first):
                if not first:
                    dve.wait_ge(cu, t - 1)
                at = bass.ds(t * CH, CH)
                dve.tensor_tensor(ohl[:, b, :, :], lo[:, at].unsqueeze(2).to_broadcast([EP, CH, P]),
                                  iob[0:EP, :].unsqueeze(1).to_broadcast([EP, CH, P]), ALU.is_equal)
                dve.tensor_tensor(ohh[:, b, :, :], hi[:, at].unsqueeze(2).to_broadcast([EP, CH, NT]),
                                  iob[0:EP, 0:NT].unsqueeze(1).to_broadcast([EP, CH, NT]), ALU.is_equal).then_inc(co, 1)
            dve.wait_ge(cl, 32)
            staged(dve, counts, [(0, count)], 2)
            dve.wait_ge(cu, counts + 1)
            dve.tensor_scalar(C.in_deg[:, :], pd[:, :], 1.0, None, ALU.add).then_inc(ch, 1)

        @block.tensor
        def _(pe):
            def pick(i, b, t, first):
                pe.wait_ge(oh, t + 1)
                for j in range(CH):
                    if not (first and b == 0 and j < BANKS):
                        pe.wait_ge(rd, t * CH + (j + 1 - BANKS))
                    out = pc[:, j % BANKS, 0:NT * H]
                    for s in range(3):
                        pe.matmul(out, olo[:, b, j:CE:CH], C.asplit[:, s, :], start=s == 0, stop=False)
                    pe.matmul(out, nhi[:, b, j:CE:CH], C.farpat[:, :], start=False, stop=True).then_inc(pk, 1)
            staged(pe, NPE, [(0, pick)], 2)

            pe.wait_ge(ch, 1)
            pe.matmul(pd[:, :], zz[:, :], zz[:, 0:NT], start=True, stop=False, skip_group_check=True)

            def count(i, b, t, first):
                pe.wait_ge(co, t + 1)
                for j in range(CH):
                    last = pe.matmul(pd[:, :], ohl[:, b, j, :], ohh[:, b, j, :], start=False, stop=False,
                                     skip_group_check=True)
                last.then_inc(cu, 1)
            staged(pe, counts, [(0, count)], 2)
            pe.matmul(pd[:, :], zz[:, :], zz[:, 0:NT], start=False, stop=True, skip_group_check=True).then_inc(cu, 1)


def zero_fill(eng, bufs, zf, sem):
    n = 0
    for buf in bufs:
        flat = buf.rearrange("(p r) d -> p (r d)", p=P)
        for at in range(0, flat.shape[1], ZCOLS):
            w = min(ZCOLS, flat.shape[1] - at)
            eng.dma_start(flat[:, at:at + w], zf[:, 0:w]).then_inc(sem, 16)
            n += 16
    return n


def edge_maxima(k, S, C, ins, T, ea):
    nc = k.nc
    EP, ET, H, NT = S.EP, S.ET, S.H, S.NT
    KC = S.KC
    ld = k.sem("dst_loaded")
    ch = k.sem("maxima_chain")
    tr = k.sem("totals_ready")
    tq = k.sem("totals_transposed")
    cr = k.sem("carry_ready")
    cb = k.sem("carry_back")
    cn = k.sem("window_counts_ready")
    cs = k.sem("window_counts_summed")
    sm = k.sem("term_tails_ready")
    fl = k.sem("dst_edge_column_blank")
    el = k.sem("terms_loaded")
    zm = k.sem("zeros_ready")
    zs = k.sem("buffers_zeroed")
    tb = k.sem("step_table_ready")
    mx = k.sem("maxima_ready")
    st = k.sem("edge_arrays_saved")
    io = k.sem("step_numbers")
    with ExitStack() as ctx:
        di = k.sb(ctx, "dst_int_wide", [EP, 1 + ET + 1], I32)
        sf = k.sb(ctx, "dst_float_list", [EP, ET])
        fs = k.sb(ctx, "starts_flag", [EP, ET])
        fe = k.sb(ctx, "ends_flag", [EP, ET])
        run = k.sb(ctx, "running", [EP, ET])
        fmin = k.sb(ctx, "flag_min", [EP, 2])
        tot = k.sb(ctx, "totals", [EP, 2, 2 * H])
        totT = k.sb(ctx, "totals_T", [H, 2, 2, EP])
        carT = k.sb(ctx, "carry_T", [H, 2, EP + 1])
        car = k.sb(ctx, "carry", [EP, 2, H])
        cnt = k.sb(ctx, "below_count", [P, NT])
        ends = k.sb(ctx, "window_end", [P, NT])
        wst = k.sb(ctx, "window_start", [P, NT])
        wn = k.sb(ctx, "window_steps", [P, NT])
        wn_i = k.sb(ctx, "window_steps_int", [P, NT], I32)
        kend = k.sb(ctx, "window_last_step", [P, NT])
        wbase = k.sb(ctx, "window_base", [P, NT])
        zero = k.sb(ctx, "window_zero", [P, NT])
        kg_i = k.sb(ctx, "step_number_int", [P, KC], I32)
        kg = k.sb(ctx, "step_number", [P, KC])
        cmp = k.sb(ctx, "step_compare", [P, KC, NT])
        ww = k.sb(ctx, "step_window", [P, KC])
        bb = k.sb(ctx, "step_base", [P, KC])
        tab = k.sb(ctx, "step_table", [P, 2, KC], I32)
        tail = k.sb(ctx, "tail_edges", [P, SUB * S.EW])
        si = k.sb(ctx, "src_int_list", [EP, ET], I32)
        zf = k.sb(ctx, "zeros_f", [P, ZCOLS])
        ptot = k.ps(ctx, "totals_ps", [H, 2, P])
        pcar = k.ps(ctx, "carry_ps", [EP, H])
        pc = k.ps(ctx, "window_ps", [P, NT])
        block = ctx.enter_context(nc.Block())
        dst = ins["dst"]
        dst_pt = dst.rearrange("(p t) -> p t", t=ET)

        @block.sync
        def _(sp):
            sp.dma_start(di[:, 1:1 + ET], dst_pt).then_inc(ld, 16)
            sp.dma_start(si[:, :], ins["src"].rearrange("(p t) -> p t", t=ET)).then_inc(ld, 16)
            sp.wait_ge(fl, 2)
            sp.dma_start(di[1:EP, 0:1], dst_pt[0:EP - 1, ET - 1:ET], allow_slow_non_contiguous=True).then_inc(ld, 16)
            sp.dma_start(di[0:EP - 1, 1 + ET:2 + ET], dst_pt[1:EP, 0:1], allow_slow_non_contiguous=True).then_inc(ld, 16)
            terms = T.terms.rearrange("(p t) h -> p t h", t=ET)
            QUARTER = ET // 4
            for q in range(0, ET, QUARTER):
                sp.dma_start(ea[:, q:q + QUARTER, 0:H], terms[:, q:q + QUARTER, :]).then_inc(el, 16)
            sp.wait_ge(sm, 2)
            sp.dma_start(T.ea[S.E:S.E + STEP, :].rearrange("(p j) h -> p (j h)", j=SUB), tail[:, :]).then_inc(st, 16)
            sp.wait_ge(tb, 1)
            for a in range(2):
                sp.dma_start(T.steps[a, :].rearrange("(p c) -> p c", c=KC), tab[:, a, :]).then_inc(st, 16)
            sp.wait_ge(mx, 1)
            sp.dma_start(T.ea[0:S.E, :].rearrange("(p t) h -> p (t h)", t=ET),
                         ea[:, :, :].rearrange("p t h -> p (t h)")).then_inc(st, 16)
            sp.wait_ge(st, 16 * 4)

        @block.gpsimd
        def _(pool):
            pool.memset(tail[:, :], 0.0).then_inc(sm, 1)
            pool.wait_ge(sm, 1)
            for j in range(SUB):
                last = pool.memset(tail[:, j * S.EW + 2 * H:j * S.EW + 2 * H + 1], -1.0)
            last.then_inc(sm, 1)
            pool.memset(zf[:, :], 0.0).then_inc(zm, 1)
            pool.iota(kg_i[:, :], pattern=[[1, KC]], base=0, channel_multiplier=KC).then_inc(io, 1)

        @block.vector
        def _(dve):
            c = Chain(dve, ch)
            dve.memset(di[:, 0:1], -1).then_inc(fl, 1)
            dve.memset(di[:, 1 + ET:2 + ET], -1).then_inc(fl, 1)
            c.mark(dve.memset(carT[:, :, :], NEG_BIG))
            c.mark(dve.memset(zero[:, :], 0.0))
            c.link(dve.memset(cnt[:, :], 0.0))
            dve.wait_ge(ld, 64)
            c.mark(dve.tensor_tensor(fs[:, :], di[:, 1:1 + ET], di[:, 0:ET], ALU.not_equal))
            c.mark(dve.tensor_tensor(fe[:, :], di[:, 1:1 + ET], di[:, 2:2 + ET], ALU.not_equal))
            c.link(dve.tensor_copy(sf[:, :], di[:, 1:1 + ET]))
            c.mark(dve.tensor_copy(ea[:, :, 2 * H + 1].bitcast(I32), si[:, :]))
            c.mark(dve.tensor_copy(ea[:, :, 2 * H], sf[:, :]))
            c.mark(dve.tensor_scalar(fs[:, :], fs[:, :], NEG_BIG, None, ALU.mult))
            c.link(dve.tensor_scalar(fe[:, :], fe[:, :], NEG_BIG, None, ALU.mult))
            for w in range(NT):
                c.link(dve.tensor_scalar(run[:, :], sf[:, :], float((w + 1) * P), 0.0, ALU.is_lt, ALU.add,
                                         accum_out=cnt[0:EP, w:w + 1]))
            dve.nop(nofuse=True).then_inc(cn, 1)
            c.mark(dve.tensor_reduce(fmin[:, 0:1], fs[:, :], AX.X, ALU.min))
            c.link(dve.tensor_reduce(fmin[:, 1:2], fe[:, :], AX.X, ALU.min))
            for a in range(2):
                c.link(dve.tensor_copy(tot[:, a, H:2 * H], fmin[:, a:a + 1].to_broadcast([EP, H])))
            dve.wait_ge(el, 16 * 4)
            for a in range(2):
                forward = a == 0

                def scan(h, out, initial):
                    data = ea[:, :, h] if forward else ea[:, ::-1, H + h]
                    flag = fs[:, :] if forward else fe[:, ::-1]
                    c.link(dve.tensor_tensor_scan(out, flag, data, initial, ALU.add, ALU.max))
                for h in range(H):
                    scan(h, run[:, :], NEG_BIG)
                    c.link(dve.tensor_copy(tot[:, a, h:h + 1], run[:, ET - 1:ET]))
                dve.nop(nofuse=True).then_inc(tr, 1)
                dve.wait_ge(tq, a + 1)
                c.link(dve.tensor_copy(totT[:, a, :, :], ptot[:, :, 0:EP]))
                if forward:
                    c.link(dve.tensor_tensor_scan(carT[:, a, 1:EP + 1], totT[:, a, 1, :], totT[:, a, 0, :], NEG_BIG,
                                                  ALU.add, ALU.max))
                else:
                    c.link(dve.tensor_tensor_scan(carT[:, a, 0:EP][:, ::-1], totT[:, a, 1, ::-1],
                                                  totT[:, a, 0, ::-1], NEG_BIG, ALU.add, ALU.max))
                dve.nop(nofuse=True).then_inc(cr, 1)
                dve.wait_ge(cb, a + 1)
                c.link(dve.tensor_copy(car[:, a, :], pcar[:, :]))
                for h in range(H):
                    scan(h, ea[:, :, H + h] if forward else ea[:, ::-1, H + h], car[:, a, h:h + 1])
            dve.nop(nofuse=True).then_inc(mx, 1)
            dve.wait_ge(cs, 1)
            dve.wait_ge(io, 1)
            c.link(dve.tensor_copy(kg[:, :], kg_i[:, :]))
            c.link(dve.memset(wst[:, 0:1], 0.0))
            c.link(dve.tensor_copy(ends[:, :], pc[:, :]))
            c.link(dve.tensor_copy(wst[:, 1:NT], ends[:, 0:NT - 1]))
            c.link(dve.tensor_tensor(wn[:, :], ends[:, :], wst[:, :], ALU.subtract))
            c.link(dve.tensor_scalar(wn_i[:, :], wn[:, :], float(STEP - 1), None, ALU.add))
            c.link(dve.tensor_scalar(wn_i[:, :], wn_i[:, :], STEP.bit_length() - 1, None, ALU.arith_shift_right))
            c.link(dve.tensor_copy(wn[:, :], wn_i[:, :]))
            c.link(dve.tensor_tensor_scan(kend[:, :], zero[:, :], wn[:, :], 0.0, ALU.add, ALU.add))
            c.link(dve.tensor_tensor(wbase[:, :], kend[:, :], wn[:, :], ALU.subtract))
            c.link(dve.scalar_tensor_tensor(out=wbase[:, :], in0=wbase[:, :], scalar=-float(STEP), in1=wst[:, :],
                                            op0=ALU.mult, op1=ALU.add))
            grid = [P, KC, NT]
            c.link(dve.tensor_tensor(cmp[:, :, :], kend[:, :].unsqueeze(1).to_broadcast(grid),
                                     kg[:, :].unsqueeze(2).to_broadcast(grid), ALU.is_le))
            c.link(dve.tensor_reduce(ww[:, :], cmp[:, :, :], AX.X, ALU.add))
            c.link(dve.tensor_tensor(cmp[:, :, :], C.iota[:, 0:NT].unsqueeze(1).to_broadcast(grid),
                                     ww[:, :].unsqueeze(2).to_broadcast(grid), ALU.is_equal))
            c.link(dve.tensor_tensor(cmp[:, :, :], cmp[:, :, :], wbase[:, :].unsqueeze(1).to_broadcast(grid),
                                     ALU.mult))
            c.link(dve.tensor_reduce(bb[:, :], cmp[:, :, :], AX.X, ALU.add))
            c.link(dve.scalar_tensor_tensor(out=bb[:, :], in0=kg[:, :], scalar=float(STEP), in1=bb[:, :],
                                            op0=ALU.mult, op1=ALU.add))
            c.link(dve.tensor_scalar(tab[:, 0, :], ww[:, :], float(NT - 1), None, ALU.min))
            c.link(dve.tensor_scalar(tab[:, 1, :], bb[:, :], float(S.E), None, ALU.min))
            dve.nop(nofuse=True).then_inc(tb, 1)

        @block.scalar
        def _(act):
            act.wait_ge(zm, 1)
            n = zero_fill(act, [T.xb1[0:S.G1 * TOK1, :]], zf, zs)
            act.wait_ge(zs, n)

        @block.tensor
        def _(pe):
            pe.wait_ge(cn, 1)
            pe.matmul(pc[:, :], C.ones[:, :], cnt[:, :], start=True, stop=True).then_inc(cs, 1)
            for a in range(2):
                pe.wait_ge(tr, a + 1)
                pe.transpose(ptot[:, 0, 0:EP], tot[:, a, 0:H], C.ident[0:EP, 0:EP])
                pe.transpose(ptot[:, 1, 0:EP], tot[:, a, H:2 * H], C.ident[0:EP, 0:EP]).then_inc(tq, 1)
                pe.wait_ge(cr, a + 1)
                pe.transpose(pcar[:, :], carT[:, a, a:a + EP], C.ident[0:H, 0:H]).then_inc(cb, 1)



def load_step_table(k, S, sp, T, tab, sem):
    sp.dma_start(tab[0:1, :, :], T.steps.rearrange("a (b k) -> b a k", b=1)).then_inc(sem, 16)


def step_windows(k, S, C, T, tag, out, own):
    nc = k.nc
    ld = k.sem(f"{tag}_windows_loaded")
    dn = k.sem(f"{tag}_windows_ready")
    with ExitStack() as ctx:
        wi = k.sb(ctx, f"{tag}_windows_int", [P, P * S.KC], I32)
        block = ctx.enter_context(nc.Block())

        @block.sync
        def _(sp):
            sp.dma_start(wi[:, :], T.steps[0, :].partition_broadcast(P)).then_inc(ld, 16)

        @block.vector
        def _(dve):
            dve.wait_ge(ld, 16)
            if own:
                dve.tensor_scalar(out[:, :], wi[:, :], float(P), C.wiota[:, 0:1], ALU.mult, ALU.add).then_inc(dn, 1)
            else:
                dve.tensor_scalar(out[:, :], wi[:, :], float(P), None, ALU.mult).then_inc(dn, 1)


def gat_edges(k, S, C, T, acc, node):
    nc = k.nc
    DEPTH = GAT_DEPTH
    ADD_LAG = 4
    H, HD, D, W = S.H, S.HD, S.D, S.D + S.H + 1
    tl = k.sem("gat_table_loaded")
    ld = k.sems("gat_step_loaded", DEPTH)
    ga = k.sems("gat_rows_gathered", DEPTH)
    lc = k.sem("gat_local_dst_ready")
    oh = k.sem("gat_onehot_ready")
    ad = k.sem("gat_dst_terms_ready")
    df = k.sem("gat_difference_ready")
    ch = k.sem("gat_exponent_chain")
    ex = k.sem("gat_exp_ready")
    ms = k.sem("gat_messages_ready")
    sc = k.sem("gat_step_summed")
    dn = k.sem("gat_step_done")
    cl = k.sem("gat_acc_clear")
    with ExitStack() as ctx:
        tab = k.sb(ctx, "gat_table", [1, 2, P * S.KC], I32)
        ed = k.sb(ctx, "gat_terms", [P, DEPTH, SUB, S.EW])
        row = k.sb(ctx, "gat_dst_row", [P, DEPTH, STEP])
        g = k.sb(ctx, "gat_rows", [P, DEPTH, SUB, D])
        oT = k.sb(ctx, "gat_onehot_T", [P, DEPTH, SUB, P])
        o = k.sb(ctx, "gat_onehot", [P, DEPTH, SUB, P])
        local = k.sb(ctx, "gat_local_dst", [P, DEPTH, SUB])
        z = k.sb(ctx, "gat_z", [P, DEPTH, SUB, 2 * H])
        y = k.sb(ctx, "gat_leaky", [P, DEPTH, SUB, 2 * H])
        q = k.sb(ctx, "gat_exponent", [P, DEPTH, SUB, H])
        m = k.sb(ctx, "gat_messages", [P, DEPTH, SUB, W])
        pa = k.ps(ctx, "gat_dst_ps", [P, 2, 512])
        po = k.ps(ctx, "gat_sum_ps", [P, 2, 512])
        warm = k.ps(ctx, "gat_warm_ps", [P, 512])
        block = ctx.enter_context(nc.Block())

        @block.sync
        def _(sp):
            load_step_table(k, S, sp, T, tab, tl)
            sp.wait_ge(tl, 16)

            bases = RoundTable(nc, mybir.EngineType.SP, tab[0:1, 1, :], DEPTH, 0, S.E)

            def load(i, b, t, first):
                base = bases.at[b]
                if not first:
                    sp.wait_ge(dn, t - (DEPTH - 1))
                    sp.nop(nofuse=True)
                sp.dma_start(ed[:, b, :, :], T.ea[bass.ds(base, STEP), :].rearrange("(p j) h -> p j h", j=SUB)).then_inc(ld[b], 16)
                sp.dma_start(row[:, b, :], T.dst_f[bass.ds(base, STEP)].partition_broadcast(P)).then_inc(ld[b], 16)
            staged(sp, S.STEPS, [(0, load)], DEPTH, [bases])

        @block.gpsimd
        def _(pool):
            def gather(i, b, t, first):
                pool.wait_ge(ld[b], i * 32 + 32)
                pool.nop(nofuse=True)
                for j in range(SUB):
                    pool.indirect_dma_start(
                        out=g[:, b, j, :], out_offset=None, in_=T.h[:, :],
                        in_offset=bass.IndirectOffsetOnAxis(ap=ed[:, b, j, 2 * H + 1:2 * H + 2].bitcast(I32), axis=0)).then_inc(ga[b], 16)
            staged(pool, S.STEPS, [(0, gather)], DEPTH)

        @block.scalar
        def _(act):
            def onehots(i, b, t, first):
                act.wait_ge(lc, t + 1)
                nc.scalar.activation(oT[:, b, :, :], row[:, b, :].rearrange("p (e j) -> p j e", j=SUB), ACT.Abs,
                                     bias=node[:, bass.ds(t, 1)], scale=-1.0)
                for j in range(SUB):
                    last = nc.scalar.activation(o[:, b, j, :], C.iota[:, :], ACT.Abs,
                                                bias=local[:, b, j:j + 1], scale=-1.0)
                last.then_inc(df, 1)
                act.wait_ge(df, t + 1)
                nc.scalar.activation(oT[:, b, :, :], oT[:, b, :, :], ACT.Relu, bias=C.one[:, 0:1],
                                     scale=-1.0).then_inc(oh, 1)
                nc.scalar.activation(o[:, b, :, :], o[:, b, :, :], ACT.Relu, bias=C.one[:, 0:1], scale=-1.0)

            def numerators(i, b, t, first):
                act.wait_ge(ch, t * 3 + 3)
                nc.scalar.activation(m[:, b, :, D:D + H], q[:, b, :, :], ACT.Exp).then_inc(ex, 1)
            staged(act, S.STEPS, [(0, onehots), (1, numerators)], DEPTH)

        @block.vector
        def _(dve):
            dve.memset(acc[:, :, :], 0.0).then_inc(cl, 1)
            for b in range(DEPTH):
                dve.memset(m[:, b, :, W - 1:W], 1.0)
            dve.wait_ge(cl, 1)
            dve.wait_ge(tl, 16)

            def local_dst(i, b, t, first):
                dve.wait_ge(ld[b], i * 32 + 32)
                dve.tensor_scalar(local[:, b, :], ed[:, b, :, 2 * H], node[:, bass.ds(t, 1)], C.wiota[:, 0:1],
                                  ALU.subtract, ALU.add).then_inc(lc, 1)

            def terms(i, b, t, first):
                dve.wait_ge(ad, t + 1)
                dve.tensor_tensor(z[:, b, :, :].rearrange("p j (a h) -> p j a h", a=2),
                                  ed[:, b, :, 0:2 * H].rearrange("p j (a h) -> p j a h", a=2),
                                  pa[:, b % 2, 0:SUB * H].rearrange("p (j h) -> p j h", j=SUB).unsqueeze(2)
                                  .to_broadcast([P, SUB, 2, H]), ALU.add).then_inc(ch, 1)

            def leaky(i, b, t, first):
                dve.wait_ge(ch, t * 3 + 1)
                dve.scalar_tensor_tensor(out=y[:, b, :, :], in0=z[:, b, :, :], scalar=0.2, in1=z[:, b, :, :],
                                         op0=ALU.mult, op1=ALU.max).then_inc(ch, 1)

            def exponents(i, b, t, first):
                dve.wait_ge(ch, t * 3 + 2)
                dve.tensor_tensor(q[:, b, :, :], y[:, b, :, 0:H], y[:, b, :, H:2 * H], ALU.subtract).then_inc(ch, 1)

            def message(j):
                def stage(i, b, t, first):
                    if j == 0:
                        dve.wait_ge(ex, t + 1)
                        dve.wait_ge(ga[b], i * (16 * SUB) + 16 * SUB)
                    ins = dve.tensor_tensor(m[:, b, j, 0:D].rearrange("p (h d) -> p h d", h=H),
                                            g[:, b, j, :].rearrange("p (h d) -> p h d", h=H),
                                            m[:, b, j, D:D + H].unsqueeze(2).to_broadcast([P, H, HD]), ALU.mult)
                    if j == SUB - 1:
                        ins.then_inc(ms, 1)
                return stage

            windows = RoundTable(nc, mybir.EngineType.DVE, tab[0:1, 0, :], DEPTH, ADD_LAG, S.NT - 1)

            def add(i, b, t, first):
                w = windows.at[b]
                dve.wait_ge(sc, t + 1)
                if not (first and b == 0):
                    dve.wait_ge(dn, t)
                a = acc[:, bass.ds(w, 1), :].rearrange("p a c -> p (a c)")
                dve.tensor_tensor(a, a, po[:, b % 2, 0:W], ALU.add).then_inc(dn, 1)
            staged(dve, S.STEPS, [(0, local_dst), (2, terms), (3, message(0)), (2, leaky), (3, message(1)), (2, exponents), (ADD_LAG, add)],
                   DEPTH, [windows])

        @block.tensor
        def _(pe):
            pe.wait_ge(tl, 16)

            windows = RoundTable(nc, mybir.EngineType.PE, tab[0:1, 0, :], DEPTH, 0, S.NT - 1)

            def dst_terms(i, b, t, first):
                w = windows.at[b]
                pe.wait_ge(oh, t + 1)
                if not (first and b < 2):
                    pe.wait_ge(ch, t * 3 - 5)
                for j in range(SUB):
                    last = pe.matmul(pa[:, b % 2, j * H:(j + 1) * H], oT[:, b, j, :],
                                     C.adst[:, bass.ds(w, 1), :].rearrange("p a h -> p (a h)"), start=True, stop=True)
                last.then_inc(ad, 1)

            def scatter(i, b, t, first):
                pe.matmul(warm[:, 0:P], C.ones[:, :], C.ones[:, :], start=True, stop=True)
                pe.wait_ge(ms, t + 1)
                if not (first and b < 2):
                    pe.wait_ge(dn, t - 1)
                for j in range(SUB):
                    last = pe.matmul(po[:, b % 2, 0:W], o[:, b, j, :], m[:, b, j, :],
                                     start=j == 0, stop=j == SUB - 1)
                last.then_inc(sc, 1)
            staged(pe, S.STEPS, [(0, dst_terms), (2, scatter)], DEPTH, [windows])


def gat_finish(k, S, C, acc, x_res, x_dram):
    nc = k.nc
    NT, H, D = S.NT, S.H, S.D
    xl = k.sem("residual_x_loaded")
    ch = k.sem("gat_finish_chain")
    with ExitStack() as ctx:
        den = k.sb(ctx, "gat_den", [P, NT, H])
        block = ctx.enter_context(nc.Block())

        @block.gpsimd
        def _(pool):
            pool.memset(x_res[:, NT - 1, :], 0.0).then_inc(xl, 1)

        @block.sync
        def _(sp):
            sp.wait_ge(xl, 1)
            full, tail = rows_of(x_dram, S)
            sp.dma_start(x_res[:, 0:NT - 1, :], full).then_inc(xl, 16)
            sp.dma_start(x_res[0:S.TAIL, NT - 1, :], tail).then_inc(xl, 16)

        @block.vector
        def _(dve):
            c = Chain(dve, ch)
            out = acc[:, :, 0:D]
            heads = out.rearrange("p n (h d) -> p n h d", h=H)
            c.mark(dve.tensor_scalar(C.out_deg[:, :], acc[:, :, D + H], 1.0, None, ALU.add))
            c.link(dve.tensor_scalar(den[:, :, :], acc[:, :, D:D + H], 1e-16, None, ALU.add))
            c.link(dve.reciprocal(den[:, :, :], den[:, :, :]))
            c.link(dve.tensor_tensor(heads, heads, den[:, :, :].unsqueeze(3).to_broadcast([P, NT, H, S.HD]), ALU.mult))
            c.link(dve.tensor_tensor(out, out, C.gat_bias[:, :].unsqueeze(1).to_broadcast([P, NT, D]), ALU.add))
            dve.wait_ge(xl, 33)
            c.link(dve.scalar_tensor_tensor(out=x_res[:, :, :], in0=out, scalar=0.0, in1=x_res[:, :, :],
                                            op0=ALU.max, op1=ALU.add))



def gnn_scale(k, S, C, T, z):
    nc = k.nc
    ch = k.sem("scale_chain")
    rt = k.sem("degree_roots")
    st = k.sem("zb_stored")
    with ExitStack() as ctx:
        sd = k.sb(ctx, "degree_root", [P, 2, S.NT])
        block = ctx.enter_context(nc.Block())

        @block.scalar
        def _(act):
            nc.scalar.activation(sd[:, 0, :], C.out_deg[:, :], ACT.Sqrt).then_inc(rt, 1)
            nc.scalar.activation(sd[:, 1, :], C.in_deg[:, :], ACT.Sqrt).then_inc(rt, 1)

        @block.vector
        def _(dve):
            c = Chain(dve, ch)
            dve.wait_ge(rt, 2)
            c.link(dve.reciprocal(C.dinv[:, :, :], sd[:, :, :]))
            for a in (1, 0):
                part = z[:, :, a * P:(a + 1) * P]
                c.mark(dve.tensor_tensor(part, part, C.dinv[:, a, :].unsqueeze(2).to_broadcast([P, S.NT, P]), ALU.mult))

        @block.sync
        def _(sp):
            sp.wait_ge(ch, 2)
            sp.dma_start(T.zb.rearrange("(i p) d -> p i d", p=P), z[:, :, P:2 * P]).then_inc(st, 16)
            sp.wait_ge(st, 16)


def gnn_edges(k, S, C, T, z, acc, base_of):
    nc = k.nc
    DEPTH = GNN_DEPTH
    ADD_LAG = 2
    DUP_OPS = 4
    SPARE = S.NT * P
    tl = k.sem("gnn_table_loaded")
    ld = k.sems("gnn_step_loaded", DEPTH)
    ga = k.sems("gnn_rows_gathered", DEPTH)
    oh = k.sem("gnn_onehot_ready")
    dp = k.sem("gnn_duplicate_chain")
    pc = k.sem("gnn_pair_ready")
    mc = k.sem("gnn_pair_copied")
    pm = k.sem("gnn_message_ready")
    ms = k.sem("gnn_message_copied")
    sc = k.sem("gnn_step_summed")
    dn = k.sem("gnn_step_done")
    sa = k.sems("gnn_rows_added", 2)
    cl = k.sem("gnn_acc_clear")
    with ExitStack() as ctx:
        tab = k.sb(ctx, "gnn_table", [1, 2, P * S.KC], I32)
        sd = k.sb(ctx, "gnn_src_dst", [P, DEPTH, SUB, 3])
        row = k.sb(ctx, "gnn_src_row", [P, DEPTH, STEP])
        g = k.sb(ctx, "gnn_rows", [P, DEPTH, SUB, P])
        o = k.sb(ctx, "gnn_onehot", [P, DEPTH, SUB, P])
        eq = k.sb(ctx, "gnn_same_src", [P, DEPTH, SUB, P])
        junk = k.sb(ctx, "gnn_junk", [P, 2, SUB, P])
        dup = k.sb(ctx, "gnn_earlier", [P, DEPTH, SUB])
        away = k.sb(ctx, "gnn_away", [P, DEPTH, SUB])
        to = k.sb(ctx, "gnn_add_idx", [P, DEPTH, SUB], I32)
        spare = k.sb(ctx, "gnn_spare", [P, 1])
        pr = k.sb(ctx, "gnn_pair", [P, DEPTH, SUB, P])
        m = k.sb(ctx, "gnn_message", [P, DEPTH, SUB, P])
        pp = k.ps(ctx, "gnn_pair_ps", [P, 2, 512])
        pq = k.ps(ctx, "gnn_message_ps", [P, 2, 512])
        po = k.ps(ctx, "gnn_sum_ps", [P, 2, 512])
        block = ctx.enter_context(nc.Block())

        @block.sync
        def _(sp):
            load_step_table(k, S, sp, T, tab, tl)
            sp.wait_ge(tl, 16)

            bases = RoundTable(nc, mybir.EngineType.SP, tab[0:1, 1, :], DEPTH, 0, S.E)

            def load(i, b, t, first):
                base = bases.at[b]
                if not first:
                    sp.wait_ge(dn, t - (DEPTH - 1))
                    sp.nop(nofuse=True)
                    sp.wait_ge(dp, (t - (DEPTH - 1)) * DUP_OPS)
                    sp.nop(nofuse=True)
                sp.dma_start(sd[:, b, :, :], T.sd[bass.ds(base, STEP), :].rearrange("(p j) c -> p j c", j=SUB)).then_inc(ld[b], 16)
                sp.dma_start(row[:, b, :], T.src_f[bass.ds(base, STEP)].partition_broadcast(P)).then_inc(ld[b], 16)
            staged(sp, S.STEPS, [(0, load)], DEPTH, [bases])

        @block.gpsimd
        def _(pool):
            def gather(i, b, t, first):
                pool.wait_ge(ld[b], i * 32 + 32)
                pool.nop(nofuse=True)
                for j in range(SUB):
                    pool.indirect_dma_start(
                        out=g[:, b, j, :], out_offset=None, in_=T.zb[:, :],
                        in_offset=bass.IndirectOffsetOnAxis(ap=sd[:, b, j, 2:3].bitcast(I32), axis=0)).then_inc(ga[b], 16)

            def add_rows(i, b, t, first):
                pool.wait_ge(ms, t + 1)
                if not (first and b < 2):
                    pool.wait_ge(sa[b % 2], i * (16 * SUB * (DEPTH // 2)) + 16 * SUB * (b // 2))
                pool.nop(nofuse=True)
                for j in range(SUB):
                    pool.indirect_dma_start(
                        out=T.yf[SUB * (b % 2) + j][:, :],
                        out_offset=bass.IndirectOffsetOnAxis(ap=to[:, b, j:j + 1], axis=0),
                        in_=m[:, b, j, :], in_offset=None, compute_op=ALU.add).then_inc(sa[b % 2], 16)
            staged(pool, S.STEPS, [(0, gather), (2, add_rows)], DEPTH)
            for b in range(2):
                pool.wait_ge(sa[b], 16 * SUB * (S.STEPS // 2))

        @block.vector
        def _(dve):
            dve.memset(acc[:, :, :], 0.0).then_inc(cl, 1)
            dve.tensor_scalar(spare[:, :], C.wiota[:, 0:1], float(SPARE), None, ALU.add).then_inc(cl, 1)
            dve.wait_ge(cl, 2)
            dve.wait_ge(tl, 16)

            def onehots(i, b, t, first):
                dve.wait_ge(ld[b], i * 32 + 32)
                if not first:
                    dve.wait_ge(sa[b % 2], i * (16 * SUB * (DEPTH // 2)) + (16 * SUB * (b // 2) - 16 * SUB * (DEPTH // 2 - 1)))
                for j in range(SUB):
                    dve.tensor_scalar(o[:, b, j, :], C.iota[:, :], base_of[:, bass.ds(t, 1)], sd[:, b, j, 1:2],
                                      ALU.add, ALU.is_equal)
                    last = dve.tensor_scalar(eq[:, b, j, :], row[:, b, :].rearrange("p (e j) -> p j e", j=SUB)[:, j, :],
                                             sd[:, b, j, 0:1], None, ALU.is_equal)
                last.then_inc(oh, 1)

            def row_numbers(i, b, t, first):
                dve.wait_ge(oh, t + 1)
                for j in range(SUB):
                    last = dve.tensor_tensor_reduce(out=junk[:, b % 2, j, :], in0=eq[:, b, j, :], in1=C.lower[:, :], scale=1.0,
                                                    scalar=0.0, op0=ALU.mult, op1=ALU.add,
                                                    accum_out=dup[:, b, j:j + 1])
                last.then_inc(dp, 1)
                dve.tensor_scalar(away[:, b, :], sd[:, b, :, 0], -1.0, spare[:, 0:1], ALU.mult, ALU.add).then_inc(dp, 1)
                dve.wait_ge(dp, t * DUP_OPS + 2)
                dve.scalar_tensor_tensor(out=away[:, b, :], in0=dup[:, b, :], scalar=0.5, in1=away[:, b, :],
                                         op0=ALU.is_gt, op1=ALU.mult).then_inc(dp, 1)
                dve.wait_ge(dp, t * DUP_OPS + 3)
                dve.tensor_tensor(to[:, b, :], away[:, b, :], sd[:, b, :, 0], ALU.add).then_inc(dp, 1)

            windows = RoundTable(nc, mybir.EngineType.DVE, tab[0:1, 0, :], DEPTH, ADD_LAG, S.NT - 1)

            def add(i, b, t, first):
                w = windows.at[b]
                dve.wait_ge(sc, t + 1)
                if not (first and b == 0):
                    dve.wait_ge(dn, t)
                a = acc[:, bass.ds(w, 1), :].rearrange("p a c -> p (a c)")
                dve.tensor_tensor(a, a, po[:, b % 2, 0:P], ALU.add).then_inc(dn, 1)
            staged(dve, S.STEPS, [(0, onehots), (1, row_numbers), (ADD_LAG, add)], DEPTH, [windows])

        @block.scalar
        def _(act):
            def pairs(i, b, t, first):
                act.wait_ge(pc, t + 1)
                nc.scalar.copy(pr[:, b, :, :], pp[:, b % 2, 0:SUB * P].rearrange("p (j e) -> p j e", j=SUB)).then_inc(mc, 1)

            def messages(i, b, t, first):
                act.wait_ge(pm, t + 1)
                act.wait_ge(dp, t * DUP_OPS + DUP_OPS)
                if not first:
                    act.wait_ge(sa[b % 2], i * (16 * SUB * (DEPTH // 2)) + (16 * SUB * (b // 2) - 16 * SUB * (DEPTH // 2 - 1)))
                nc.scalar.copy(m[:, b, :, :], pq[:, b % 2, 0:SUB * P].rearrange("p (j e) -> p j e", j=SUB)).then_inc(ms, 1)
            staged(act, S.STEPS, [(0, pairs), (1, messages)], DEPTH)

        @block.tensor
        def _(pe):
            pe.wait_ge(tl, 16)

            def pairs(i, b, t, first):
                pe.wait_ge(oh, t + 1)
                if not (first and b < 2):
                    pe.wait_ge(mc, t - 1)
                for j in range(SUB):
                    last = pe.matmul(pp[:, b % 2, j * P:(j + 1) * P], o[:, b, j, :], eq[:, b, j, :],
                                     start=True, stop=True)
                last.then_inc(pc, 1)

            windows = RoundTable(nc, mybir.EngineType.PE, tab[0:1, 0, :], DEPTH, 1, S.NT - 1)

            def messages(i, b, t, first):
                w = windows.at[b]
                pe.wait_ge(mc, t + 1)
                if not (first and b < 2):
                    pe.wait_ge(ms, t - 1)
                for j in range(SUB):
                    last = pe.matmul(pq[:, b % 2, j * P:(j + 1) * P], pr[:, b, j, :],
                                     z[:, bass.ds(w, 1), 0:P].rearrange("p a c -> p (a c)"), start=True, stop=True)
                last.then_inc(pm, 1)
                pe.wait_ge(ga[b], i * (16 * SUB) + 16 * SUB)
                if not (first and b < 2):
                    pe.wait_ge(dn, t - 1)
                for j in range(SUB):
                    last = pe.matmul(po[:, b % 2, 0:P], o[:, b, j, :], g[:, b, j, :], start=j == 0, stop=j == SUB - 1)
                last.then_inc(sc, 1)
            staged(pe, S.STEPS, [(0, pairs), (1, messages)], DEPTH, [windows])


def gnn_finish(k, S, C, T, z, acc, x_res):
    nc = k.nc
    NT = S.NT
    SLOTS = 4
    ld = k.sems("forward_sums_loaded", SLOTS)
    us = k.sem("forward_sums_used")
    ch = k.sem("forward_finish_chain")
    cb = k.sem("backward_finish_chain")
    with ExitStack() as ctx:
        f = k.sb(ctx, "forward_sums_sb", [P, SLOTS, GROUP, P])
        block = ctx.enter_context(nc.Block())
        parts = [(g, y) for g in range(NT // GROUP) for y in range(2 * SUB)]

        def finish(c, a):
            part = z[:, :, a * P:(a + 1) * P]
            x_part = x_res[:, :, a * P:(a + 1) * P]
            shape = [P, NT, P]
            c.link(c.eng.tensor_tensor(part, part, C.dinv[:, 1 - a, :].unsqueeze(2).to_broadcast(shape), ALU.mult))
            c.link(c.eng.tensor_tensor(part, part, C.gnn_bias[:, a * P:(a + 1) * P].unsqueeze(1).to_broadcast(shape),
                                       ALU.add))
            c.link(c.eng.tensor_tensor(x_part, x_part, part, ALU.add))

        @block.sync
        def _(sp):
            for n, (g, y) in enumerate(parts):
                if n >= SLOTS:
                    sp.wait_ge(us, n - SLOTS + 1)
                sp.dma_start(f[:, n % SLOTS, :, :], T.yf[y][g * GROUP * P:(g + 1) * GROUP * P, :]
                             .rearrange("(i p) d -> p i d", p=P)).then_inc(ld[n % SLOTS], 16)

        @block.vector
        def _(dve):
            for n, (g, y) in enumerate(parts):
                part = z[:, g * GROUP:(g + 1) * GROUP, 0:P]
                dve.wait_ge(ld[n % SLOTS], 16 * (n // SLOTS + 1))
                if n:
                    dve.wait_ge(us, n)
                dve.tensor_tensor(part, part, f[:, n % SLOTS, :, :], ALU.add).then_inc(us, 1)
            dve.wait_ge(us, len(parts))
            finish(Chain(dve, ch), 0)

        @block.gpsimd
        def _(pool):
            c = Chain(pool, cb)
            back = z[:, :, P:2 * P]
            c.link(pool.tensor_tensor(back, back, acc[:, :, :], ALU.add))
            finish(c, 1)



def route(k, S, C, tag, tok, logits, bias, choices, n_exp, capacity, idx_put, idx_get, weight, gtab):
    nc = k.nc
    NT, X = S.NT, n_exp
    groups = S.G1 if capacity is None else S.G2
    ch = k.sem(f"{tag}_route_chain")
    ex = k.sem(f"{tag}_route_exp_in")
    eo = k.sem(f"{tag}_route_exp_out")
    mr = k.sem(f"{tag}_route_mask_ready")
    rk = k.sem(f"{tag}_route_ranks")
    io = k.sem(f"{tag}_route_iota")
    with ExitStack() as ctx:
        lg = k.sb(ctx, f"{tag}_logits", [P, NT, X])
        t0 = k.sb(ctx, f"{tag}_t0", [P, NT, X])
        pv = k.sb(ctx, f"{tag}_pv", [P, NT, X])
        mk = k.sb(ctx, f"{tag}_masks", [P, choices, NT, X])
        both = k.sb(ctx, f"{tag}_both", [P, NT, X])
        mx = k.sb(ctx, f"{tag}_mx", [P, choices, NT])
        ix = k.sb(ctx, f"{tag}_ix", [P, NT])
        dd = k.sb(ctx, f"{tag}_dd", [P, NT])
        valid = k.sb(ctx, f"{tag}_valid", [P, NT])
        pos = k.sb(ctx, f"{tag}_pos", [P, NT, X])
        tot = k.sb(ctx, f"{tag}_tot", [P, X, NT])
        car = k.sb(ctx, f"{tag}_car", [P, X, NT + 1])
        zero = k.sb(ctx, f"{tag}_zero", [P, max(NT, X)])
        ng = k.sb(ctx, f"{tag}_ng", [P, X])
        ng_i = k.sb(ctx, f"{tag}_ng_i", [P, X], I32)
        gend = k.sb(ctx, f"{tag}_gend", [P, X])
        base = k.sb(ctx, f"{tag}_base", [P, X])
        sl = k.sb(ctx, f"{tag}_slot", [P, NT])
        kp = k.sb(ctx, f"{tag}_kept", [P, NT])
        gc = k.sb(ctx, f"{tag}_gcmp", [P, groups, X])
        gw = k.sb(ctx, f"{tag}_gw", [P, groups])
        pk = k.ps(ctx, f"{tag}_rank_ps", [P, 512])
        pt = k.ps(ctx, f"{tag}_total_ps", [P, 512])
        block = ctx.enter_context(nc.Block())
        grid = [P, NT, X]

        def wide(v):
            return v.unsqueeze(2).to_broadcast(grid)

        def over(v):
            return v.unsqueeze(1).to_broadcast(grid)

        @block.vector
        def _(dve):
            c = Chain(dve, ch)
            tt, ts = dve.tensor_tensor, dve.tensor_scalar
            c.link(tt(lg[:, :, :], logits[:, :, :], over(bias[:, :]), ALU.add))
            c.link(dve.memset(zero[:, :], 0.0))
            c.link(ts(valid[:, :], C.wiota[:, :], float(S.N) - 0.5, None, ALU.is_lt))

            def first_of(values, m, out):
                c.link(tt(t0[:, :, :], values[:, :, :], wide(m), ALU.is_equal))
                c.link(ts(t0[:, :, :], t0[:, :, :], -float(X), float(X), ALU.mult, ALU.add))
                c.link(tt(t0[:, :, :], t0[:, :, :], over(C.iota[:, 0:X]), ALU.add))
                c.link(dve.tensor_reduce(ix[:, :], t0[:, :, :], AX.X, ALU.min))
                c.link(tt(out, over(C.iota[:, 0:X]), wide(ix[:, :]), ALU.is_equal))

            c.link(dve.tensor_reduce(mx[:, 0, :], lg[:, :, :], AX.X, ALU.max))
            if choices == 2:
                first_of(lg, mx[:, 0, :], mk[:, 0, :, :])
                c.link(dve.tensor_copy(pv[:, :, :], lg[:, :, :]))
                c.link(ts(t0[:, :, :], mk[:, 0, :, :], 2.0 * NEG_BIG, None, ALU.mult))
                c.link(tt(pv[:, :, :], pv[:, :, :], t0[:, :, :], ALU.add))
                c.link(dve.tensor_reduce(mx[:, 1, :], pv[:, :, :], AX.X, ALU.max))
                first_of(pv, mx[:, 1, :], mk[:, 1, :, :])
                c.link(tt(dd[:, :], mx[:, 1, :], mx[:, 0, :], ALU.subtract))
                dve.nop(nofuse=True).then_inc(ex, 1)
                dve.wait_ge(eo, 1)
                c.link(ts(sl[:, :], kp[:, :], 1.0, None, ALU.add))
                c.link(dve.reciprocal(weight[:, 0, :], sl[:, :]))
                c.link(tt(weight[:, 1, :], weight[:, 0, :], kp[:, :], ALU.mult))
                c.link(tt(both[:, :, :], mk[:, 0, :, :], mk[:, 1, :, :], ALU.add))
            else:
                c.link(tt(pv[:, :, :], lg[:, :, :], wide(mx[:, 0, :]), ALU.subtract))
                dve.nop(nofuse=True).then_inc(ex, 1)
                dve.wait_ge(eo, 1)
                c.link(dve.tensor_reduce(sl[:, :], pos[:, :, :], AX.X, ALU.add))
                c.link(dve.reciprocal(dd[:, :], sl[:, :]))
                c.link(tt(pv[:, :, :], pos[:, :, :], wide(dd[:, :]), ALU.mult))
                c.link(dve.tensor_reduce(mx[:, 0, :], pv[:, :, :], AX.X, ALU.max))
                first_of(pv, mx[:, 0, :], mk[:, 0, :, :])
                c.link(dve.tensor_copy(weight[:, 0, :], mx[:, 0, :]))
                c.link(dve.tensor_copy(both[:, :, :], mk[:, 0, :, :]))
            c.link(tt(both[:, :, :], both[:, :, :], wide(valid[:, :]), ALU.mult))
            dve.nop(nofuse=True).then_inc(mr, 1)
            dve.wait_ge(rk, 1)
            c.link(dve.tensor_copy(tot[:, :, :], pt[:, 0:NT * X].rearrange("p (n x) -> p x n", x=X)))
            c.link(dve.memset(car[:, :, 0:1], 0.0))
            for e in range(X):
                c.link(dve.tensor_tensor_scan(car[:, e, 1:NT + 1], zero[:, 0:NT], tot[:, e, :], 0.0, ALU.add, ALU.add))
            c.link(tt(pos[:, :, :], pk[:, 0:NT * X].rearrange("p (n x) -> p n x", x=X),
                      car[:, :, 0:NT].rearrange("p x n -> p n x"), ALU.add))
            if capacity is None:
                c.link(ts(ng_i[:, :], car[:, :, NT], float(tok - 1), None, ALU.add))
                c.link(ts(ng_i[:, :], ng_i[:, :], tok.bit_length() - 1, None, ALU.arith_shift_right))
                c.link(dve.tensor_copy(ng[:, :], ng_i[:, :]))
                c.link(dve.tensor_tensor_scan(gend[:, :], zero[:, 0:X], ng[:, :], 0.0, ALU.add, ALU.add))
                c.link(tt(base[:, :], gend[:, :], ng[:, :], ALU.subtract))
                c.link(ts(base[:, :], base[:, :], float(tok), None, ALU.mult))
                gg = [P, groups, X]
                c.link(tt(gc[:, :, :], gend[:, :].unsqueeze(1).to_broadcast(gg),
                          C.iota[:, 0:groups].unsqueeze(2).to_broadcast(gg), ALU.is_le))
                c.link(dve.tensor_reduce(gw[:, :], gc[:, :, :], AX.X, ALU.add))
                c.link(ts(gtab[0:1, :], gw[0:1, :], float(X - 1), None, ALU.min))
            else:
                c.link(ts(base[:, :], C.iota[:, 0:X], float(groups * tok // X), None, ALU.mult))
            for n in range(choices):
                def chosen(v, out):
                    c.link(tt(t0[:, :, :], mk[:, n, :, :], v, ALU.mult))
                    c.link(dve.tensor_reduce(out, t0[:, :, :], AX.X, ALU.add))
                chosen(pos[:, :, :], sl[:, :])
                chosen(over(base[:, :]), dd[:, :])
                if capacity is None:
                    c.link(dve.tensor_copy(kp[:, :], valid[:, :]))
                else:
                    c.link(ts(kp[:, :], sl[:, :], float(capacity) - 0.5, None, ALU.is_lt))
                    c.link(tt(weight[:, n, :], weight[:, n, :], kp[:, :], ALU.mult))
                    c.link(tt(kp[:, :], kp[:, :], valid[:, :], ALU.mult))
                    c.link(ts(sl[:, :], sl[:, :], float(capacity - 1), None, ALU.min))
                c.link(tt(sl[:, :], sl[:, :], dd[:, :], ALU.add))
                c.link(ts(idx_get[:, n, :], sl[:, :], float(groups * tok - 1), None, ALU.min))
                c.link(ts(dd[:, :], C.wiota[:, :], float(groups * tok + n * S.ROWS), None, ALU.add))
                c.link(tt(sl[:, :], sl[:, :], dd[:, :], ALU.subtract))
                c.link(tt(sl[:, :], sl[:, :], kp[:, :], ALU.mult))
                c.link(tt(idx_put[:, n, :], sl[:, :], dd[:, :], ALU.add))

        @block.scalar
        def _(act):
            act.wait_ge(ex, 1)
            if choices == 2:
                nc.scalar.activation(kp[:, :], dd[:, :], ACT.Exp).then_inc(eo, 1)
            else:
                nc.scalar.activation(pos[:, :, :], pv[:, :, :], ACT.Exp).then_inc(eo, 1)

        @block.tensor
        def _(pe):
            pe.wait_ge(mr, 1)
            flat = both[:, :, :].rearrange("p n x -> p (n x)")
            pe.matmul(pk[:, 0:NT * X], C.upper[:, :], flat, start=True, stop=True)
            pe.matmul(pt[:, 0:NT * X], C.ones[:, :], flat, start=True, stop=True).then_inc(rk, 1)


def put_rows(k, S, tag, xn_all, idx_put, choices, buf, zeroed):
    nc = k.nc
    pt = k.sem(f"{tag}_rows_put")
    zm = k.sem(f"{tag}_zeros_ready")
    zs = k.sem(f"{tag}_buffers_zeroed")
    with ExitStack() as ctx:
        zf = k.sb(ctx, f"{tag}_zeros_f", [P, ZCOLS])
        block = ctx.enter_context(nc.Block())

        @block.gpsimd
        def _(pool):
            for i in range(S.NT):
                for n in range(choices):
                    pool.indirect_dma_start(
                        out=buf[:, :], out_offset=bass.IndirectOffsetOnAxis(ap=idx_put[:, n, i:i + 1], axis=0),
                        in_=xn_all[:, i, :], in_offset=None).then_inc(pt, 16)
            pool.wait_ge(pt, 16 * S.NT * choices)

        if zeroed:
            @block.vector
            def _(dve):
                dve.memset(zf[:, :], 0.0).then_inc(zm, 1)

            @block.sync
            def _(sp):
                sp.wait_ge(zm, 1)
                n = zero_fill(sp, zeroed, zf, zs)
                sp.wait_ge(zs, n)


def experts(k, S, C, tag, tok, groups, F, func, xb, yb, w1, b1, w2, b2, expert_of):
    nc = k.nc
    FC = F // P
    Q = tok // P
    D = S.D
    wl = k.sems(f"{tag}_weights_loaded", 2)
    xl = k.sems(f"{tag}_rows_loaded", 2)
    tp = k.sem(f"{tag}_rows_turned")
    tc = k.sem(f"{tag}_turned_copied")
    hp = k.sem(f"{tag}_hidden_product")
    hc = k.sem(f"{tag}_hidden_ready")
    yp = k.sem(f"{tag}_out_product")
    yc = k.sem(f"{tag}_out_ready")
    ys = k.sems(f"{tag}_out_stored", 2)
    with ExitStack() as ctx:
        w1s = k.sb(ctx, f"{tag}_w1", [P, 2, 2, F])
        w2s = k.sb(ctx, f"{tag}_w2", [P, 2, FC, D])
        b1s = k.sb(ctx, f"{tag}_b1", [P, 2, FC])
        b2s = k.sb(ctx, f"{tag}_b2", [P, 2, D])
        xr = k.sb(ctx, f"{tag}_rows", [P, 2, Q, D])
        xT = k.sb(ctx, f"{tag}_rows_T", [P, 2, 2, tok])
        hT = k.sb(ctx, f"{tag}_hidden", [P, FC, tok])
        yo = k.sb(ctx, f"{tag}_out_rows", [P, 2, Q, D])
        px = k.ps(ctx, f"{tag}_turn_ps", [P, 2, 512])
        ph = k.ps(ctx, f"{tag}_hidden_ps", [P, 2, 512])
        py = k.ps(ctx, f"{tag}_out_ps", [P, 2, 512])
        block = ctx.enter_context(nc.Block())

        @block.sync
        def _(sp):
            def load(i, b, t, first):
                e = expert_of(sp, t)
                if not first:
                    sp.wait_ge(yc, (t - 1) * Q)
                    sp.nop(nofuse=True)
                at = t * tok
                sp.dma_start(xr[:, b, :, :], xb[bass.ds(at, tok), :].rearrange("(q p) d -> p q d", p=P)).then_inc(xl[b], 16)
                sp.dma_start(w1s[:, b, :, :], w1[bass.ds(e, 1), :, :].rearrange("a (c p) f -> p (a c) f", p=P)).then_inc(wl[b], 16)
                sp.dma_start(b1s[:, b, :], b1[bass.ds(e, 1), :].rearrange("a (p c) -> p (a c)", p=P)).then_inc(wl[b], 16)
                sp.dma_start(w2s[:, b, :, :], w2[bass.ds(e, 1), :, :].rearrange("a (p c) d -> p (a c) d", p=P)).then_inc(wl[b], 16)
                sp.dma_start(b2s[:, b, :], b2[bass.ds(e, 1), :].rearrange("a d -> (a d)").partition_broadcast(P)).then_inc(wl[b], 16)

            def store(i, b, t, first):
                sp.wait_ge(yc, t * Q + Q)
                sp.nop(nofuse=True)
                sp.dma_start(yb[bass.ds(t * tok, tok), :].rearrange("(q p) d -> p q d", p=P), yo[:, b, :, :]).then_inc(ys[b], 16)
            staged(sp, groups, [(0, load), (2, store)], 2)
            for b in range(2):
                sp.wait_ge(ys[b], 16 * (groups // 2))

        @block.tensor
        def _(pe):
            def turn(i, b, t, first):
                pe.wait_ge(xl[b], i * 16 + 16)
                if not (first and b == 0):
                    pe.wait_ge(tc, t * 2)
                for c in range(2):
                    for q in range(Q):
                        last = pe.transpose(px[:, c, q * P:(q + 1) * P], xr[:, b, q, c * P:(c + 1) * P], C.ident[:, :])
                    last.then_inc(tp, 1)

            def hidden(i, b, t, first):
                pe.wait_ge(tc, t * 2 + 2)
                pe.wait_ge(wl[b], i * 64 + 64)
                for f in range(FC):
                    if not (first and b == 0 and f < 2):
                        pe.wait_ge(hc, t * FC + (f - 1))
                    for c in range(2):
                        last = pe.matmul(ph[:, f % 2, 0:tok], w1s[:, b, c, f:F:FC], xT[:, b, c, :],
                                         start=c == 0, stop=c == 1)
                    last.then_inc(hp, 1)

            def outs(i, b, t, first):
                pe.wait_ge(hc, t * FC + FC)
                for q in range(Q):
                    if not (first and b == 0 and q < 2):
                        pe.wait_ge(yc, t * Q + (q - 1))
                    for f in range(FC):
                        last = pe.matmul(py[:, q % 2, 0:D], hT[:, f, q * P:(q + 1) * P], w2s[:, b, f, :],
                                         start=f == 0, stop=f == FC - 1)
                    last.then_inc(yp, 1)
            staged(pe, groups, [(1, hidden), (0, turn), (1, outs)], 2)

        @block.scalar
        def _(act):
            def hidden(i, b, t, first):
                for f in range(FC):
                    act.wait_ge(hp, t * FC + (f + 1))
                    if f == 0 and not (first and b == 0):
                        act.wait_ge(yp, t * Q)
                    nc.scalar.activation(hT[:, f, :], ph[:, f % 2, 0:tok], func, bias=b1s[:, b, f:f + 1]).then_inc(hc, 1)
            staged(act, groups, [(0, hidden)], 2)

        @block.vector
        def _(dve):
            def turned(i, b, t, first):
                for c in range(2):
                    dve.wait_ge(tp, t * 2 + (c + 1))
                    if not first:
                        dve.wait_ge(hp, (t - 1) * FC)
                    dve.tensor_copy(xT[:, b, c, :], px[:, c, 0:tok]).then_inc(tc, 1)

            def outs(i, b, t, first):
                if not first:
                    dve.wait_ge(ys[b], i * 16)
                for q in range(Q):
                    dve.wait_ge(yp, t * Q + (q + 1))
                    dve.tensor_tensor(yo[:, b, q, :], py[:, q % 2, 0:D], b2s[:, b, :], ALU.add).then_inc(yc, 1)
            staged(dve, groups, [(0, turned), (1, outs)], 2)


def take_rows(k, S, tag, idx_get, choices, weight, buf, x_res, guard, out):
    nc = k.nc
    NT, D = S.NT, S.D
    parts = NT // GROUP
    gt = k.sems(f"{tag}_rows_taken", parts)
    ch = k.sem(f"{tag}_take_chain")
    dn = k.sem(f"{tag}_x_ready")
    st = k.sem(f"{tag}_output_stored")
    with ExitStack() as ctx:
        y = k.sb(ctx, f"{tag}_taken", [P, choices, NT, D])
        if guard:
            ok = k.sb(ctx, f"{tag}_in_range", [P, 3, GROUP, D], I32)
            lim = k.sb(ctx, f"{tag}_limits", [P, 3, 1])
        block = ctx.enter_context(nc.Block())

        @block.gpsimd
        def _(pool):
            for g in range(parts):
                for n in range(choices):
                    for i in range(g * GROUP, (g + 1) * GROUP):
                        pool.indirect_dma_start(
                            out=y[:, n, i, :], out_offset=None, in_=buf[:, :],
                            in_offset=bass.IndirectOffsetOnAxis(ap=idx_get[:, n, i:i + 1], axis=0)).then_inc(gt[g], 16)

        @block.vector
        def _(dve):
            c = Chain(dve, ch)
            shape = [P, GROUP, D]
            if guard:
                c.link(dve.memset(lim[:, 0, :], 0.0))
                c.link(dve.memset(lim[:, 1, :], 1e4))
                c.link(dve.memset(lim[:, 2, :], -1e4))
            for g in range(parts):
                at = slice(g * GROUP, (g + 1) * GROUP)
                dve.wait_ge(gt[g], 16 * GROUP * choices)
                for n in range(choices):
                    v = y[:, n, at, :]
                    c.link(dve.tensor_tensor(v, v, weight[:, n, at].unsqueeze(2).to_broadcast(shape), ALU.mult))
                    if guard:
                        c.mark(dve.tensor_tensor(ok[:, 0, :, :], v, v, ALU.not_equal))
                        c.mark(dve.tensor_scalar(ok[:, 1, :, :], v, 3.4028234663852886e38, None, ALU.is_gt))
                        c.link(dve.tensor_scalar(ok[:, 2, :, :], v, -3.4028234663852886e38, None, ALU.is_lt))
                        for m in range(3):
                            c.link(dve.copy_predicated(v, ok[:, m, :, :], lim[:, m, :].unsqueeze(1).to_broadcast(shape)))
                    ins = dve.tensor_tensor(x_res[:, at, :], x_res[:, at, :], v, ALU.add)
                    if n == choices - 1:
                        ins.then_inc(dn, 1)
                    else:
                        c.link(ins)

        if out is not None:
            @block.sync
            def _(sp):
                full, tail = rows_of(out, S)
                for g in range(parts):
                    a, b = g * GROUP, min((g + 1) * GROUP, NT - 1)
                    sp.wait_ge(dn, g + 1)
                    sp.dma_start(full[:, a:b, :], x_res[:, a:b, :]).then_inc(st, 16)
                sp.dma_start(tail, x_res[0:S.TAIL, NT - 1, :]).then_inc(st, 16)
                sp.wait_ge(st, 16 * (parts + 1))


class Namespace:
    pass


def store_rows(k, S, x_res, out):
    nc = k.nc
    st = k.sem("output_stored")
    with ExitStack() as ctx:
        block = ctx.enter_context(nc.Block())

        @block.sync
        def _(sp):
            full, tail = rows_of(out, S)
            sp.dma_start(full, x_res[:, 0:S.NT - 1, :]).then_inc(st, 16)
            sp.dma_start(tail, x_res[0:S.TAIL, S.NT - 1, :]).then_inc(st, 16)
            sp.wait_ge(st, 32)


def gnn_moe_kernel(nc, ins, out):
    S = Shapes(ins["x"], ins["src"], ins["L0_gnn_W"], ins["L0_ffn_W1"], ins["L1_ffn_w1"])
    NT, D, H = S.NT, S.D, S.H
    with ExitStack() as top:
        k = Core(nc, top)
        C, T = Namespace(), Namespace()
        C.ident = k.sb(top, "ident", [P, P])
        C.ones = k.sb(top, "ones", [P, P])
        C.iota = k.sb(top, "iota", [P, P])
        C.upper = k.sb(top, "upper", [P, P])
        C.lower = k.sb(top, "lower", [P, P])
        C.wiota = k.sb(top, "wiota", [P, NT])
        C.eps = k.sb(top, "eps", [P, 1])
        C.one = k.sb(top, "one", [P, 1])
        C.waug = k.sb(top, "w_aug", [P, 2, D + 2 * H])
        C.wfb = k.sb(top, "w_fb", [P, 2, D])
        C.wr = k.sb(top, "w_router", [P, 2, S.NX1])
        C.wg = k.sb(top, "w_gate", [P, 2, S.NX2])
        C.br = k.sb(top, "b_router", [P, S.NX1])
        C.bg = k.sb(top, "b_gate", [P, S.NX2])
        C.gat_bias = k.sb(top, "gat_bias", [P, D])
        C.gnn_bias = k.sb(top, "gnn_bias", [P, D])
        C.gamma = k.sb(top, "gamma", [P, D])
        C.beta = k.sb(top, "beta", [P, D])
        C.adst = k.sb(top, "a_dst", [P, NT, H])
        C.in_deg = k.sb(top, "in_deg", [P, NT])
        C.out_deg = k.sb(top, "out_deg", [P, NT])
        C.dinv = k.sb(top, "inv_root_degrees", [P, 2, NT])
        T.h = k.dram("h_rows", [NT * P, D])
        T.zb = k.dram("zb_rows", [NT * P, P])
        T.yf = [k.dram(f"forward_sums_{n}", [(NT + 1) * P, P]) for n in range(2 * SUB)]
        T.xb1 = k.dram("moe1_slots_in", [S.G1 * TOK1 + 2 * S.ROWS, D])
        T.xb2 = k.dram("moe2_slots_in", [S.G2 * TOK2 + S.ROWS, D])
        T.yb1 = k.dram("moe1_slots_out", [S.G1 * TOK1, D])
        T.yb2 = k.dram("moe2_slots_out", [S.G2 * TOK2, D])
        T.src_f = k.dram("edge_src_f", [S.E + STEP])
        T.src_hi = k.dram("edge_src_hi", [S.E], BF16)
        T.src_lo = k.dram("edge_src_lo", [S.E], BF16)
        T.terms = k.dram("edge_src_terms", [S.E, H])
        T.sd = k.dram("edge_src_dst", [S.E + STEP, 3])
        T.asrc = k.dram("a_src_rows", [NT * P, H])
        T.ea = k.dram("edge_terms", [S.E + STEP, S.EW])
        T.dst_f = k.dram("edge_dst", [S.E + STEP])
        T.steps = k.dram("step_table_dram", [2, P * S.KC], I32)

        setup(k, S, ins, C)
        edge_lists(k, S, ins, T)
        with ExitStack() as outer:
            C.asplit = k.sb(outer, "a_src_split", [P, 3, NT * H], BF16)
            C.farpat = k.sb(outer, "far_pattern", [NT, NT * H], BF16)
            with ExitStack() as ctx:
                x0 = k.sb(ctx, "x_in", [P, NT, D])
                pr = k.sb(ctx, "gat_products", [P, NT, D + 2 * H])
                project_nodes(k, S, C, "gat", x0, C.waug, D + 2 * H, pr, load_x=ins["x"])
                store_gat_tables(k, S, C, pr, T)
            with ExitStack() as ctx:
                source_terms(k, S, C, ins, T)
                ea = k.sb(ctx, "edge_terms_sb", [S.EP, S.ET, S.EW])
                edge_maxima(k, S, C, ins, T, ea)
        x_res = k.sb(top, "x_res", [P, NT, D])
        with ExitStack() as ctx:
            node = k.sb(ctx, "gat_step_nodes", [P, P * S.KC])
            acc = k.sb(ctx, "gat_acc", [P, NT, D + H + 1])
            step_windows(k, S, C, T, "gat", node, True)
            gat_edges(k, S, C, T, acc, node)
            gat_finish(k, S, C, acc, x_res, ins["x"])
        k.recycle()

        def moe(tag, tok, rhs, bias, choices, X, capacity, affine, groups, F, func, xb, yb, w, guard, zeroed, store):
            with ExitStack() as ctx:
                put = k.sb(ctx, f"{tag}_put_idx", [P, choices, NT], I32)
                get = k.sb(ctx, f"{tag}_get_idx", [P, choices, NT], I32)
                weight = k.sb(ctx, f"{tag}_weight", [P, choices, NT])
                gtab = k.sb(ctx, f"{tag}_group_expert", [1, groups], I32)
                with ExitStack() as inner:
                    xn = k.sb(inner, f"{tag}_xn_all", [P, NT, D])
                    logits = k.sb(inner, f"{tag}_raw_logits", [P, NT, X])
                    project_nodes(k, S, C, tag, x_res, rhs, X, logits, xn_all=xn, affine=affine)
                    route(k, S, C, tag, tok, logits, bias, choices, X, capacity, put, get, weight, gtab)
                    put_rows(k, S, tag, xn, put, choices, xb, zeroed)
                per = groups // X
                if capacity is None:
                    def expert_of(eng, t):
                        return eng.value_load(gtab[0:1, bass.ds(t, 1)], min_val=0, max_val=X - 1)
                else:
                    def expert_of(eng, t):
                        assert per == 2
                        return t // 2
                experts(k, S, C, tag, tok, groups, F, func, xb, yb, *w, expert_of)
                take_rows(k, S, tag, get, choices, weight, yb, x_res, guard, store)

        moe("moe1", TOK1, C.wr, C.br, 2, S.NX1, None, (C.gamma, C.beta), S.G1, S.F1, ACT.Gelu, T.xb1, T.yb1,
            (ins["L0_ffn_W1"], ins["L0_ffn_b1"], ins["L0_ffn_W2"], ins["L0_ffn_b2"]), False,
            [*T.yf, T.xb2[0:S.G2 * TOK2, :]], None)
        with ExitStack() as ctx:
            z = k.sb(ctx, "gnn_z", [P, NT, D])
            project_nodes(k, S, C, "gnn", x_res, C.wfb, D, z)
            gnn_scale(k, S, C, T, z)
            acc = k.sb(ctx, "gnn_acc", [P, NT, P])
            with ExitStack() as inner:
                base_of = k.sb(inner, "gnn_step_bases", [P, P * S.KC])
                step_windows(k, S, C, T, "gnn", base_of, False)
                gnn_edges(k, S, C, T, z, acc, base_of)
            gnn_finish(k, S, C, T, z, acc, x_res)
        k.recycle()
        moe("moe2", TOK2, C.wg, C.bg, 1, S.NX2, S.CAP, None, S.G2, S.F2, ACT.Relu, T.xb2, T.yb2,
            (ins["L1_ffn_w1"], ins["L1_ffn_b1"], ins["L1_ffn_w2"], ins["L1_ffn_b2"]), True, [], out)


_INS = ["x", "src", "dst", "L0_gnn_W", "L0_gnn_att_src", "L0_gnn_att_dst", "L0_gnn_bias", "L0_ffn_gamma",
        "L0_ffn_beta", "L0_ffn_Wr", "L0_ffn_br", "L0_ffn_W1", "L0_ffn_b1", "L0_ffn_W2", "L0_ffn_b2", "L1_gnn_W_f",
        "L1_gnn_W_b", "L1_gnn_bias_param", "L1_ffn_gate_w", "L1_ffn_gate_b", "L1_ffn_w1", "L1_ffn_b1", "L1_ffn_w2",
        "L1_ffn_b2"]


def kernel(**inputs):
    import numpy as np
    import concourse.bacc as bacc
    from concourse.bass_utils import run_bass_kernel_spmd

    nc = bacc.Bacc("TRN2", target_bir_lowering=False, num_devices=1)
    arrays, ins = {}, {}
    for name in _INS:
        a = np.ascontiguousarray(inputs[name])
        arrays["in_" + name] = a
        ins[name] = nc.dram_tensor("in_" + name, a.shape, mybir.dt.from_np(a.dtype), kind="ExternalInput").ap()
    shape = inputs["x"].shape
    out = nc.dram_tensor("out", shape, F32, kind="ExternalOutput").ap()
    gnn_moe_kernel(nc, ins, out)
    r = run_bass_kernel_spmd(nc, [arrays], core_ids=[0])
    return r.results[0]["out"]
```
